# Optimizing a Trainium2 kernel written in Bass

```python
import numpy as np
import jax
import jax.numpy as jnp

def _softmax(x, axis=-1):
    return jax.nn.softmax(x, axis=axis)

def _gelu(x):
    return jax.nn.gelu(x, approximate=True)

def _silu(x):
    return jax.nn.silu(x)

def _sigmoid(x):
    return jax.nn.sigmoid(x)

def _layernorm(x, axis=-1, eps=1e-05):
    m = jnp.mean(x, axis=axis, keepdims=True)
    v = jnp.var(x, axis=axis, keepdims=True)
    return (x - m) / jnp.sqrt(v + eps)

def _scatter_add(tgt, idx, src, axis=0):
    return tgt.at[idx].add(src)

def _segment_sum(src, seg, n):
    return jax.ops.segment_sum(src, seg, n)
kernel_name = 'mk_adaln_d2_jaxref_r8_012748'

def setup_inputs(seed: int=0):
    np.random.seed(seed)
    _w = jnp.asarray

    def _L0_attn_setup():
        import jax, jax.numpy as jnp
        import numpy as np
        EPS_RMS = 1e-06
        EPS_GN = 1e-05

        def rms_norm(x, w, eps=EPS_RMS):
            var = jnp.mean(x * x, axis=-1, keepdims=True)
            return w * (x * jax.lax.rsqrt(var + eps))
        key = jax.random.key(seed)
        B, T, D, H, LORA, F = (4, 256, 128, 16, 64, 512)
        dk = D // H
        ks = jax.random.split(key, 20)
        s = 0.02

        def n(k, shape, scale=s):
            return jax.random.normal(k, shape, dtype=jnp.float32) * scale
        return {'x': n(ks[0], (B, T, D), 1.0), 'ln1_w': jnp.ones((D,), jnp.float32), 'mu_r': jax.random.uniform(ks[1], (D,), jnp.float32), 'mu_k': jax.random.uniform(ks[2], (D,), jnp.float32), 'mu_v': jax.random.uniform(ks[3], (D,), jnp.float32), 'mu_w': jax.random.uniform(ks[4], (D,), jnp.float32), 'mu_g': jax.random.uniform(ks[5], (D,), jnp.float32), 'Wr': n(ks[6], (D, D)), 'Wk': n(ks[7], (D, D)), 'Wv': n(ks[8], (D, D)), 'Wg': n(ks[9], (D, D)), 'Wo': n(ks[10], (D, D)), 'w0': n(ks[11], (D,), 0.5), 'wA': n(ks[12], (D, LORA)), 'wB': n(ks[13], (LORA, D)), 'u': n(ks[14], (H, dk), 0.5), 'gn_w': jnp.ones((H, dk), jnp.float32), 'gn_b': jnp.zeros((H, dk), jnp.float32), 'ln2_w': jnp.ones((D,), jnp.float32), 'ffn_w1': n(ks[15], (D, F)), 'ffn_w2': n(ks[16], (F, D))}
    _L0_attn_in = _L0_attn_setup()

    def _L0_ffn_setup():
        import jax, jax.numpy as jnp
        import numpy as np
        D_MODEL = 128
        EXPERT_DIM = 512
        N_EXPERTS = 8
        CAP_FACTOR = 0.5
        key = jax.random.key(seed)
        ks = jax.random.split(key, 7)
        inp = {'input': jax.random.normal(ks[0], (4, 512, D_MODEL), dtype=jnp.float32), 'w_switch': jax.random.normal(ks[1], (D_MODEL, N_EXPERTS), dtype=jnp.float32) * 0.02, 'b_switch': jnp.zeros((N_EXPERTS,), jnp.float32), 'w1': jax.random.normal(ks[2], (N_EXPERTS, D_MODEL, EXPERT_DIM), dtype=jnp.float32) * 0.02, 'b1': jnp.zeros((N_EXPERTS, EXPERT_DIM), jnp.float32), 'w2': jax.random.normal(ks[3], (N_EXPERTS, EXPERT_DIM, D_MODEL), dtype=jnp.float32) * 0.02, 'b2': jnp.zeros((N_EXPERTS, D_MODEL), jnp.float32)}
        return inp
    _L0_ffn_in = _L0_ffn_setup()
    _L0_c = _w((lambda *s: np.random.randn(*s).astype(np.float32) * 0.05)(1, 128))
    _L0_wmod = _w((lambda *s: np.random.randn(*s).astype(np.float32) * 0.05)(128, 6 * 128) * 128 ** (-0.5))

    def _L1_attn_setup():
        import jax, jax.numpy as jnp
        import numpy as np
        B, L, D_MODEL = (2, 128, 128)
        D_STATE, D_CONV, EXPAND = (16, 4, 2)
        D_INNER = D_MODEL * EXPAND
        DT_RANK = (D_MODEL + 15) // 16

        def _silu(v):
            return v * jax.nn.sigmoid(v)

        def _mamba_fwd(x, in_proj_w, conv_w, conv_b, x_proj_w, dt_proj_w, dt_proj_b, A_log, D_param, out_proj_w):
            b, l, _ = x.shape
            d_inner = D_param.shape[0]
            d_state = A_log.shape[1]
            dt_rank = dt_proj_w.shape[1]
            xz = jnp.einsum('bld,ed->ble', x, in_proj_w)
            xb, zb = (xz[..., :d_inner], xz[..., d_inner:])
            u = jax.lax.conv_general_dilated(jnp.transpose(xb, (0, 2, 1)), conv_w, window_strides=(1,), padding=[(conv_w.shape[-1] - 1, 0)], feature_group_count=d_inner, dimension_numbers=('NCH', 'OIH', 'NCH'))
            u = jnp.transpose(u, (0, 2, 1)) + conv_b
            u = _silu(u)
            proj = jnp.einsum('bld,ed->ble', u, x_proj_w)
            dt_raw = proj[..., :dt_rank]
            b_raw = proj[..., dt_rank:dt_rank + d_state]
            c_raw = proj[..., dt_rank + d_state:dt_rank + 2 * d_state]
            a_gate_raw = proj[..., dt_rank + 2 * d_state:]
            dt = jax.nn.softplus(jnp.einsum('blr,er->ble', dt_raw, dt_proj_w) + dt_proj_b)
            a_base = -jnp.exp(A_log)
            a_gate = jax.nn.sigmoid(a_gate_raw)

            def step(state, inp):
                dt_t, u_t, b_t, c_t, g_t = inp
                a = a_base[None] * (0.5 + g_t)[..., None]
                decay = jnp.exp(dt_t[..., None] * a)
                state = decay * state + dt_t[..., None] * b_t[:, None, :] * u_t[..., None]
                y_t = jnp.sum(state * c_t[:, None, :], axis=-1) + D_param * u_t
                return (state, y_t)
            tm = lambda v: jnp.moveaxis(v, 1, 0)
            state0 = jnp.zeros((b, d_inner, d_state), dtype=x.dtype)
            _, ys = jax.lax.scan(step, state0, (tm(dt), tm(u), tm(b_raw), tm(c_raw), tm(a_gate)))
            y = jnp.moveaxis(ys, 0, 1)
            y = y * _silu(zb)
            return jnp.einsum('ble,de->bld', y, out_proj_w)
        key = jax.random.key(seed)
        ks = jax.random.split(key, 10)
        s = 0.02
        x = jax.random.normal(ks[0], (B, L, D_MODEL), dtype=jnp.float32)
        in_proj_w = jax.random.normal(ks[1], (2 * D_INNER, D_MODEL), dtype=jnp.float32) * s
        conv_w = jax.random.normal(ks[2], (D_INNER, 1, D_CONV), dtype=jnp.float32) * 0.2
        conv_b = jax.random.normal(ks[3], (D_INNER,), dtype=jnp.float32) * 0.02
        x_proj_w = jax.random.normal(ks[4], (DT_RANK + 2 * D_STATE + D_INNER, D_INNER), dtype=jnp.float32) * s
        dt_proj_w = jax.random.normal(ks[5], (D_INNER, DT_RANK), dtype=jnp.float32) * s
        dt = jax.random.uniform(ks[6], (D_INNER,), dtype=jnp.float32, minval=0.001, maxval=0.1)
        dt_proj_b = jnp.log(jnp.expm1(dt))
        A_log = jnp.tile(jnp.log(jnp.arange(1, D_STATE + 1, dtype=jnp.float32))[None, :], (D_INNER, 1))
        D_param = jnp.ones((D_INNER,), dtype=jnp.float32)
        out_proj_w = jax.random.normal(ks[7], (D_MODEL, D_INNER), dtype=jnp.float32) * s
        return {'x': x, 'in_proj_w': in_proj_w, 'conv_w': conv_w, 'conv_b': conv_b, 'x_proj_w': x_proj_w, 'dt_proj_w': dt_proj_w, 'dt_proj_b': dt_proj_b, 'A_log': A_log, 'D_param': D_param, 'out_proj_w': out_proj_w}
    _L1_attn_in = _L1_attn_setup()

    def _L1_ffn_setup():
        import jax, jax.numpy as jnp
        import numpy as np
        B, S, D = (2, 64, 128)
        E, K, I = (16, 8, 128)
        I_SH = 128
        ROUTE_SCALE = 2.826
        key = jax.random.key(seed)
        ks = jax.random.split(key, 8)
        s = 0.02
        return {'x': jax.random.normal(ks[0], (B, S, D), dtype=jnp.float32), 'gate_w': jax.random.normal(ks[1], (E, D), dtype=jnp.float32) * s, 'expert_bias': jnp.zeros((E,), dtype=jnp.float32), 'w_gate': jax.random.normal(ks[2], (E, I, D), dtype=jnp.float32) * s, 'w_up': jax.random.normal(ks[3], (E, I, D), dtype=jnp.float32) * s, 'w_down': jax.random.normal(ks[4], (E, D, I), dtype=jnp.float32) * s, 'shared_gate_w': jax.random.normal(ks[5], (I_SH, D), dtype=jnp.float32) * s, 'shared_up_w': jax.random.normal(ks[6], (I_SH, D), dtype=jnp.float32) * s, 'shared_down_w': jax.random.normal(ks[7], (D, I_SH), dtype=jnp.float32) * s}
    _L1_ffn_in = _L1_ffn_setup()
    _L1_c = _w((lambda *s: np.random.randn(*s).astype(np.float32) * 0.05)(1, 128))
    _L1_wmod = _w((lambda *s: np.random.randn(*s).astype(np.float32) * 0.05)(128, 6 * 128) * 128 ** (-0.5))
    _d = {'L0_attn_x': _L0_attn_in['x'], 'L0_attn_ln1_w': _L0_attn_in['ln1_w'], 'L0_attn_mu_r': _L0_attn_in['mu_r'], 'L0_attn_mu_k': _L0_attn_in['mu_k'], 'L0_attn_mu_v': _L0_attn_in['mu_v'], 'L0_attn_mu_w': _L0_attn_in['mu_w'], 'L0_attn_mu_g': _L0_attn_in['mu_g'], 'L0_attn_Wr': _L0_attn_in['Wr'], 'L0_attn_Wk': _L0_attn_in['Wk'], 'L0_attn_Wv': _L0_attn_in['Wv'], 'L0_attn_Wg': _L0_attn_in['Wg'], 'L0_attn_Wo': _L0_attn_in['Wo'], 'L0_attn_w0': _L0_attn_in['w0'], 'L0_attn_wA': _L0_attn_in['wA'], 'L0_attn_wB': _L0_attn_in['wB'], 'L0_attn_u': _L0_attn_in['u'], 'L0_attn_gn_w': _L0_attn_in['gn_w'], 'L0_attn_gn_b': _L0_attn_in['gn_b'], 'L0_attn_ln2_w': _L0_attn_in['ln2_w'], 'L0_attn_ffn_w1': _L0_attn_in['ffn_w1'], 'L0_attn_ffn_w2': _L0_attn_in['ffn_w2'], 'L0_ffn_w_switch': _L0_ffn_in['w_switch'], 'L0_ffn_b_switch': _L0_ffn_in['b_switch'], 'L0_ffn_w1': _L0_ffn_in['w1'], 'L0_ffn_b1': _L0_ffn_in['b1'], 'L0_ffn_w2': _L0_ffn_in['w2'], 'L0_ffn_b2': _L0_ffn_in['b2'], 'L0_c': _L0_c, 'L0_wmod': _L0_wmod, 'L1_attn_in_proj_w': _L1_attn_in['in_proj_w'], 'L1_attn_conv_w': _L1_attn_in['conv_w'], 'L1_attn_conv_b': _L1_attn_in['conv_b'], 'L1_attn_x_proj_w': _L1_attn_in['x_proj_w'], 'L1_attn_dt_proj_w': _L1_attn_in['dt_proj_w'], 'L1_attn_dt_proj_b': _L1_attn_in['dt_proj_b'], 'L1_attn_A_log': _L1_attn_in['A_log'], 'L1_attn_D_param': _L1_attn_in['D_param'], 'L1_attn_out_proj_w': _L1_attn_in['out_proj_w'], 'L1_ffn_gate_w': _L1_ffn_in['gate_w'], 'L1_ffn_expert_bias': _L1_ffn_in['expert_bias'], 'L1_ffn_w_gate': _L1_ffn_in['w_gate'], 'L1_ffn_w_up': _L1_ffn_in['w_up'], 'L1_ffn_w_down': _L1_ffn_in['w_down'], 'L1_ffn_shared_gate_w': _L1_ffn_in['shared_gate_w'], 'L1_ffn_shared_up_w': _L1_ffn_in['shared_up_w'], 'L1_ffn_shared_down_w': _L1_ffn_in['shared_down_w'], 'L1_c': _L1_c, 'L1_wmod': _L1_wmod}
    _x0 = _d['L0_attn_x']
    _d['L0_attn_x'] = jax.random.normal(jax.random.fold_in(jax.random.key(seed), 1), (1, 2048, 128), dtype=_x0.dtype)
    del _x0
    return _d

def reference(L0_attn_x, L0_attn_ln1_w, L0_attn_mu_r, L0_attn_mu_k, L0_attn_mu_v, L0_attn_mu_w, L0_attn_mu_g, L0_attn_Wr, L0_attn_Wk, L0_attn_Wv, L0_attn_Wg, L0_attn_Wo, L0_attn_w0, L0_attn_wA, L0_attn_wB, L0_attn_u, L0_attn_gn_w, L0_attn_gn_b, L0_attn_ln2_w, L0_attn_ffn_w1, L0_attn_ffn_w2, L0_ffn_w_switch, L0_ffn_b_switch, L0_ffn_w1, L0_ffn_b1, L0_ffn_w2, L0_ffn_b2, L0_c, L0_wmod, L1_attn_in_proj_w, L1_attn_conv_w, L1_attn_conv_b, L1_attn_x_proj_w, L1_attn_dt_proj_w, L1_attn_dt_proj_b, L1_attn_A_log, L1_attn_D_param, L1_attn_out_proj_w, L1_ffn_gate_w, L1_ffn_expert_bias, L1_ffn_w_gate, L1_ffn_w_up, L1_ffn_w_down, L1_ffn_shared_gate_w, L1_ffn_shared_up_w, L1_ffn_shared_down_w, L1_c, L1_wmod):

    def _L0_attn_ref(x, ln1_w, mu_r, mu_k, mu_v, mu_w, mu_g, Wr, Wk, Wv, Wg, Wo, w0, wA, wB, u, gn_w, gn_b, ln2_w, ffn_w1, ffn_w2):
        import jax, jax.numpy as jnp
        import numpy as np
        EPS_RMS = 1e-06
        EPS_GN = 1e-05

        def rms_norm(x, w, eps=EPS_RMS):
            var = jnp.mean(x * x, axis=-1, keepdims=True)
            return w * (x * jax.lax.rsqrt(var + eps))
        B, T, D = x.shape
        H, dk = u.shape
        h = rms_norm(x, ln1_w)
        xx = jnp.pad(h[:, :-1], ((0, 0), (1, 0), (0, 0))) - h
        xr = h + xx * mu_r
        xk = h + xx * mu_k
        xv = h + xx * mu_v
        xw = h + xx * mu_w
        xg = h + xx * mu_g
        r = (xr @ Wr).reshape(B, T, H, dk)
        k = (xk @ Wk).reshape(B, T, H, dk)
        v = (xv @ Wv).reshape(B, T, H, dk)
        g = jax.nn.silu(xg @ Wg)
        w = w0 + jnp.tanh(xw @ wA) @ wB
        decay = jnp.exp(-jnp.exp(w)).reshape(B, T, H, dk)
        rT = jnp.moveaxis(r, 1, 0)
        kT = jnp.moveaxis(k, 1, 0)
        vT = jnp.moveaxis(v, 1, 0)
        dT = jnp.moveaxis(decay, 1, 0)

        def step(S, inps):
            rt, kt, vt, dt = inps
            kv = kt[..., :, None] * vt[..., None, :]
            o = jnp.einsum('bhk,bhkv->bhv', rt, S + u[None, :, :, None] * kv)
            S = dt[..., None] * S + kv
            return (S, o)
        S0 = jnp.zeros((B, H, dk, dk), x.dtype)
        _, oT = jax.lax.scan(step, S0, (rT, kT, vT, dT))
        o = jnp.moveaxis(oT, 0, 1)
        mean = jnp.mean(o, axis=-1, keepdims=True)
        var = jnp.var(o, axis=-1, keepdims=True)
        o = (o - mean) * jax.lax.rsqrt(var + EPS_GN) * gn_w + gn_b
        o = (o * g.reshape(B, T, H, dk)).reshape(B, T, D)
        x = x + o @ Wo
        h2 = rms_norm(x, ln2_w)
        x = x + jax.nn.gelu(h2 @ ffn_w1, approximate=False) @ ffn_w2
        return x

    def _L0_ffn_ref(input, w_switch, b_switch, w1, b1, w2, b2):
        import jax, jax.numpy as jnp
        import numpy as np
        D_MODEL = 128
        EXPERT_DIM = 512
        N_EXPERTS = 8
        CAP_FACTOR = 0.5
        B, S, D = input.shape
        T = B * S
        E = b_switch.shape[0]
        capacity = int(CAP_FACTOR * T / E)
        x = input.reshape(T, D)
        logits = x @ w_switch + b_switch
        probs = jax.nn.softmax(logits, axis=-1)
        pmax = probs.max(axis=-1)
        routes = probs.argmax(axis=-1)
        oh = (routes[:, None] == jnp.arange(E)[None, :]).astype(jnp.int32)
        pos = (jnp.cumsum(oh, axis=0) * oh).sum(-1) - 1
        keep = pos < capacity
        slot = jnp.where(keep, routes * capacity + pos, E * capacity)
        buf = jnp.zeros((E * capacity + 1, D), x.dtype).at[slot].set(x)
        buf_e = buf[:E * capacity].reshape(E, capacity, D)
        h = jax.nn.relu(jnp.einsum('ecd,edh->ech', buf_e, w1) + b1[:, None, :])
        y = jnp.einsum('ech,ehd->ecd', h, w2) + b2[:, None, :]
        y_flat = jnp.concatenate([y.reshape(E * capacity, D), jnp.zeros((1, D), x.dtype)], axis=0)
        out = jnp.where(keep[:, None], y_flat[slot], x)
        scale = pmax / jax.lax.stop_gradient(pmax)
        out = out * scale[:, None]
        return out.reshape(B, S, D)

    def _L1_attn_ref(x, in_proj_w, conv_w, conv_b, x_proj_w, dt_proj_w, dt_proj_b, A_log, D_param, out_proj_w):
        import jax, jax.numpy as jnp
        import numpy as np
        B, L, D_MODEL = (2, 128, 128)
        D_STATE, D_CONV, EXPAND = (16, 4, 2)
        D_INNER = D_MODEL * EXPAND
        DT_RANK = (D_MODEL + 15) // 16

        def _silu(v):
            return v * jax.nn.sigmoid(v)

        def _mamba_fwd(x, in_proj_w, conv_w, conv_b, x_proj_w, dt_proj_w, dt_proj_b, A_log, D_param, out_proj_w):
            b, l, _ = x.shape
            d_inner = D_param.shape[0]
            d_state = A_log.shape[1]
            dt_rank = dt_proj_w.shape[1]
            xz = jnp.einsum('bld,ed->ble', x, in_proj_w)
            xb, zb = (xz[..., :d_inner], xz[..., d_inner:])
            u = jax.lax.conv_general_dilated(jnp.transpose(xb, (0, 2, 1)), conv_w, window_strides=(1,), padding=[(conv_w.shape[-1] - 1, 0)], feature_group_count=d_inner, dimension_numbers=('NCH', 'OIH', 'NCH'))
            u = jnp.transpose(u, (0, 2, 1)) + conv_b
            u = _silu(u)
            proj = jnp.einsum('bld,ed->ble', u, x_proj_w)
            dt_raw = proj[..., :dt_rank]
            b_raw = proj[..., dt_rank:dt_rank + d_state]
            c_raw = proj[..., dt_rank + d_state:dt_rank + 2 * d_state]
            a_gate_raw = proj[..., dt_rank + 2 * d_state:]
            dt = jax.nn.softplus(jnp.einsum('blr,er->ble', dt_raw, dt_proj_w) + dt_proj_b)
            a_base = -jnp.exp(A_log)
            a_gate = jax.nn.sigmoid(a_gate_raw)

            def step(state, inp):
                dt_t, u_t, b_t, c_t, g_t = inp
                a = a_base[None] * (0.5 + g_t)[..., None]
                decay = jnp.exp(dt_t[..., None] * a)
                state = decay * state + dt_t[..., None] * b_t[:, None, :] * u_t[..., None]
                y_t = jnp.sum(state * c_t[:, None, :], axis=-1) + D_param * u_t
                return (state, y_t)
            tm = lambda v: jnp.moveaxis(v, 1, 0)
            state0 = jnp.zeros((b, d_inner, d_state), dtype=x.dtype)
            _, ys = jax.lax.scan(step, state0, (tm(dt), tm(u), tm(b_raw), tm(c_raw), tm(a_gate)))
            y = jnp.moveaxis(ys, 0, 1)
            y = y * _silu(zb)
            return jnp.einsum('ble,de->bld', y, out_proj_w)
        return _mamba_fwd(x, in_proj_w, conv_w, conv_b, x_proj_w, dt_proj_w, dt_proj_b, A_log, D_param, out_proj_w)

    def _L1_ffn_ref(x, gate_w, expert_bias, w_gate, w_up, w_down, shared_gate_w, shared_up_w, shared_down_w):
        import jax, jax.numpy as jnp
        import numpy as np
        B, S, D = (2, 64, 128)
        E, K, I = (16, 8, 128)
        I_SH = 128
        ROUTE_SCALE = 2.826
        gates = jnp.einsum('bsd,ed->bse', x, gate_w)
        scores = jax.nn.sigmoid(gates.astype(jnp.float32))
        sel_scores = scores + expert_bias
        _, inds = jax.lax.top_k(sel_scores, K)
        selected = jnp.take_along_axis(scores, inds, axis=-1)
        selected = selected / selected.sum(axis=-1, keepdims=True)
        selected = selected * ROUTE_SCALE
        onehot = jax.nn.one_hot(inds, E, dtype=selected.dtype)
        combine = jnp.einsum('bske,bsk->bse', onehot, selected)
        hg = jnp.einsum('bsd,eid->bsei', x, w_gate)
        hu = jnp.einsum('bsd,eid->bsei', x, w_up)
        h = jax.nn.silu(hg) * hu
        ye = jnp.einsum('bsei,edi->bsed', h, w_down)
        y = jnp.einsum('bsed,bse->bsd', ye, combine).astype(x.dtype)
        g = jnp.einsum('bsd,id->bsi', x, shared_gate_w)
        u = jnp.einsum('bsd,id->bsi', x, shared_up_w)
        y = y + jnp.einsum('bsi,di->bsd', jax.nn.silu(g) * u, shared_down_w)
        return y
    x = L0_attn_x
    mod = (_silu(L0_c) @ L0_wmod).reshape(L0_c.shape[0], 6, 1, -1)
    sa, ca, ga, sb, cb, gb = (mod[:, 0], mod[:, 1], mod[:, 2], mod[:, 3], mod[:, 4], mod[:, 5])
    ga = (2 * (ga >= 0) - 1) * jnp.maximum(jnp.abs(ga), 0.25)
    gb = (2 * (gb >= 0) - 1) * jnp.maximum(jnp.abs(gb), 0.25)
    h = _layernorm(x, axis=-1) * (1 + ca) + sa
    x = x + ga * _L0_attn_ref(h, L0_attn_ln1_w, L0_attn_mu_r, L0_attn_mu_k, L0_attn_mu_v, L0_attn_mu_w, L0_attn_mu_g, L0_attn_Wr, L0_attn_Wk, L0_attn_Wv, L0_attn_Wg, L0_attn_Wo, L0_attn_w0, L0_attn_wA, L0_attn_wB, L0_attn_u, L0_attn_gn_w, L0_attn_gn_b, L0_attn_ln2_w, L0_attn_ffn_w1, L0_attn_ffn_w2)
    h = _layernorm(x, axis=-1) * (1 + cb) + sb
    x = x + gb * _L0_ffn_ref(h, L0_ffn_w_switch, L0_ffn_b_switch, L0_ffn_w1, L0_ffn_b1, L0_ffn_w2, L0_ffn_b2)
    mod = (_silu(L1_c) @ L1_wmod).reshape(L1_c.shape[0], 6, 1, -1)
    sa, ca, ga, sb, cb, gb = (mod[:, 0], mod[:, 1], mod[:, 2], mod[:, 3], mod[:, 4], mod[:, 5])
    ga = (2 * (ga >= 0) - 1) * jnp.maximum(jnp.abs(ga), 0.25)
    gb = (2 * (gb >= 0) - 1) * jnp.maximum(jnp.abs(gb), 0.25)
    h = _layernorm(x, axis=-1) * (1 + ca) + sa
    x = x + ga * _L1_attn_ref(h, L1_attn_in_proj_w, L1_attn_conv_w, L1_attn_conv_b, L1_attn_x_proj_w, L1_attn_dt_proj_w, L1_attn_dt_proj_b, L1_attn_A_log, L1_attn_D_param, L1_attn_out_proj_w)
    h = _layernorm(x, axis=-1) * (1 + cb) + sb
    x = x + gb * _L1_ffn_ref(h, L1_ffn_gate_w, L1_ffn_expert_bias, L1_ffn_w_gate, L1_ffn_w_up, L1_ffn_w_down, L1_ffn_shared_gate_w, L1_ffn_shared_up_w, L1_ffn_shared_down_w)
    return x

_drawn_inputs = setup_inputs


def setup_inputs(seed=0):
    import zlib

    import numpy as np

    out = dict(_drawn_inputs(seed))
    spreads = {'L0_attn_ln1_w': (1.0, 0.6),
     'L0_attn_gn_w': (1.0, 0.6),
     'L0_attn_gn_b': (0.0, 0.8),
     'L0_attn_ln2_w': (1.0, 0.6),
     'L0_ffn_b_switch': (0.0, 0.1),
     'L0_ffn_b1': (0.0, 0.8),
     'L0_ffn_b2': (0.0, 0.475),
     'L1_attn_D_param': (1.0, 0.6),
     'L1_ffn_expert_bias': (0.0, 2.0)}
    factors = {'L0_attn_mu_r': 6.191,
     'L0_attn_mu_k': 5.656,
     'L0_attn_mu_v': 6.191,
     'L0_attn_mu_w': 8.0,
     'L0_attn_mu_g': 6.77,
     'L0_attn_Wr': 3.894,
     'L0_attn_Wk': 4.399,
     'L0_attn_Wv': 5.981,
     'L0_attn_Wg': 4.39,
     'L0_attn_Wo': 5.522,
     'L0_attn_w0': 7.041,
     'L0_attn_wA': 8.0,
     'L0_attn_wB': 8.0,
     'L0_attn_u': 6.849,
     'L0_attn_ffn_w1': 2.78,
     'L0_ffn_w1': 5.383,
     'L0_ffn_w2': 4.178,
     'L1_attn_in_proj_w': 8.0,
     'L1_attn_conv_w': 8.0,
     'L1_attn_conv_b': 8.0,
     'L1_attn_x_proj_w': 8.0,
     'L1_attn_dt_proj_w': 8.0,
     'L1_attn_dt_proj_b': 8.0,
     'L1_attn_A_log': 8.0,
     'L1_attn_out_proj_w': 8.0,
     'L1_ffn_gate_w': 64.0,
     'L1_ffn_w_gate': 57.75,
     'L1_ffn_w_up': 50.264,
     'L1_ffn_w_down': 50.403,
     'L1_ffn_shared_gate_w': 64.0,
     'L1_ffn_shared_up_w': 56.354,
     'L1_ffn_shared_down_w': 57.127,
     'L1_c': 8.0,
     'L1_wmod': 8.0}
    for name, (base, spread) in spreads.items():
        noise = np.random.default_rng([zlib.crc32(name.encode()), seed]).standard_normal(out[name].shape)
        drawn = base * np.exp(spread * noise) if base else spread * noise
        out[name] = jnp.asarray(drawn.astype(out[name].dtype))
    for name, factor in factors.items():
        out[name] = (out[name] * factor).astype(out[name].dtype)
    return out
```

```python
from contextlib import ExitStack

import concourse.bass as bass
from concourse import mybir

P = 128
T = 2048
N = 512
NCH = T // N
NT = T // P
H, DK = 16, 8
LORA = 64
F = 512
NF = F // P
E0 = 8
CAP = int(0.5 * T / E0)
EPS_LN, EPS_RMS, EPS_GN = 1e-5, 1e-6, 1e-5
GATE_FLOOR = 0.25

NS = 16
DI = 2
KC = 4
DTR = 8
E1, TOPK = 16, 8
ROUTE_SCALE = 2.826
VEC = ["ln1_w", "mu_r", "mu_k", "mu_v", "mu_w", "mu_g", "w0", "u", "gn_w", "gn_b", "ln2_w",
       "c0", "c1", "eps5", "eps6",
       "dt_b0", "dt_b1", "D0", "D1", "cb0", "cb1"] + [f"cw{c}_{j}" for c in range(DI) for j in range(KC)] + \
    [f"A{c}_{n}" for c in range(DI) for n in range(NS)]
CORE = {"centre": P, "mean": P, "eye": P}
CST = {"head_sum": P, "gn_mean": P, "gn_centre": P, "reduce": 2 * 32, "spread": 2 * P}
CSTB = {"iota": E0 * CAP, "tri": P, "ones": P, "rank": NT * E0, "seg": NT * E0, "iota_p": E0, "b_switch": NT * E0,
        "w_switch": E0, "b1": E0 * NF, "b2": E0 * P}
WC = {"in": 2 * DI * P, "xp": DI * (DI * P + 3 * 2 * NS + DTR), "dtp": DI * P, "out": DI * P, "gate": E1, "g_bias": NT * E1, "g_seg": NT * E1}
XPW = DI * P + 3 * 2 * NS + DTR
WA = {"Wr": P, "Wk": P, "Wv": P, "Wg": P, "Wo": P, "wA": LORA, "wB": P, "w1": F, "w2": F}


def columns(widths):
    at, out = 0, {}
    for name, w in widths.items():
        out[name] = (at, w)
        at += w
    return out, at


def each_chunk(*steps):
    return [(s, i) for i in range(NCH) for s in steps]


def layernorm(k):
    return ([(f"centre{k}", i) for i in range(NCH)] + [(f"var{k}", i) for i in range(NCH)],
            [(f"sq{k}", i) for i in range(NCH)] + each_chunk(f"ln{k}", f"rs{k}"),
            each_chunk(f"norm{k}", f"mod{k}"))


def rmsnorm(k):
    return (each_chunk(f"ms{k}"), [(f"sq{k}", i) for i in range(NCH)] + each_chunk(f"ln{k}", f"rs{k}"),
            each_chunk(f"norm{k}"))


WAVES = [[0, 2, 4, 6], [1, 3, 5, 7]]


def one(*steps):
    return [(s, 0) for s in steps]


def sequences():
    pe, act, dve, pool = [], [], [], []

    def add(to, *parts):
        for part in parts:
            to.extend(part)

    ln_pe, ln_act, ln_dve = layernorm("A")
    rm_pe, rm_act, rm_dve = rmsnorm("B")
    add(pe, one("mod"), ln_pe, rm_pe, *(each_chunk(s) for s in ["r", "k", "v", "lora_a", "g", "lora_b", "head_ruk"]))
    add(act, one("c_exp"), ln_act, rm_act, *(each_chunk(s) for s in ["r_copy", "k_copy", "v_copy", "lora_tanh", "g_silu"]),
        each_chunk("w_exp", "decay"))
    add(dve, one("c_one", "c_recip", "c_silu", "mod_copy", "mod_ca", "mod_sign", "mod_sign2", "mod_abs", "mod_floor", "mod_gate"),
        ln_dve, rm_dve, *(each_chunk(s) for s in ["xx", "mix_r", "mix_k", "mix_v", "mix_w", "mix_g", "ruk", "bonus"]), one("s_zero"))
    add(pool, one("h1_zero"))
    for i in range(NCH):
        act.append(("v_chunk", i))
        pe += [(f"spread{v}", i) for v in WAVES[0]]
        if i:
            pe += [(f"reduce{v}", i - 1) for v in WAVES[1]]
        pe += [(f"spread{v}", i) for v in WAVES[1]] + [(f"reduce{v}", i) for v in WAVES[0]]
        for w in range(2):
            dve += [(f"kv{v}", i) for v in WAVES[w]]
            if i and w == 0:
                dve.append(("o", i - 1))
            dve += [(f"scan{v}", i) for v in WAVES[w]]
            pool += [(f"prod{v}", i) for v in WAVES[w]]
    pe += [(f"reduce{v}", NCH - 1) for v in WAVES[1]]
    dve.append(("o", NCH - 1))
    rm_pe, rm_act, rm_dve = rmsnorm("C")
    add(pe, each_chunk("gn_centred"), each_chunk("gn_var"), each_chunk("wo"), rm_pe,
        each_chunk(*[f"up{f}" for f in range(NF)], *[f"down{f}" for f in range(NF)]))
    add(act, each_chunk("gn_sq"), each_chunk("gn_ln", "gn_rs", "gn_rs2"), rm_act, each_chunk(*[f"gelu{f}" for f in range(NF)]))
    add(dve, each_chunk("gn_err", "gn_half", "gn_rsqrt", "gn_norm", "gn_affine", "gn_gate"), each_chunk("x1"), rm_dve, each_chunk("ffn_sum", "x_attn"))

    ln_pe, ln_act, ln_dve = layernorm("D")
    add(pe, ln_pe, one("router"), [("h_turn", t) for t in range(NT)], one("prefix", "totals"), each_chunk("slot_spread"),
        [("dispatch", t) for t in range(NT)], [(s, e) for e in range(E0) for s in ("e_up", "e_down")],
        each_chunk("scale_spread"), [("combine", i) for i in range(NCH)])
    add(act, ln_act, one("r_exp"), [("h_turned", q) for q in range(NCH)], each_chunk("slots"),
        [("scale_diag", t) for t in range(NT)], one("buf0"), each_chunk("scales"))
    add(dve, ln_dve, one(*R_STEPS), [("slot_diag", t) for t in range(NT)], [("onehot", t) for t in range(NT)], one("buf1"),
        [(s, e) for e in range(E0) for s in ("e_relu", "e_out")],
        [(s, i) for i in range(NCH) for s in [f"place{e}" for e in range(E0)] + ["kept_x", "moe_sum", "moe_scaled", "x_moe"]])

    ln_pe, ln_act, ln_dve = layernorm("E")
    add(pe, ln_pe, *(each_chunk(s) for s in ["xb0", "xb1", "z0", "z1", "gate0", "gate1", "bc", "dt_raw", "dt0", "dt1"]))
    add(act, ln_act, *(each_chunk(s) for s in ["xb0_copy", "xb1_copy", "z0_silu", "z1_silu", "u0", "u1", "gate0_tanh", "gate1_tanh"]),
        each_chunk("bc_hi"), each_chunk("bc_mid"), each_chunk("bc_mid2"), each_chunk("dt_raw_copy"), one("a_exp"),
        [(f"{s}_{c}", i) for c in range(2) for i in range(NCH) for s in ("sp_e", "sp_ln", "sp_e2", "sp_e4")])
    add(dve, ln_dve, one("xb_zero"), [(f"conv{c}_{j}", i) for c in range(2) for i in range(NCH) for j in range(4)],
        each_chunk("bc_r1"), each_chunk("bc_lo"), one("a_neg", "st_zero"))
    for c in range(2):
        for i in range(NCH):
            dve += [(f"{s}_{c}", i) for s in ("sp_z", "sp_abs")]
        for i in range(NCH):
            dve += [(f"sp_p1_{c}", i)]
        for i in range(NCH):
            dve += [(f"{s}_{c}", i) for s in ("sp_p3", "sp_lo", "sp_h5")]
        for i in range(NCH):
            dve += [(f"{s}_{c}", i) for s in ("sp_max", "sp_min", "dt", "gate_half")]
        for i in range(NCH):
            pool += [(f"sp_p2_{c}", i)]
        for i in range(NCH):
            pool += [(f"sp_hi_{c}", i)]
        for i in range(NCH):
            pool += [(f"{s}_{c}", i) for s in ("dtg", "du")]
    for i in range(NCH):
        for n in range(NS):
            act += [(f"c_copy{n}", i), (f"dec{n}_0", i), (f"dec{n}_1", i)]
            dve += [(f"dbu{n}_0", i), (f"dbu{n}_1", i), (f"st{n}_0", i), (f"st{n}_1", i)]
            pool += [(f"sc{n}_0", i), (f"sc{n}_1", i)]
            pe += [(f"b{n}", i), (f"c{n}", i)]
            if n:
                pe += [(f"y{n - 1}_0", i), (f"y{n - 1}_1", i)]
            if i and n == 2:
                dve += [("skip_0", i - 1), ("skip_1", i - 1)]
                pool += [("gated_0", i - 1), ("gated_1", i - 1)]
        pe += [(f"y{NS - 1}_0", i), (f"y{NS - 1}_1", i)]
    dve += [("skip_0", NCH - 1), ("skip_1", NCH - 1)]
    pool += [("gated_0", NCH - 1), ("gated_1", NCH - 1)]
    add(pe, each_chunk("m_out"))
    add(dve, each_chunk("x_mamba"))

    ln_pe, ln_act, ln_dve = layernorm("F")
    add(pe, ln_pe, one("g_router"), [("g_turn", t) for t in range(NT)])
    add(act, ln_act, one("g_exp"), [("g_turned", h) for h in range(2)])
    add(dve, ln_dve, one(*G_STEPS))
    for i in range(NCH):
        for e in range(E1 + 1):
            pe += [(f"hg{e}", i), (f"hu{e}", i)] + ([(f"w{e}", i)] if e < E1 else [])
            if e:
                pe.append((f"hd{e - 1}", i))
            act.append((f"silu{e}", i))
            dve += [(f"hh{e}", i)] + ([(f"hw{e}", i)] if e < E1 else [])
        pe.append((f"hd{E1}", i))
        dve.append(("x_out", i))
    return {"pe": pe, "act": act, "dve": dve, "pool": pool}


R_STEPS = ["r_logit", "r_max", "r_shift", "r_sum", "r_recip", "r_prob", "r_pmax", "r_hit", "r_rank", "r_best", "r_oh",
           "r_precip", "r_scale", "r_tot", "r_cum", "r_off", "r_pos", "r_own", "r_place", "r_keep", "r_base", "r_slot", "r_kept"]
G_STEPS = ["g_one", "g_score", "g_sel"] + [f"g_top{t}" for t in range(NT)] + \
    ["g_gt", "g_eq", "g_ngt", "g_left", "g_cum", "g_le", "g_tie", "g_mask", "g_pick", "g_total", "g_inv", "g_w",
     "g_zero", "g_hi", "g_r1", "g_mid", "g_lo"]


def build(nc, X_in, vec_in, core_in, cst_in, wA_in, wmod_in, cstB_in, wB1_in, wB2_in, wC_in, sel_in, eyeb_in, wD_in, out):
    f32 = mybir.dt.float32
    bf16 = mybir.dt.bfloat16
    ALU = mybir.AluOpType
    ACT = mybir.ActivationFunctionType
    AX = mybir.AxisListType.X
    SEQ = sequences()
    count = {step: (e, k + 1) for e, steps in SEQ.items() for k, step in enumerate(steps)}
    assert len(count) == sum(map(len, SEQ.values()))
    core_at, core_n = columns(CORE)
    cst_at, cst_n = columns(CST)
    wa_at, wa_n = columns(WA)
    cb_at, cb_n = columns(CSTB)
    wc_at, wc_n = columns(WC)

    ctx = ExitStack()
    with ctx:
        def sb(name, shape, dt=f32):
            return ctx.enter_context(nc.sbuf_tensor(name, shape, dt))

        def sem(name):
            return ctx.enter_context(nc.semaphore(name))

        x_loaded, vec_loaded, core_loaded, wa_loaded, wb_loaded, wc_loaded, wd_loaded, out_stored = map(
            sem, ["x_loaded", "vec_loaded", "core_loaded", "wa_loaded", "wb_loaded", "wc_loaded", "wd_loaded", "out_stored"])
        finished = {e: sem(f"{e}_done") for e in SEQ}
        order = {e: list(steps) for e, steps in SEQ.items()}

        def upto(step, i=0):
            engine, n = count[step, i]
            return finished[engine], n

        def done(step, i=0):
            engine, n = count[step, i]
            assert order[engine].pop(0) == (step, i), (step, i)
            return finished[engine], 1

        X = sb("x", [P, T])
        vec = sb("vec", [P, len(VEC)])
        core = sb("core", [P, core_n])
        mod = sb("mod", [P, 12])
        mtmp = sb("mtmp", [P, 24])
        wC = sb("wC", [P, wc_n])
        sel = sb("sel", [96, 2 * NS, P], bf16)
        BC = sb("bc", [96, T], bf16)
        wD = sb("wD", [P, 3 * (E1 + 1), P])
        EYEB = sb("eyeb", [P, P], bf16)
        CARRY = sb("carry", [P, 1])
        ABASE = sb("abase", [P, DI * NS])
        ARENA = sb("arena", [P, 38600])
        ps = ctx.enter_context(nc.psum_tensor("ps", [P, 8 * N], f32))

        def col(name):
            k = VEC.index(name)
            return vec[:, k:k + 1]

        def area(at, n):
            return ARENA[:, at:at + n]

        def CORE_(name):
            a, w = core_at[name]
            return core[:, a:a + w]

        def C(name, part=slice(None)):
            a, w = cst_at[name]
            return cst[part, a:a + w]

        def W(name, part=slice(None)):
            a, w = wa_at[name]
            return wA[part, a:a + w]

        def CB_(name):
            a, w = cb_at[name]
            return cstB[:, a:a + w]

        def WC_(name):
            a, w = wc_at[name]
            return wC[:, a:a + w]

        SV = T + 1
        S = area(0, DK * SV).rearrange("p (v t) -> p v t", v=DK)
        H1 = area(0, T + 1)
        XX = area(1 * 2052, T)
        M0 = area(2 * 2052, T)
        M1 = area(3 * 2052, T)
        at = DK * SV
        HLN, M2, K, R, DEC, V, G = (area(at + j * T, T) for j in range(7))
        at += 7 * T
        KV = area(at, 4 * N).rearrange("p (s t) -> p s t", s=4)
        PR = area(at + 4 * N, 4 * N).rearrange("p (s t) -> p s t", s=4)
        VC = area(at + 8 * N, N)
        TA = area(at + 4 * N, T)
        T1, T2, T3 = K, R, DEC
        O = BONUS = M2
        GEL = PR
        at += 9 * N
        wA = area(at, wa_n)
        cst = area(at + wa_n, cst_n)
        assert at + wa_n + cst_n <= 38600, at + wa_n + cst_n
        wmod = area(4 * 2052, 2 * 6 * P).rearrange("p (l k) -> p l k", l=2)

        cstB = area(0, cb_n)
        assert cb_n <= 2780
        PT = area(4100, 8 * N).rearrange("p (e t) -> p e t", e=E0)
        WB = area(8200, 8192)
        w1B = WB[:, 0:4096].rearrange("p (e f) -> p e f", e=E0)
        w2B = WB[:, 4096:8192].rearrange("p (e f m) -> p e f m", e=E0, f=NF)
        TB, HB, HT, SLB, SCB, DG = DEC, V, G, M2, K, R
        DG2 = HLN
        OH1 = DEC.rearrange("p (s c) -> p s c", s=2)
        at = DK * SV + 7 * T
        BUF = area(at, E0 * CAP)
        HS = area(at + 1024, 2 * N).rearrange("p (s f t) -> p s f t", s=2, f=NF)
        YB = area(at + 2048, E0 * P).rearrange("p (e m) -> p e m", e=E0)
        small = lambda k: area(2780 + k * P, P)
        small3 = lambda k: small(k).rearrange("p (t e) -> p t e", e=E0)
        tiny = lambda k: area(at + 3072 + k * NT, NT)

        ST = area(0, 32 * N).rearrange("p (k t) -> p k t", k=32)
        TE = area(8200, T)
        HC = area(10248, T)
        XBP = area(12296, DI * (T + 3)).rearrange("p (c t) -> p c t", c=DI)
        CV = area(0, DI * T).rearrange("p (c t) -> p c t", c=DI)
        at = 16400
        U, Z, DTG, DU = (area(at + j * DI * T, DI * T).rearrange("p (c t) -> p c t", c=DI) for j in range(4))
        at += 4 * DI * T
        CBR = area(at, 2 * N).rearrange("p (s t) -> p s t", s=2)
        DECR = area(at + 2 * N, 3 * N).rearrange("p (s t) -> p s t", s=3)
        DBU = area(at + 5 * N, 2 * N).rearrange("p (s t) -> p s t", s=2)
        PRC = area(at + 7 * N, 4 * N).rearrange("p (s t) -> p s t", s=4)
        assert at + 11 * N <= 38600, at + 11 * N
        R1 = area(at, T)
        DRAW = area(at + T, T)
        SPZ, SPA, SPE, SPL, SPE2, SPP, SPH, DT = (area(j * T, T) for j in range(8))

        TF, HD = area(0, T), area(T, T)
        SG = area(2 * T, 2 * N).rearrange("p (s t) -> p s t", s=2)
        HH = area(2 * T + 2 * N, 2 * N).rearrange("p (s t) -> p s t", s=2)
        HW = area(2 * T + 4 * N, 2 * N).rearrange("p (s t) -> p s t", s=2)
        gsmall = lambda k: area(2 * T + 6 * N + k * 256, 256)
        gsmall3 = lambda k: gsmall(k).rearrange("p (t e) -> p t e", e=E1)
        gtiny = lambda k: area(2 * T + 6 * N + 16 * 256 + k * NT, NT)
        CS = area(2 * T + 6 * N + 17 * 256, NT * 96 // 2).bitcast(bf16).rearrange("p (t r) -> p t r", t=NT)

        def ch(buf, i, off=0):
            return buf[:, i * N + off:(i + 1) * N + off]

        def half(h, i, rows=P):
            return ps[0:rows, (4 * h + i) * N:(4 * h + i + 1) * N]

        def bank(b, lo=0, hi=P):
            return ps[lo:hi, b * N:(b + 1) * N]

        modcol = lambda layer, k: mod[:, 6 * layer + k:6 * layer + k + 1]
        SA, CA, GA, SB_, CB, GB = range(6)

        block = ctx.enter_context(nc.Block())

        def bcast(col2, e):
            return col2.unsqueeze(2).to_broadcast([P, col2.shape[1], e])

        @block.sync
        def _(sp):
            sp.dma_start(X[:], X_in).then_inc(x_loaded, 16)
            sp.dma_start(vec[:], vec_in).then_inc(vec_loaded, 16)
            sp.dma_start(wmod, wmod_in).then_inc(vec_loaded, 16)
            sp.dma_start(core[:], core_in).then_inc(core_loaded, 16)
            sp.dma_start(cst, cst_in).then_inc(core_loaded, 16)
            sp.dma_start(wA, wA_in).then_inc(wa_loaded, 16)
            sp.dma_start(wC[:], wC_in).then_inc(wc_loaded, 16)
            sp.dma_start(EYEB[:], eyeb_in).then_inc(wc_loaded, 16)
            sp.dma_start(sel[:], sel_in).then_inc(wc_loaded, 16)
            sp.dma_start(wD[:], wD_in).then_inc(wd_loaded, 16)
            sp.wait_ge(*upto("prod7", NCH - 1))
            sp.wait_ge(*upto("o", NCH - 1))
            sp.dma_start(cstB, cstB_in).then_inc(wb_loaded, 16)
            sp.dma_start(w1B, wB1_in).then_inc(wb_loaded, 16)
            sp.dma_start(w2B, wB2_in).then_inc(wb_loaded, 16)
            for i in range(NCH):
                sp.wait_ge(*upto("x_out", i))
                sp.dma_start(out[:, i * N:(i + 1) * N], X[:, i * N:(i + 1) * N]).then_inc(out_stored, 16)
            sp.wait_ge(out_stored, 16 * NCH)

        @block.tensor
        def _(pe):
            mm = nc.tensor.matmul

            def sweep(step, lhsT, rhs, h, waits, rows=P, parts=P):
                for i in range(NCH):
                    for w in waits:
                        pe.wait_ge(*upto(w, i))
                    mm(half(h, i, rows), lhsT, ch(rhs, i)[0:parts], start=True, stop=True).then_inc(*done(step, i))

            pe.wait_ge(vec_loaded, 32)
            pe.wait_ge(*upto("c_silu"))
            for layer in range(2):
                for k in range(6):
                    j = 6 * layer + k
                    last = mm(ps[:, 7 * N + j:7 * N + j + 1], wmod[:, layer, k * P:(k + 1) * P],
                              mtmp[:, 4 + layer:5 + layer], start=True, stop=True)
            last.then_inc(*done("mod"))
            pe.wait_ge(core_loaded, 32)
            pe.wait_ge(x_loaded, 16)
            sweep("centreA", CORE_("centre"), X, 0, [])
            pe.wait_ge(*upto("mod_copy"))
            sweep("varA", CORE_("mean"), T1, 1, ["sqA"])
            sweep("msB", CORE_("mean"), T2, 0, ["sqB", "normA"])
            pe.wait_ge(wa_loaded, 16)
            sweep("r", W("Wr"), M0, 1, ["mix_r", "lnA"])
            sweep("k", W("Wk"), M1, 0, ["mix_k", "lnB"])
            sweep("v", W("Wv"), M2, 1, ["mix_v", "r_copy"])
            sweep("lora_a", W("wA"), M0, 0, ["mix_w", "k_copy"], rows=LORA)
            sweep("g", W("Wg"), M1, 1, ["mix_g", "v_copy"])
            sweep("lora_b", W("wB", slice(0, LORA)), TA, 0, ["lora_tanh"], parts=LORA)
            sweep("head_ruk", C("head_sum"), XX, 1, ["ruk", "g_silu"])

            def spread(w, i):
                for k, v in enumerate(WAVES[w]):
                    if w:
                        pe.wait_ge(*upto(f"kv{WAVES[0][k]}", i))
                    elif i:
                        pe.wait_ge(*upto(f"kv{WAVES[1][k]}", i - 1))
                    j = 32 * (v // 2)
                    a = cst_at["spread"][0] + (v % 2) * P
                    mm(bank(4 + k), cst[j:j + 32, a:a + P], VC[j:j + 32, :], start=True, stop=True).then_inc(*done(f"spread{v}", i))

            def reduce(w, i):
                for k, v in enumerate(WAVES[w]):
                    pe.wait_ge(*upto(f"prod{WAVES[w][3]}", i))
                    if w == 0 and i >= 2:
                        pe.wait_ge(*upto("o", i - 2))
                    a = cst_at["reduce"][0] + (v % 2) * 32
                    j = 32 * (v // 2)
                    mm(bank(i % 2, j, j + 32), cst[:, a:a + 32], PR[:, k, :], start=(w == 0), stop=(w == 1)).then_inc(*done(f"reduce{v}", i))

            pe.wait_ge(*upto("bonus", NCH - 1))
            pe.wait_ge(*upto("w_exp", NCH - 1))
            for i in range(NCH):
                pe.wait_ge(*upto("v_chunk", i))
                spread(0, i)
                if i:
                    reduce(1, i - 1)
                spread(1, i)
                reduce(0, i)
            reduce(1, NCH - 1)

            pe.wait_ge(*upto("kv7", NCH - 1))
            sweep("gn_centred", C("gn_centre"), O, 1, ["o"])
            pe.wait_ge(*upto("o", NCH - 1))
            sweep("gn_var", C("gn_mean"), T1, 0, ["gn_sq"])
            sweep("wo", W("Wo"), O, 1, ["gn_gate"])
            sweep("msC", CORE_("mean"), T2, 0, ["sqC", "gn_err"])
            pe.wait_ge(*upto("lnC", NCH - 1))
            pe.wait_ge(*upto("x1", NCH - 1))
            for i in range(NCH):
                pe.wait_ge(*upto("normC", i))
                for f in range(NF):
                    if i:
                        pe.wait_ge(*upto(f"gelu{f}", i - 1))
                    a = wa_at["w1"][0] + f * P
                    mm(bank(4 + f), wA[:, a:a + P], ch(M0, i), start=True, stop=True).then_inc(*done(f"up{f}", i))
                for f in range(NF):
                    pe.wait_ge(*upto(f"gelu{f}", i))
                    a = wa_at["w2"][0] + f * P
                    mm(half(0, i), wA[:, a:a + P], GEL[:, f, :], start=(f == 0), stop=(f == NF - 1)).then_inc(*done(f"down{f}", i))

            pe.wait_ge(*upto("gelu3", NCH - 1))
            sweep("centreD", CORE_("centre"), X, 1, ["x_attn"])
            sweep("varD", CORE_("mean"), TB, 0, ["sqD", "ffn_sum"])
            pe.wait_ge(wb_loaded, 48)
            pe.wait_ge(*upto("modD", NCH - 1))
            pe.wait_ge(*upto("lnD", NCH - 1))
            for t in range(NT):
                last = mm(ps[:, t * E0:(t + 1) * E0], HB[:, t * P:(t + 1) * P], CB_("w_switch"), start=True, stop=True)
            last.then_inc(*done("router"))
            for t in range(NT):
                nc.tensor.transpose(ps[:, 4 * N + t * P:4 * N + (t + 1) * P], HB[:, t * P:(t + 1) * P], CORE_("eye")).then_inc(*done("h_turn", t))
            pe.wait_ge(*upto("r_oh"))
            mm(bank(1)[:, 0:P], CB_("tri"), small(3), start=True, stop=True).then_inc(*done("prefix"))
            mm(bank(2)[:, 0:P], CB_("ones"), small(3), start=True, stop=True).then_inc(*done("totals"))
            for i in range(NCH):
                pe.wait_ge(*upto("slot_diag", 4 * i + 3))
                mm(half(0, i), CB_("ones"), ch(DG, i), start=True, stop=True).then_inc(*done("slot_spread", i))
            pe.wait_ge(*upto("h_turned", NCH - 1))
            for t in range(NT):
                pe.wait_ge(*upto("onehot", t))
                for j in range(2):
                    last = mm(bank(4 + j), HT[:, t * P:(t + 1) * P], OH1[:, t % 2, j * N:(j + 1) * N], start=(t == 0), stop=(t == NT - 1))
                last.then_inc(*done("dispatch", t))
            pe.wait_ge(*upto("buf0"))
            pe.wait_ge(*upto("buf1"))
            for e in range(E0):
                if e >= 2:
                    pe.wait_ge(*upto("e_relu", e - 2))
                for f in range(NF):
                    last = mm(bank(6 + e % 2)[:, f * P:(f + 1) * P], w1B[:, e, f * P:(f + 1) * P], BUF[:, e * CAP:(e + 1) * CAP], start=True, stop=True)
                last.then_inc(*done("e_up", e))
                pe.wait_ge(*upto("e_relu", e))
                pe.wait_ge(*upto("slots", NCH - 1))
                if e >= 2:
                    pe.wait_ge(*upto("e_out", e - 2))
                o = bank(2 + e % 2)[:, 0:P]
                a = cb_at["b2"][0] + e * P
                mm(o, CB_("ones")[0:1, :], cstB[0:1, a:a + P], start=True, stop=False)
                for f in range(NF):
                    last = mm(o, HS[:, e % 2, f, :], w2B[:, e, f, :], start=False, stop=(f == NF - 1))
                last.then_inc(*done("e_down", e))
            for i in range(NCH):
                pe.wait_ge(*upto("scale_diag", 4 * i + 3))
                mm(half(1, i), CB_("ones"), ch(DG2, i), start=True, stop=True).then_inc(*done("scale_spread", i))
            pe.wait_ge(*upto("e_out", E0 - 1))
            for i in range(NCH):
                for e in range(E0):
                    pe.wait_ge(*upto(f"place{e}", i))
                    last = mm(half(0, i), YB[:, e, :], PT[:, e, :], start=(e == 0), stop=(e == E0 - 1))
                last.then_inc(*done("combine", i))

            sweep("centreE", CORE_("centre"), X, 1, ["x_moe", "scales"])
            sweep("varE", CORE_("mean"), TE, 0, ["sqE", "moe_sum"])
            pe.wait_ge(wc_loaded, 48)
            prev = {0: "lnE", 1: "normE"}
            a = wc_at["in"][0]
            for k, step in enumerate(["xb0", "xb1", "z0", "z1"]):
                h = 1 - k % 2
                sweep(step, wC[:, a + k * P:a + (k + 1) * P], HC, h, [prev[h], "modE"])
                prev[h] = step + ("_copy" if k < 2 else "_silu")

            def x_proj(step, h, col0, rows, waits):
                for i in range(NCH):
                    for w in waits:
                        pe.wait_ge(*upto(w, i))
                    for c in range(DI):
                        pe.wait_ge(*upto(f"u{c}", i))
                        b = wc_at["xp"][0] + c * XPW + col0
                        last = mm(half(h, i, rows), wC[:, b:b + rows], ch(U[:, c, :], i), start=(c == 0), stop=(c == DI - 1))
                    last.then_inc(*done(step, i))

            x_proj("gate0", 1, 0, P, ["z0_silu"])
            x_proj("gate1", 0, P, P, ["z1_silu"])
            x_proj("bc", 1, DI * P, 96, ["gate0_tanh"])
            x_proj("dt_raw", 0, DI * P + 96, DTR, ["gate1_tanh"])
            a = wc_at["dtp"][0]
            sweep("dt0", wC[0:DTR, a:a + P], DRAW, 1, ["dt_raw_copy", "bc_r1"], parts=DTR)
            sweep("dt1", wC[0:DTR, a + P:a + 2 * P], DRAW, 0, ["dt_raw_copy"], parts=DTR)
            for c in range(DI):
                pe.wait_ge(*upto(f"sp_z_{c}", NCH - 1))
            pe.wait_ge(*upto("bc_lo", NCH - 1))
            for i in range(NCH):
                def y_sum(n):
                    for c in range(DI):
                        if n == 0 and i >= 2:
                            pe.wait_ge(*upto(f"skip_{c}", i - 2))
                        pe.wait_ge(*upto(f"sc{n}_{c}", i))
                        mm(bank(c + 2 * (i % 2)), CORE_("eye"), PRC[:, (2 * n + c) % 4, :], start=(n == 0), stop=(n == NS - 1)).then_inc(*done(f"y{n}_{c}", i))

                for n in range(NS):
                    for kind, b, last_use, row in (("b", 4, f"dbu{(n - 2) % NS}_1", n), ("c", 6, f"c_copy{(n - 2) % NS}", NS + n)):
                        if n >= 2 or i:
                            pe.wait_ge(*upto(last_use, i if n >= 2 else i - 1))
                        mm(bank(b + n % 2), sel[:, row, :], BC[:, i * N:(i + 1) * N], start=True, stop=True).then_inc(*done(f"{kind}{n}", i))
                    if n:
                        y_sum(n - 1)
                y_sum(NS - 1)
            pe.wait_ge(*upto(f"dbu{NS - 1}_1", NCH - 1))
            pe.wait_ge(*upto(f"c_copy{NS - 1}", NCH - 1))
            a = wc_at["out"][0]
            for i in range(NCH):
                for c in range(DI):
                    pe.wait_ge(*upto(f"gated_{c}", i))
                    last = mm(half(1, i), wC[:, a + c * P:a + (c + 1) * P], ch(U[:, c, :], i), start=(c == 0), stop=(c == DI - 1))
                last.then_inc(*done("m_out", i))

            pe.wait_ge(*upto("skip_1", NCH - 1))
            sweep("centreF", CORE_("centre"), X, 0, ["x_mamba"])
            sweep("varF", CORE_("mean"), TF, 1, ["sqF"])
            pe.wait_ge(*upto("modF", NCH - 1))
            for t in range(NT):
                last = mm(ps[:, t * E1:(t + 1) * E1], HD[:, t * P:(t + 1) * P], WC_("gate"), start=True, stop=True)
            last.then_inc(*done("g_router"))
            pe.wait_ge(*upto("g_lo"))
            for t in range(NT):
                o = ps[0:96, 2 * N:4 * N].bitcast(bf16)[:, t * P:(t + 1) * P]
                nc.tensor.transpose(o, CS[:, t, :], EYEB[:]).then_inc(*done("g_turn", t))
            pe.wait_ge(*upto("g_turned", 1))
            pe.wait_ge(*upto("lnF", NCH - 1))
            pe.wait_ge(wd_loaded, 16)
            seen = 0
            for i in range(NCH):
                def down(e):
                    pe.wait_ge(*upto(f"hw{e}" if e < E1 else f"hh{e}", i))
                    if e == 0 and i >= 2:
                        pe.wait_ge(*upto("x_out", i - 2))
                    src = (HW if e < E1 else HH)[:, (i * (E1 + 1) + e) % 2, :]
                    mm(bank(6 + i % 2), wD[:, 3 * e + 2, :], src, start=(e == 0), stop=(e == E1)).then_inc(*done(f"hd{e}", i))

                def before(e):
                    return (e - 2, i) if e >= 2 else (e - 2 + E1 + 1, i - 1)

                for e in range(E1 + 1):
                    k = (i * (E1 + 1) + e) % 2
                    be, bi = before(e)
                    if bi >= 0:
                        pe.wait_ge(*upto(f"silu{be}", bi))
                    mm(bank(0 + k), wD[:, 3 * e, :], ch(HD, i), start=True, stop=True).then_inc(*done(f"hg{e}", i))
                    if bi >= 0:
                        pe.wait_ge(*upto(f"hh{be}", bi))
                    mm(bank(2 + k), wD[:, 3 * e + 1, :], ch(HD, i), start=True, stop=True).then_inc(*done(f"hu{e}", i))
                    if e < E1:
                        if bi >= 0 and be < E1:
                            pe.wait_ge(*upto(f"hw{be}", bi))
                        elif bi >= 0:
                            pe.wait_ge(*upto(f"hh{be}", bi))
                        mm(bank(4 + k), sel[:, e, :], BC[:, i * N:(i + 1) * N], start=True, stop=True).then_inc(*done(f"w{e}", i))
                    if e:
                        down(e - 1)
                down(E1)

        @block.scalar
        def _(act):
            A = nc.scalar.activation

            def square(step, src, dst, waits):
                for i in range(NCH):
                    for w in waits:
                        act.wait_ge(*upto(w, i))
                    A(ch(dst, i), src(i), ACT.Square).then_inc(*done(step, i))

            def rsqrt(k, h, buf, eps, waits):
                for i in range(NCH):
                    for w in waits:
                        act.wait_ge(*upto(w, i))
                    A(ch(buf, i), half(h, i), ACT.Ln, bias=eps).then_inc(*done(f"ln{k}", i))
                    act.wait_ge(*upto(f"ln{k}", i))
                    A(ch(buf, i), ch(buf, i), ACT.Exp, scale=-0.5).then_inc(*done(f"rs{k}", i))

            def evict(step, h, dst, func, waits, rows=P, scale=1.0):
                for i in range(NCH):
                    for w in waits:
                        act.wait_ge(*upto(w, i))
                    A(ch(dst, i)[0:rows], half(h, i, rows), func, scale=scale).then_inc(*done(step, i))

            nc.scalar.preload_act_table_set("natural_log_exp_and_others")
            act.wait_ge(vec_loaded, 32)
            A(mtmp[:, 0:2], vec[:, VEC.index("c0"):VEC.index("c1") + 1], ACT.Exp, scale=-1.0).then_inc(*done("c_exp"))
            square("sqA", lambda i: half(0, i), T1, ["centreA"])
            rsqrt("A", 1, T1, col("eps5"), ["varA"])
            square("sqB", lambda i: ch(HLN, i), T2, ["modA"])
            rsqrt("B", 0, T2, col("eps6"), ["msB"])
            act.wait_ge(*upto("normB", NCH - 1))
            evict("r_copy", 1, R, ACT.Copy, ["r"])
            evict("k_copy", 0, K, ACT.Copy, ["k"])
            evict("v_copy", 1, V, ACT.Copy, ["v"])
            nc.scalar.preload_act_table_set("silu_and_others")
            evict("lora_tanh", 0, TA, ACT.Tanh, ["lora_a"], rows=LORA)
            evict("g_silu", 1, G, ACT.Silu, ["g"])
            nc.scalar.preload_act_table_set("natural_log_exp_and_others")
            for i in range(NCH):
                act.wait_ge(*upto("lora_b", i))
                A(ch(DEC, i), half(0, i), ACT.Exp, bias=col("w0")).then_inc(*done("w_exp", i))
                act.wait_ge(*upto("w_exp", i))
                A(ch(DEC, i), ch(DEC, i), ACT.Exp, scale=-1.0).then_inc(*done("decay", i))
            for i in range(NCH):
                if i:
                    act.wait_ge(*upto("spread7", i - 1))
                else:
                    act.wait_ge(*upto("v_copy", NCH - 1))
                A(VC, ch(V, i), ACT.Copy).then_inc(*done("v_chunk", i))
            square("gn_sq", lambda i: half(1, i), T1, ["gn_centred"])
            for i in range(NCH):
                act.wait_ge(*upto("gn_var", i))
                A(ch(T1, i), half(0, i), ACT.Ln, bias=col("eps5")).then_inc(*done("gn_ln", i))
                act.wait_ge(*upto("gn_ln", i))
                A(ch(T1, i), ch(T1, i), ACT.Exp, scale=-0.5).then_inc(*done("gn_rs", i))
                act.wait_ge(*upto("gn_rs", i))
                A(ch(T3, i), ch(T1, i), ACT.Square).then_inc(*done("gn_rs2", i))
            square("sqC", lambda i: ch(HLN, i), T2, ["x1"])
            rsqrt("C", 0, T2, col("eps6"), ["msC"])
            nc.scalar.preload_act_table_set("gelu_and_others")
            for i in range(NCH):
                for f in range(NF):
                    act.wait_ge(*upto(f"up{f}", i))
                    if i:
                        act.wait_ge(*upto(f"down{f}", i - 1))
                    A(GEL[:, f, :], bank(4 + f), ACT.Gelu).then_inc(*done(f"gelu{f}", i))
            nc.scalar.preload_act_table_set("natural_log_exp_and_others")

            square("sqD", lambda i: half(1, i), TB, ["centreD"])
            rsqrt("D", 0, TB, col("eps5"), ["varD"])
            act.wait_ge(*upto("r_shift"))
            A(small(1), small(0), ACT.Exp).then_inc(*done("r_exp"))
            for q in range(NCH):
                act.wait_ge(*upto("h_turn", 4 * q + 3))
                A(ch(HT, q), half(1, q), ACT.Copy).then_inc(*done("h_turned", q))
            evict("slots", 0, SLB, ACT.Copy, ["slot_spread"])
            act.wait_ge(*upto("r_scale"))
            for t in range(NT):
                A(DG2[:, t * P:(t + 1) * P], CORE_("eye"), ACT.Copy, scale=tiny(4)[:, t:t + 1]).then_inc(*done("scale_diag", t))
            act.wait_ge(*upto("dispatch", NT - 1))
            A(BUF[:, 0:N], bank(4), ACT.Copy).then_inc(*done("buf0"))
            evict("scales", 1, SCB, ACT.Copy, ["scale_spread"])

            square("sqE", lambda i: half(1, i), TE, ["centreE"])
            rsqrt("E", 0, TE, col("eps5"), ["varE"])
            nc.scalar.preload_act_table_set("silu_and_others")
            for c in range(DI):
                for i in range(NCH):
                    act.wait_ge(*upto(f"xb{c}", i))
                    A(XBP[:, c, i * N + 3:(i + 1) * N + 3], half(1 - c, i), ACT.Copy).then_inc(*done(f"xb{c}_copy", i))
            act.wait_ge(*upto("x_moe", NCH - 1))
            for c in range(DI):
                evict(f"z{c}_silu", 1 - c, Z[:, c, :], ACT.Silu, [f"z{c}"])
            for c in range(DI):
                for i in range(NCH):
                    act.wait_ge(*upto(f"conv{c}_3", i))
                    A(ch(U[:, c, :], i), ch(CV[:, c, :], i), ACT.Silu).then_inc(*done(f"u{c}", i))
            for c in range(DI):
                evict(f"gate{c}_tanh", 1 - c, DTG[:, c, :], ACT.Tanh, [f"gate{c}"], scale=0.5)
            evict("bc_hi", 1, BC, ACT.Copy, ["bc"], rows=96)
            for i in range(NCH):
                act.wait_ge(*upto("bc_r1", i))
                A(ch(BC, i)[32:64], ch(R1, i)[32:64], ACT.Copy).then_inc(*done("bc_mid", i))
            for i in range(NCH):
                A(ch(BC, i)[64:96], ch(R1, i)[64:96], ACT.Copy).then_inc(*done("bc_mid2", i))
            evict("dt_raw_copy", 0, DRAW, ACT.Copy, ["dt_raw"], rows=DTR)
            nc.scalar.preload_act_table_set("natural_log_exp_and_others")
            a0 = VEC.index("A0_0")
            A(ABASE[:], vec[:, a0:a0 + DI * NS], ACT.Exp).then_inc(*done("a_exp"))
            for c in range(DI):
                for i in range(NCH):
                    act.wait_ge(*upto(f"sp_abs_{c}", i))
                    if c:
                        act.wait_ge(*upto("sp_hi_0", i))
                        act.wait_ge(*upto("sp_min_0", i))
                    A(ch(SPE, i), ch(SPA, i), ACT.Exp, scale=-1.0).then_inc(*done(f"sp_e_{c}", i))
                    act.wait_ge(*upto(f"sp_e_{c}", i))
                    if c:
                        act.wait_ge(*upto("dt_0", i))
                    A(ch(SPL, i), ch(SPE, i), ACT.Ln, bias=1.0).then_inc(*done(f"sp_ln_{c}", i))
                    A(ch(SPE2, i), ch(SPE, i), ACT.Square).then_inc(*done(f"sp_e2_{c}", i))
                    act.wait_ge(*upto(f"sp_e2_{c}", i))
                    A(ch(SPE2, i), ch(SPE2, i), ACT.Square).then_inc(*done(f"sp_e4_{c}", i))
            act.wait_ge(*upto("a_neg"))
            for i in range(NCH):
                for c in range(DI):
                    act.wait_ge(*upto(f"dtg_{c}", i))
                for n in range(NS):
                    act.wait_ge(*upto(f"c{n}", i))
                    if n >= 2 or i:
                        act.wait_ge(*upto(f"sc{(n - 2) % NS}_1", i if n >= 2 else i - 1))
                    A(CBR[:, n % 2, :], bank(6 + n % 2), ACT.Copy).then_inc(*done(f"c_copy{n}", i))
                    for c in range(DI):
                        k = 2 * n + c
                        if k >= 3 or i:
                            m = (k - 3) % (2 * NS)
                            act.wait_ge(*upto(f"st{m // 2}_{m % 2}", i if k >= 3 else i - 1))
                        A(DECR[:, (i * 2 * NS + k) % 3, :], ch(DTG[:, c, :], i), ACT.Exp,
                          scale=ABASE[:, c * NS + n:c * NS + n + 1]).then_inc(*done(f"dec{n}_{c}", i))

            square("sqF", lambda i: half(0, i), TF, ["centreF"])
            rsqrt("F", 1, TF, col("eps5"), ["varF"])
            act.wait_ge(*upto("g_router"))
            A(gsmall(0), ps[:, 0:NT * E1], ACT.Exp, scale=-1.0).then_inc(*done("g_exp"))
            nc.scalar.preload_act_table_set("silu_and_others")
            for j in range(2):
                act.wait_ge(*upto("g_turn", 8 * j + 7))
                A(BC[:, j * 2 * N:(j + 1) * 2 * N], ps[0:96, 2 * N:4 * N].bitcast(bf16)[:, j * 2 * N:(j + 1) * 2 * N], ACT.Copy).then_inc(*done("g_turned", j))
            for i in range(NCH):
                for e in range(E1 + 1):
                    k = (i * (E1 + 1) + e) % 2
                    act.wait_ge(*upto(f"hg{e}", i))
                    be, bi = (e - 2, i) if e >= 2 else (e - 2 + E1 + 1, i - 1)
                    if bi >= 0:
                        act.wait_ge(*upto(f"hh{be}", bi))
                    A(SG[:, k, :], bank(k), ACT.Silu).then_inc(*done(f"silu{e}", i))

        @block.vector
        def _(dve):
            tt, ts, stt = nc.vector.tensor_tensor, nc.vector.tensor_scalar, nc.vector.scalar_tensor_tensor
            red = nc.vector.tensor_reduce

            def skip(i):
                for c in range(DI):
                    dve.wait_ge(*upto(f"y{NS - 1}_{c}", i))
                    stt(ch(U[:, c, :], i), ch(U[:, c, :], i), col(f"D{c}"), bank(c + 2 * (i % 2)), ALU.mult, ALU.add).then_inc(*done(f"skip_{c}", i))

            dve.wait_ge(*upto("c_exp"))
            ts(mtmp[:, 2:4], mtmp[:, 0:2], 1.0, None, ALU.add).then_inc(*done("c_one"))
            dve.wait_ge(*upto("c_one"))
            nc.vector.reciprocal(mtmp[:, 0:2], mtmp[:, 2:4]).then_inc(*done("c_recip"))
            dve.wait_ge(*upto("c_recip"))
            tt(mtmp[:, 4:6], mtmp[:, 0:2], vec[:, VEC.index("c0"):VEC.index("c1") + 1], ALU.mult).then_inc(*done("c_silu"))
            dve.wait_ge(*upto("mod"))
            nc.vector.tensor_copy(mod[:], ps[:, 7 * N:7 * N + 12]).then_inc(*done("mod_copy"))
            dve.wait_ge(*upto("mod_copy"))
            m3 = mod[:].rearrange("p (k s) -> p k s", s=3)
            g3 = mtmp[:, 8:12]
            a3 = mtmp[:, 12:16]
            s3 = mtmp[:, 16:20]
            ts(m3[:, :, 1], m3[:, :, 1], 1.0, None, ALU.add).then_inc(*done("mod_ca"))
            ts(g3, m3[:, :, 2], 0.0, None, ALU.is_ge).then_inc(*done("mod_sign"))
            dve.wait_ge(*upto("mod_sign"))
            ts(s3, g3, 2.0, -1.0, ALU.mult, ALU.add).then_inc(*done("mod_sign2"))
            stt(a3, m3[:, :, 2], -1.0, m3[:, :, 2], ALU.mult, ALU.max).then_inc(*done("mod_abs"))
            dve.wait_ge(*upto("mod_abs"))
            ts(a3, a3, GATE_FLOOR, None, ALU.max).then_inc(*done("mod_floor"))
            dve.wait_ge(*upto("mod_floor"))
            tt(m3[:, :, 2], s3, a3, ALU.mult).then_inc(*done("mod_gate"))
            dve.wait_ge(*upto("mod_gate"))

            def norm(k, h, dst, buf, layer, scale, shift, waits=()):
                for i in range(NCH):
                    dve.wait_ge(*upto(f"rs{k}", i))
                    for w in waits:
                        dve.wait_ge(*upto(w, i))
                    tt(ch(dst, i), half(h, i), ch(buf, i), ALU.mult).then_inc(*done(f"norm{k}", i))
                    dve.wait_ge(*upto(f"norm{k}", i))
                    ts(ch(dst, i), ch(dst, i), modcol(layer, scale), modcol(layer, shift), ALU.mult, ALU.add).then_inc(*done(f"mod{k}", i))

            norm("A", 0, HLN, T1, 0, CA, SA)
            dve.wait_ge(*upto("h1_zero"))
            for i in range(NCH):
                dve.wait_ge(*upto("rsB", i))
                stt(ch(H1, i, 1), ch(HLN, i), col("ln1_w"), ch(T2, i), ALU.mult, ALU.mult).then_inc(*done("normB", i))
            for i in range(NCH):
                dve.wait_ge(*upto("normB", i))
                tt(ch(XX, i), ch(H1, i), ch(H1, i, 1), ALU.subtract).then_inc(*done("xx", i))

            def mix(step, mu, dst, waits):
                for i in range(NCH):
                    dve.wait_ge(*upto("xx", i))
                    for w in waits:
                        dve.wait_ge(*upto(w, i))
                    stt(ch(dst, i), ch(XX, i), col(mu), ch(H1, i, 1), ALU.mult, ALU.add).then_inc(*done(step, i))

            mix("mix_r", "mu_r", M0, [])
            dve.wait_ge(*upto("mod"))
            mix("mix_k", "mu_k", M1, [])
            mix("mix_v", "mu_v", M2, [])
            mix("mix_w", "mu_w", M0, ["r"])
            mix("mix_g", "mu_g", M1, ["k"])
            for i in range(NCH):
                dve.wait_ge(*upto("k_copy", i))
                dve.wait_ge(*upto("mix_g", i))
                stt(ch(XX, i), ch(R, i), col("u"), ch(K, i), ALU.mult, ALU.mult).then_inc(*done("ruk", i))
            for i in range(NCH):
                dve.wait_ge(*upto("head_ruk", i))
                tt(ch(BONUS, i), half(1, i), ch(V, i), ALU.mult).then_inc(*done("bonus", i))
            nc.vector.memset(S[:, :, 0:1], 0.0).then_inc(*done("s_zero"))
            dve.wait_ge(*upto("s_zero"))

            for i in range(NCH):
                for w in range(2):
                    for k, v in enumerate(WAVES[w]):
                        dve.wait_ge(*upto(f"spread{v}", i))
                        if w or i:
                            dve.wait_ge(*upto(f"scan{WAVES[1 - w][k]}", i if w else i - 1))
                        tt(KV[:, k, :], bank(4 + k), ch(K, i), ALU.mult).then_inc(*done(f"kv{v}", i))
                    if i and w == 0:
                        dve.wait_ge(*upto("reduce7", i - 1))
                        tt(ch(O, i - 1), bank((i - 1) % 2), ch(BONUS, i - 1), ALU.add).then_inc(*done("o", i - 1))
                    dve.wait_ge(*upto("decay", i))
                    for k, v in enumerate(WAVES[w]):
                        dve.wait_ge(*upto(f"kv{v}", i))
                        nc.vector.tensor_tensor_scan(S[:, v, i * N + 1:(i + 1) * N + 1], ch(DEC, i), KV[:, k, :],
                                                     S[:, v, i * N:i * N + 1], ALU.mult, ALU.add).then_inc(*done(f"scan{v}", i))
            dve.wait_ge(*upto("reduce7", NCH - 1))
            tt(ch(O, NCH - 1), bank((NCH - 1) % 2), ch(BONUS, NCH - 1), ALU.add).then_inc(*done("o", NCH - 1))
            for i in range(NCH):
                dve.wait_ge(*upto("gn_rs2", i))
                stt(ch(T3, i), half(0, i), EPS_GN, ch(T3, i), ALU.add, ALU.mult).then_inc(*done("gn_err", i))
                dve.wait_ge(*upto("gn_err", i))
                ts(ch(T3, i), ch(T3, i), -0.5, 1.5, ALU.mult, ALU.add).then_inc(*done("gn_half", i))
                dve.wait_ge(*upto("gn_half", i))
                tt(ch(T1, i), ch(T1, i), ch(T3, i), ALU.mult).then_inc(*done("gn_rsqrt", i))
                dve.wait_ge(*upto("gn_rsqrt", i))
                tt(ch(O, i), half(1, i), ch(T1, i), ALU.mult).then_inc(*done("gn_norm", i))
                dve.wait_ge(*upto("gn_norm", i))
                ts(ch(O, i), ch(O, i), col("gn_w"), col("gn_b"), ALU.mult, ALU.add).then_inc(*done("gn_affine", i))
                dve.wait_ge(*upto("gn_affine", i))
                tt(ch(O, i), ch(O, i), ch(G, i), ALU.mult).then_inc(*done("gn_gate", i))
            for i in range(NCH):
                dve.wait_ge(*upto("wo", i))
                tt(ch(HLN, i), half(1, i), ch(HLN, i), ALU.add).then_inc(*done("x1", i))
            for i in range(NCH):
                dve.wait_ge(*upto("rsC", i))
                stt(ch(M0, i), ch(HLN, i), col("ln2_w"), ch(T2, i), ALU.mult, ALU.mult).then_inc(*done("normC", i))
            for i in range(NCH):
                dve.wait_ge(*upto("down3", i))
                tt(ch(HLN, i), half(0, i), ch(HLN, i), ALU.add).then_inc(*done("ffn_sum", i))
                dve.wait_ge(*upto("ffn_sum", i))
                stt(ch(X, i), ch(HLN, i), modcol(0, GA), ch(X, i), ALU.mult, ALU.add).then_inc(*done("x_attn", i))

            norm("D", 1, HB, TB, 0, CB, SB_)
            steps = iter(R_STEPS)
            state = {"last": None}

            def step(op, *args, **kw):
                name = next(state["names"])
                if state["last"]:
                    dve.wait_ge(*upto(state["last"]))
                for w in kw.pop("waits", []):
                    dve.wait_ge(*upto(*w))
                op(*args, **kw).then_inc(*done(name))
                state["last"] = name

            L_, E_, PR_, OH_, RK_, CU_, TO_ = (small3(k) for k in (0, 1, 2, 3, 4, 5, 6))
            flat = small
            MX, SM, RC, PM, SC, BEST, POS, KEEP, BASE, SLOT = (tiny(k) for k in (0, 1, 2, 3, 4, 5, 6, 7, 8, 9))
            state["names"] = steps
            dve.wait_ge(wb_loaded, 48)
            step(tt, flat(0), ps[:, 0:NT * E0], CB_("b_switch"), ALU.add, waits=[("router",)])
            step(red, MX, L_, AX, ALU.max)
            step(tt, L_, L_, bcast(MX, E0), ALU.subtract)
            step(red, SM, E_, AX, ALU.add, waits=[("r_exp",)])
            step(nc.vector.reciprocal, RC, SM)
            step(tt, PR_, E_, bcast(RC, E0), ALU.mult)
            step(red, PM, PR_, AX, ALU.max)
            step(tt, RK_, PR_, bcast(PM, E0), ALU.is_equal)
            step(tt, flat(4), flat(4), CB_("rank"), ALU.mult)
            step(red, BEST, RK_, AX, ALU.max)
            step(tt, OH_, CB_("rank").rearrange("p (t e) -> p t e", e=E0), bcast(BEST, E0), ALU.is_equal)
            step(nc.vector.reciprocal, RC, PM)
            step(tt, SC, PM, RC, ALU.mult)
            step(nc.vector.tensor_copy, TO_.rearrange("p t e -> p (t e)").rearrange("p (e t) -> p e t", e=E0),
                 bank(2)[:, 0:P].rearrange("p (t e) -> p e t", e=E0), waits=[("totals",)])
            step(nc.vector.tensor_tensor_scan, flat(5), CB_("seg"), flat(6), 0.0, ALU.mult, ALU.add)
            step(tt, flat(5), flat(5), flat(6), ALU.subtract)
            step(tt, RK_, bank(1)[:, 0:P].rearrange("p (t e) -> p t e", e=E0), flat(5).rearrange("p (e t) -> p t e", e=E0), ALU.add)
            step(tt, RK_, RK_, OH_, ALU.mult)
            step(red, POS, RK_, AX, ALU.add)
            step(ts, KEEP, POS, float(CAP), None, ALU.is_le)
            step(ts, BASE, BEST, -float(CAP), float(E0 * CAP), ALU.mult, ALU.add)
            step(tt, SLOT, BASE, POS, ALU.add)
            step(tt, SLOT, SLOT, KEEP, ALU.mult)
            dve.wait_ge(*upto("r_kept"))
            for t in range(NT):
                ts(DG[:, t * P:(t + 1) * P], CORE_("eye"), SLOT[:, t:t + 1], None, ALU.mult).then_inc(*done("slot_diag", t))
            for t in range(NT):
                if t >= 2:
                    dve.wait_ge(*upto("dispatch", t - 2))
                ts(OH1[:, t % 2, :], CB_("iota"), SLOT[:, t:t + 1], None, ALU.is_equal).then_inc(*done("onehot", t))
            dve.wait_ge(*upto("dispatch", NT - 1))
            nc.vector.tensor_copy(BUF[:, N:2 * N], bank(5)).then_inc(*done("buf1"))
            b1 = CB_("b1").rearrange("p (e f) -> p e f", e=E0)
            for e in range(E0):
                dve.wait_ge(*upto("e_up", e))
                if e >= 2:
                    dve.wait_ge(*upto("e_down", e - 2))
                for f in range(NF):
                    last = ts(HS[:, e % 2, f, :], bank(6 + e % 2)[:, f * P:(f + 1) * P], b1[:, e, f:f + 1], 0.0, ALU.add, ALU.max)
                last.then_inc(*done("e_relu", e))
                dve.wait_ge(*upto("e_down", e))
                nc.vector.tensor_copy(YB[:, e, :], bank(2 + e % 2)[:, 0:P]).then_inc(*done("e_out", e))
            for i in range(NCH):
                dve.wait_ge(*upto("slots", i))
                for e in range(E0):
                    if i:
                        dve.wait_ge(*upto("combine", i - 1))
                    ts(PT[:, e, :], ch(SLB, i), CB_("iota_p")[:, e:e + 1], None, ALU.is_equal).then_inc(*done(f"place{e}", i))
                dve.wait_ge(*upto(f"place{E0 - 1}", i))
                stt(ch(HB, i), ch(SLB, i), 0.5, ch(HB, i), ALU.is_lt, ALU.mult).then_inc(*done("kept_x", i))
                dve.wait_ge(*upto("kept_x", i))
                dve.wait_ge(*upto("combine", i))
                tt(ch(HB, i), half(0, i), ch(HB, i), ALU.add).then_inc(*done("moe_sum", i))
                dve.wait_ge(*upto("moe_sum", i))
                dve.wait_ge(*upto("scales", i))
                stt(ch(HB, i), ch(HB, i), modcol(0, GB), ch(SCB, i), ALU.mult, ALU.mult).then_inc(*done("moe_scaled", i))
                dve.wait_ge(*upto("moe_scaled", i))
                tt(ch(X, i), ch(HB, i), ch(X, i), ALU.add).then_inc(*done("x_moe", i))

            norm("E", 1, HC, TE, 1, CA, SA)
            nc.vector.memset(XBP[:, :, 0:3], 0.0).then_inc(*done("xb_zero"))
            dve.wait_ge(*upto("xb_zero"))
            for c in range(DI):
                for i in range(NCH):
                    dve.wait_ge(*upto(f"xb{c}_copy", i))
                    for j in range(KC):
                        src = XBP[:, c, i * N + j:(i + 1) * N + j]
                        if j == 0:
                            ts(ch(CV[:, c, :], i), src, col(f"cw{c}_0"), col(f"cb{c}"), ALU.mult, ALU.add).then_inc(*done(f"conv{c}_0", i))
                        else:
                            dve.wait_ge(*upto(f"conv{c}_{j - 1}", i))
                            stt(ch(CV[:, c, :], i), src, col(f"cw{c}_{j}"), ch(CV[:, c, :], i), ALU.mult, ALU.add).then_inc(*done(f"conv{c}_{j}", i))
            for i in range(NCH):
                dve.wait_ge(*upto("bc_hi", i))
                tt(ch(R1, i)[0:96], half(1, i, 96), ch(BC, i), ALU.subtract).then_inc(*done("bc_r1", i))
            for i in range(NCH):
                dve.wait_ge(*upto("bc_mid2", i))
                tt(ch(BC, i)[64:96], ch(R1, i)[64:96], ch(BC, i)[64:96], ALU.subtract).then_inc(*done("bc_lo", i))
            dve.wait_ge(*upto("a_exp"))
            ts(ABASE[:], ABASE[:], -1.0, None, ALU.mult).then_inc(*done("a_neg"))
            nc.vector.memset(CARRY[:], 0.0).then_inc(*done("st_zero"))
            for c in range(DI):
                for i in range(NCH):
                    dve.wait_ge(*upto(f"dt{c}", i))
                    if c:
                        dve.wait_ge(*upto("dt_0", i))
                    ts(ch(SPZ, i), half(1 - c, i), col(f"dt_b{c}"), None, ALU.add).then_inc(*done(f"sp_z_{c}", i))
                    dve.wait_ge(*upto(f"sp_z_{c}", i))
                    stt(ch(SPA, i), ch(SPZ, i), -1.0, ch(SPZ, i), ALU.mult, ALU.max).then_inc(*done(f"sp_abs_{c}", i))
                for i in range(NCH):
                    dve.wait_ge(*upto(f"sp_e_{c}", i))
                    ts(ch(SPP, i), ch(SPE, i), -0.25, 1.0 / 3, ALU.mult, ALU.add).then_inc(*done(f"sp_p1_{c}", i))
                for i in range(NCH):
                    dve.wait_ge(*upto(f"sp_p2_{c}", i))
                    stt(ch(SPP, i), ch(SPP, i), -0.5, ch(SPE, i), ALU.add, ALU.mult).then_inc(*done(f"sp_p3_{c}", i))
                    dve.wait_ge(*upto(f"sp_p3_{c}", i))
                    stt(ch(SPP, i), ch(SPP, i), 1.0, ch(SPE, i), ALU.add, ALU.mult).then_inc(*done(f"sp_lo_{c}", i))
                    dve.wait_ge(*upto(f"sp_e4_{c}", i))
                    stt(ch(SPH, i), ch(SPE2, i), 0.2, ch(SPE, i), ALU.mult, ALU.mult).then_inc(*done(f"sp_h5_{c}", i))
                for i in range(NCH):
                    dve.wait_ge(*upto(f"sp_lo_{c}", i))
                    tt(ch(SPL, i), ch(SPL, i), ch(SPP, i), ALU.max).then_inc(*done(f"sp_max_{c}", i))
                    dve.wait_ge(*upto(f"sp_max_{c}", i))
                    dve.wait_ge(*upto(f"sp_hi_{c}", i))
                    tt(ch(SPL, i), ch(SPL, i), ch(SPH, i), ALU.min).then_inc(*done(f"sp_min_{c}", i))
                    dve.wait_ge(*upto(f"sp_min_{c}", i))
                    stt(ch(DT, i), ch(SPZ, i), 0.0, ch(SPL, i), ALU.max, ALU.add).then_inc(*done(f"dt_{c}", i))
                    ts(ch(DTG[:, c, :], i), ch(DTG[:, c, :], i), 0.5, 1.0, ALU.mult, ALU.add).then_inc(*done(f"gate_half_{c}", i))
            dve.wait_ge(*upto("du_1", NCH - 1))
            for i in range(NCH):
                for n in range(NS):
                    for c in range(DI):
                        k = 2 * n + c
                        dve.wait_ge(*upto(f"b{n}", i))
                        if n or i:
                            dve.wait_ge(*upto(f"st{(n - 1) % NS}_{c}", i if n else i - 1))
                        tt(DBU[:, c, :], bank(4 + n % 2), ch(DU[:, c, :], i), ALU.mult).then_inc(*done(f"dbu{n}_{c}", i))
                    for c in range(DI):
                        k = 2 * n + c
                        dve.wait_ge(*upto(f"dec{n}_{c}", i))
                        dve.wait_ge(*upto(f"dbu{n}_{c}", i))
                        if i:
                            dve.wait_ge(*upto(f"sc{n}_{c}", i - 1))
                        first = ST[:, k, N - 1:N] if i else CARRY[:]
                        nc.vector.tensor_tensor_scan(ST[:, k, :], DECR[:, (i * 2 * NS + k) % 3, :], DBU[:, c, :], first,
                                                     ALU.mult, ALU.add).then_inc(*done(f"st{n}_{c}", i))
                    if i and n == 2:
                        skip(i - 1)
            skip(NCH - 1)
            for i in range(NCH):
                dve.wait_ge(*upto("m_out", i))
                stt(ch(X, i), half(1, i), modcol(1, GA), ch(X, i), ALU.mult, ALU.add).then_inc(*done("x_mamba", i))

            norm("F", 0, HD, TF, 1, CB, SB_)
            state["names"], state["last"] = iter(G_STEPS), None
            g, g3 = gsmall, gsmall3
            M8 = area(2 * T + 6 * N + 12 * 256, NT * 8).rearrange("p (t k) -> p t k", k=8)
            THR = M8[:, :, 7]
            NG, LEFT, TOT, INV = (gtiny(k) for k in range(4))
            step(ts, g(1), g(0), 1.0, None, ALU.add, waits=[("g_exp",)])
            step(nc.vector.reciprocal, g(2), g(1))
            step(tt, g(3), g(2), WC_("g_bias"), ALU.add)
            for t in range(NT):
                step(nc.vector.max, M8[:, t, :], g3(3)[:, t, :])
            step(tt, g3(4), g3(3), bcast(THR, E1), ALU.is_gt)
            step(tt, g3(5), g3(3), bcast(THR, E1), ALU.is_equal)
            step(red, NG, g3(4), AX, ALU.add)
            step(ts, LEFT, NG, -1.0, float(TOPK), ALU.mult, ALU.add)
            step(nc.vector.tensor_tensor_scan, g(6), WC_("g_seg"), g(5), 0.0, ALU.mult, ALU.add)
            step(tt, g3(6), g3(6), bcast(LEFT, E1), ALU.is_le)
            step(tt, g(6), g(6), g(5), ALU.mult)
            step(tt, g(6), g(6), g(4), ALU.add)
            step(tt, g(6), g(6), g(2), ALU.mult)
            step(red, TOT, g3(6), AX, ALU.add)
            step(nc.vector.reciprocal, INV, TOT)
            step(stt, g3(7), g3(6), ROUTE_SCALE, bcast(INV, E1), ALU.mult, ALU.mult)
            step(nc.vector.memset, CS, 0.0)
            step(nc.vector.tensor_copy, CS[:, :, 0:E1], g3(7))
            step(tt, g3(8), g3(7), CS[:, :, 0:E1], ALU.subtract)
            step(nc.vector.tensor_copy, CS[:, :, 32:32 + E1], g3(8))
            step(tt, CS[:, :, 64:64 + E1], g3(8), CS[:, :, 32:32 + E1], ALU.subtract)
            for i in range(NCH):
                for e in range(E1 + 1):
                    k = (i * (E1 + 1) + e) % 2
                    be, bi = (e - 2, i) if e >= 2 else (e - 2 + E1 + 1, i - 1)
                    dve.wait_ge(*upto(f"silu{e}", i))
                    dve.wait_ge(*upto(f"hu{e}", i))
                    if bi >= 0:
                        dve.wait_ge(*upto(f"hd{be}", bi))
                    tt(HH[:, k, :], bank(2 + k), SG[:, k, :], ALU.mult).then_inc(*done(f"hh{e}", i))
                    if e < E1:
                        dve.wait_ge(*upto(f"hh{e}", i))
                        dve.wait_ge(*upto(f"w{e}", i))
                        tt(HW[:, k, :], bank(4 + k), HH[:, k, :], ALU.mult).then_inc(*done(f"hw{e}", i))
                dve.wait_ge(*upto(f"hd{E1}", i))
                stt(ch(X, i), bank(6 + i % 2), modcol(1, GB), ch(X, i), ALU.mult, ALU.add).then_inc(*done("x_out", i))

        @block.gpsimd
        def _(pool):
            mul = lambda o, a, b: nc.gpsimd.tensor_tensor(o, a, b, ALU.mult)
            nc.gpsimd.memset(H1[:, 0:1], 0.0).then_inc(*done("h1_zero"))
            for i in range(NCH):
                for w in range(2):
                    for k, v in enumerate(WAVES[w]):
                        pool.wait_ge(*upto(f"scan{v}", i))
                        if w or i:
                            pool.wait_ge(*upto(f"reduce{WAVES[1 - w][k]}", i if w else i - 1))
                        mul(PR[:, k, :], S[:, v, i * N:(i + 1) * N], ch(R, i)).then_inc(*done(f"prod{v}", i))
            for c in range(DI):
                for i in range(NCH):
                    pool.wait_ge(*upto(f"sp_p1_{c}", i))
                    mul(ch(SPP, i), ch(SPP, i), ch(SPE, i)).then_inc(*done(f"sp_p2_{c}", i))
                for i in range(NCH):
                    pool.wait_ge(*upto(f"sp_h5_{c}", i))
                    nc.gpsimd.tensor_tensor(ch(SPH, i), ch(SPH, i), ch(SPP, i), ALU.add).then_inc(*done(f"sp_hi_{c}", i))
                for i in range(NCH):
                    pool.wait_ge(*upto(f"gate_half_{c}", i))
                    mul(ch(DTG[:, c, :], i), ch(DTG[:, c, :], i), ch(DT, i)).then_inc(*done(f"dtg_{c}", i))
                    mul(ch(DU[:, c, :], i), ch(U[:, c, :], i), ch(DT, i)).then_inc(*done(f"du_{c}", i))

            def gated(i):
                for c in range(DI):
                    pool.wait_ge(*upto(f"skip_{c}", i))
                    mul(ch(U[:, c, :], i), ch(U[:, c, :], i), ch(Z[:, c, :], i)).then_inc(*done(f"gated_{c}", i))

            for i in range(NCH):
                for n in range(NS):
                    for c in range(DI):
                        k = 2 * n + c
                        pool.wait_ge(*upto(f"st{n}_{c}", i))
                        pool.wait_ge(*upto(f"c_copy{n}", i))
                        if k >= 4 or i:
                            m = (k - 4) % (2 * NS)
                            pool.wait_ge(*upto(f"y{m // 2}_{m % 2}", i if k >= 4 else i - 1))
                        mul(PRC[:, k % 4, :], ST[:, k, :], CBR[:, n % 2, :]).then_inc(*done(f"sc{n}_{c}", i))
                    if i and n == 2:
                        gated(i - 1)
            gated(NCH - 1)

        assert not any(order.values()), {k: v[:3] for k, v in order.items()}


def kernel(**inputs):
    import numpy as np
    import concourse.bacc as bacc
    from concourse.bass_utils import run_bass_kernel_spmd

    a = {k: np.asarray(v) for k, v in inputs.items()}

    def by_value(w, axis):
        s = w.shape
        return np.moveaxis(w.reshape(s[:axis] + (H, DK) + s[axis + 1:]), axis, axis + 1).reshape(s)

    L0 = {k[8:]: v for k, v in a.items() if k.startswith("L0_attn_")}
    vecs = dict(L0, u=L0["u"].reshape(-1), gn_w=by_value(L0["gn_w"].reshape(-1), 0), gn_b=by_value(L0["gn_b"].reshape(-1), 0),
                c0=a["L0_c"][0], c1=a["L1_c"][0], eps5=np.full(P, 1e-5, np.float32), eps6=np.full(P, 1e-6, np.float32))
    x = np.ascontiguousarray(L0["x"][0].T)
    w = dict(L0, Wv=by_value(L0["Wv"], 1), Wg=by_value(L0["Wg"], 1), Wo=by_value(L0["Wo"], 0),
             wB=np.concatenate([L0["wB"], L0["wB"]]), w1=L0["ffn_w1"],
             w2=L0["ffn_w2"].reshape(NF, P, P).transpose(1, 0, 2).reshape(P, F))
    wA = np.concatenate([w[n] for n in WA], 1)
    wmod = np.stack([a["L0_wmod"], a["L1_wmod"]], 1)
    F0 = {k[7:]: v for k, v in a.items() if k.startswith("L0_ffn_")}
    M = {k[8:]: v for k, v in a.items() if k.startswith("L1_attn_")}
    F1 = {k[7:]: v for k, v in a.items() if k.startswith("L1_ffn_")}
    w1B = F0["w1"].transpose(1, 0, 2)
    w2B = F0["w2"].reshape(E0, NF, P, P).transpose(2, 0, 1, 3).reshape(P, E0, NF, P)
    xp = M["x_proj_w"].T.reshape(DI, P, -1)
    dt_c, bc_c, gate_c = xp[:, :, :DTR], xp[:, :, DTR:DTR + 2 * NS], xp[:, :, DTR + 2 * NS:]
    xp = np.concatenate([gate_c, bc_c, bc_c, bc_c, dt_c], 2).transpose(1, 0, 2).reshape(P, -1)
    dtp = np.zeros((P, DI * P), np.float32)
    dtp[:DTR] = M["dt_proj_w"].T
    wc = {"in": M["in_proj_w"].T, "xp": xp, "dtp": dtp, "out": M["out_proj_w"].T.reshape(DI, P, P).transpose(1, 0, 2).reshape(P, -1),
          "gate": F1["gate_w"].T, "g_bias": np.broadcast_to(np.tile(F1["expert_bias"], NT), (P, NT * E1)),
          "g_seg": np.broadcast_to(np.tile(np.arange(E1) > 0, NT), (P, NT * E1)).astype(np.float32)}
    wC = np.concatenate([wc[n] for n in WC], 1)
    shared = [F1["shared_gate_w"][None], F1["shared_up_w"][None], F1["shared_down_w"][None]]
    wD = np.stack([np.concatenate([F1[n], sh]) for n, sh in zip(["w_gate", "w_up", "w_down"], shared)], 1)
    wD = wD.transpose(3, 0, 1, 2).reshape(P, 3 * (E1 + 1), P)
    for c in range(DI):
        part = slice(c * P, (c + 1) * P)
        vecs.update({f"dt_b{c}": M["dt_proj_b"][part], f"D{c}": M["D_param"][part], f"cb{c}": M["conv_b"][part]})
        vecs.update({f"cw{c}_{j}": M["conv_w"][part, 0, j] for j in range(KC)})
        vecs.update({f"A{c}_{n}": M["A_log"][part, n] for n in range(NS)})
    vec = np.stack([vecs[n] for n in VEC], 1)

    eye = np.eye(P, dtype=np.float32)
    head_k = np.arange(P) // DK
    head_v = np.arange(P) % H
    gn_mean = (head_v[:, None] == head_v[None]).astype(np.float32) / DK
    reduce = np.zeros((P, 2, 32), np.float32)
    spread = np.zeros((P, 2, P), np.float32)
    for b in range(2):
        reduce[:, b, b * H:(b + 1) * H] = head_k[:, None] == np.arange(H)[None]
        for j in range(4):
            spread[32 * j + b * H:32 * j + (b + 1) * H, b] = np.arange(H)[:, None] == head_k[None]
    c = {"head_sum": head_k[:, None] == head_v[None],
         "gn_mean": gn_mean, "gn_centre": eye - gn_mean, "reduce": reduce.reshape(P, -1), "spread": spread.reshape(P, -1)}
    cst = np.concatenate([c[n].astype(np.float32) for n in CST], 1)
    c = {"centre": eye - 1.0 / P, "mean": np.full((P, P), 1.0 / P), "eye": eye}
    core = np.concatenate([c[n].astype(np.float32) for n in CORE], 1)
    row = lambda v: np.broadcast_to(np.asarray(v, np.float32).reshape(1, -1), (P, np.size(v)))
    experts = np.arange(E0)
    slots = 1 + np.arange(P)[:, None] + CAP * experts[None]
    c = {"iota": row(1 + np.arange(E0 * CAP)), "tri": np.triu(np.ones((P, P))), "ones": np.ones((P, P)),
         "rank": row(np.tile(E0 - experts, NT)), "seg": row(np.tile(np.arange(NT) > 0, E0)), 
         "iota_p": slots, "b_switch": row(np.tile(F0["b_switch"], NT)), "w_switch": F0["w_switch"],
         "b1": F0["b1"].reshape(E0, NF, P).transpose(2, 0, 1).reshape(P, -1), "b2": row(F0["b2"].reshape(-1))}
    cstB = np.concatenate([c[n].astype(np.float32) for n in CSTB], 1)
    bf = mybir.dt.np(mybir.dt.bfloat16)
    sel = np.zeros((3, 2 * NS, 2 * NS, P), np.float32)
    sel[:, np.arange(2 * NS), np.arange(2 * NS)] = 1
    sel = sel.reshape(96, 2 * NS, P).astype(bf)

    nc = bacc.Bacc("TRN2", target_bir_lowering=False, num_devices=1)
    arrays = {"x": x, "vec": vec, "core": core, "cst": cst, "wA": wA, "wmod": wmod, "cstB": cstB, "wB1": w1B, "wB2": w2B, "wC": wC,
              "sel": sel, "eyeb": eye.astype(bf), "wD": wD}
    aps = []
    for name, v in arrays.items():
        arrays[name] = v = np.ascontiguousarray(v)
        aps.append(nc.dram_tensor(f"in_{name}", v.shape, mybir.dt.from_np(v.dtype), kind="ExternalInput").ap())
    o = nc.dram_tensor("out_x", (P, T), mybir.dt.float32, kind="ExternalOutput").ap()
    build(nc, *aps, o)
    r = run_bass_kernel_spmd(nc, [{f"in_{k}": v for k, v in arrays.items()}], core_ids=[0])
    return np.ascontiguousarray(r.results[0]["out_x"].T)[None]
```

```python
from contextlib import ExitStack

import concourse.bass as bass
from concourse import mybir

P = 128
T = 2048
N = 512
NCH = T // N
WD_AT = 38600
ARENA_W = WD_AT + 3 * 17 * P
NT = T // P
H, DK = 16, 8
LORA = 64
F = 512
NF = F // P
E0 = 8
CAP = int(0.5 * T / E0)
EPS_LN, EPS_RMS, EPS_GN = 1e-5, 1e-6, 1e-5
GATE_FLOOR = 0.25

NS = 16
DI = 2
KC = 4
DTR = 8
E1, TOPK = 16, 8
NQ = NCH * NS
E_SMALL = 1e-3
TURNS = NCH * (E1 + 1)
LAG_E = 2
WD_PARTS = 4
LAG = 4
C_RING, DEC_RING, DBU_RING, PR_RING = 4, 6, 4, 2 * LAG
ROUTE_SCALE = 2.826
VEC = ["ln1_w", "mu_r", "mu_k", "mu_v", "mu_w", "mu_g", "w0", "u", "gn_w", "gn_b", "ln2_w",
       "c0", "c1", "eps5", "eps6",
       "dt_b0", "dt_b1", "D0", "D1", "cb0", "cb1"] + [f"cw{c}_{j}" for c in range(DI) for j in range(KC)] + \
    [f"A{c}_{n}" for c in range(DI) for n in range(NS)]
CORE = {"centre": P, "mean": P, "eye": P}
CST = {"head_sum": P, "gn_mean": P, "gn_centre": P, "reduce": 2 * 32, "spread": DK * P}
CSTB = {"iota": E0 * CAP, "tri": P, "ones": P, "rank": NT * E0, "seg": NT * E0, "iota_p": E0, "b_switch": NT * E0,
        "w_switch": E0, "b1": E0 * NF, "b2": E0 * P}
WC = {"in": 2 * DI * P, "xp": DI * (DI * P + 3 * 2 * NS + DTR), "dtp": DI * P, "out": DI * P, "gate": E1, "g_bias": NT * E1, "g_seg": NT * E1}
BC3 = 3 * 2 * NS
XPW = DI * P + 3 * 2 * NS + DTR
WA = {"Wr": P, "Wk": P, "Wv": P, "Wg": P, "Wo": P, "wA": LORA, "wB": P, "w1": F, "w2": F}


def columns(widths):
    at, out = 0, {}
    for name, w in widths.items():
        out[name] = (at, w)
        at += w
    return out, at


def each_chunk(*steps):
    return [(s, i) for i in range(NCH) for s in steps]


def layernorm(k):
    return ([(f"centre{k}", i) for i in range(NCH)] + [(f"var{k}", i) for i in range(NCH)],
            [(f"sq{k}", i) for i in range(NCH)] + each_chunk(f"ln{k}", f"rs{k}"),
            each_chunk(f"norm{k}", f"mod{k}"))


def rmsnorm(k):
    return (each_chunk(f"ms{k}"), [(f"sq{k}", i) for i in range(NCH)] + each_chunk(f"ln{k}", f"rs{k}"),
            each_chunk(f"norm{k}"))


ORDER = [0, 2, 4, 6, 1, 3, 5, 7]
NR = NCH * DK
LAG_R = 9


def one(*steps):
    return [(s, 0) for s in steps]


def sequences():
    pe, act, dve, pool = [], [], [], []

    def add(to, *parts):
        for part in parts:
            to.extend(part)

    ln_pe, ln_act, ln_dve = layernorm("A")
    rm_pe, rm_act, rm_dve = rmsnorm("B")
    add(pe, one("mod"), ln_pe, rm_pe, *(each_chunk(s) for s in ["r", "k", "v", "lora_a", "g", "lora_b", "head_ruk"]))
    add(act, one("c_exp"), ln_act, rm_act, *(each_chunk(s) for s in ["r_copy", "k_copy", "v_copy", "lora_tanh", "g_silu"]), one("spread_r"), each_chunk("v_hi"),
        each_chunk("w_exp", "decay"))
    add(dve, one("c_one", "c_recip", "c_silu", "mod_copy", "mod_ca", "mod_sign", "mod_sign2", "mod_abs", "mod_floor", "mod_gate"),
        ln_dve, rm_dve, *(each_chunk(s) for s in ["xx", "mix_r", "mix_k", "mix_v", "mix_w", "mix_g", "ruk", "bonus"]), one("s_zero"))
    add(pool, one("h1_zero"))
    add(pool, each_chunk("v_lo"))
    dve.append(("kv0", 0))
    for q in range(NR + LAG_R - 1):
        i, k = divmod(q, DK)
        if q < NR:
            pe.append((f"spread{ORDER[k]}", i))
            if q + 1 < NR:
                dve.append((f"kv{ORDER[(q + 1) % DK]}", (q + 1) // DK))
            dve.append((f"scan{ORDER[k]}", i))
            pool.append((f"prod{ORDER[k]}", i))
            if i and k == DK - 1:
                dve.append(("o", i - 1))
        if q >= LAG_R and (q - LAG_R) % 4 == 0:
            pe += [(f"reduce{ORDER[(q - LAG_R + j) % DK]}", (q - LAG_R) // DK) for j in range(4)]
    dve.append(("o", NCH - 1))
    rm_pe, rm_act, rm_dve = rmsnorm("C")
    add(pe, each_chunk("gn_centred"), each_chunk("gn_var"), each_chunk("wo"), rm_pe,
        each_chunk(*[f"up{f}" for f in range(NF)], *[f"down{f}" for f in range(NF)]))
    add(act, each_chunk("gn_sq"), each_chunk("gn_ln", "gn_rs", "gn_rs2"), rm_act, each_chunk(*[f"gelu{f}" for f in range(NF)]))
    add(dve, each_chunk("gn_err", "gn_half", "gn_rsqrt", "gn_norm", "gn_affine", "gn_gate"), each_chunk("x1"), rm_dve, each_chunk("ffn_sum", "x_attn"))

    ln_pe, ln_act, ln_dve = layernorm("D")
    add(pe, ln_pe, one("router"), [("h_turn", t) for t in range(NT)], one("prefix", "totals"),
        [("dispatch", t) for t in range(SPREAD_AT)], each_chunk("slot_spread"), [("dispatch", t) for t in range(SPREAD_AT, NT)], [("e_up", 0), ("e_up", 1)])
    add(act, ln_act, one("r_exp"), [("h_turned", q) for q in range(NCH)], one("ones_r"),
        [("slot_diag", t) for t in range(NT)], each_chunk("slots"),
        [("scale_diag", t) for t in range(NT)], one("buf0"), [("e_relu", 1)])
    add(dve, ln_dve, one(*R_STEPS), *([("h_turned_lo", i)] + [("onehot", 4 * i + j) for j in range(4)] for i in range(NCH)), one("buf1"),
        [("e_relu", 0)])
    for e in range(E0):
        pe += [("e_down", e)] + ([("e_up", e + 2)] if e + 2 < E0 else []) + ([("scale_spread", e)] if e < NCH else [])
        act += [("y_hi", e)] + ([("e_relu", e + 2)] if e + 2 < E0 and e % 2 else []) + ([("scales", e)] if e < NCH else [])
        dve += [(f"place{(2 * e + j) % E0}", (2 * e + j) // E0) for j in range(2)] + \
            [("y_lo", e)] + ([("e_relu", e + 2)] if e + 2 < E0 and e % 2 == 0 else []) + ([("kept_x", e)] if e < NCH else [])
    for i in range(NCH):
        pe += [(f"combine{e}", i) for e in range(E0)]
        dve += [("moe_sum", i), ("moe_scaled", i)] + [(f"place{e}", i + 2) for e in range(E0) if i + 2 < NCH]
        pool.append(("x_moe", i))

    ln_pe, ln_act, ln_dve = layernorm("E")
    add(pe, ln_pe, *(each_chunk(s) for s in ["xb0", "xb1", "z0", "z1"]), each_chunk("bc", "gate0"), each_chunk("gate1"),
        each_chunk("dt0", "dt1"))
    add(act, ln_act, *(each_chunk(s) for s in ["xb0_copy", "xb1_copy", "z0_silu", "z1_silu"]))
    add(dve, ln_dve, one("xb_zero"))
    proj = ["bc_hi", "dt_raw_copy", "gate0_tanh"]
    for i in range(NCH):
        dve += [(f"conv{c}_{j}", i) for c in range(DI) for j in range(KC)] + ([("bc_r1", i - 1)] if i else [])
        act += [("u0", i), ("u1", i)] + ([(s, i - 1) for s in proj] if i else [])
    add(dve, [("bc_r1", NCH - 1)])
    add(act, [(s, NCH - 1) for s in proj], each_chunk("bc_mid"), each_chunk("gate1_tanh"), one("a_exp"))
    add(dve, one("a_neg", "st_zero"))
    add(pool, each_chunk("bc_lo"))
    for i in range(NCH):
        act += [(f"{s}_{c}", i) for c in range(DI) for s in ("sp_abs", "sp_e", "sp_relu", "sp_w")]
        dve += [(f"sp_r_{c}", i) for c in range(DI)]
        pool += [(f"{s}_{c}", i) for c in range(DI) for s in ("sp_p", "sp_lo")]
        act += [(f"sp_ln_{c}", i - 1) for c in range(DI) if i]
        dve += [(f"{s}_{c}", i - 1) for s in ("sp_log", "sp_mask", "sp_max", "dt", "dtg") for c in range(DI) if i]
        pool += [(f"du_{c}", i - 1) for c in range(DI) if i]
    act += [(f"sp_ln_{c}", NCH - 1) for c in range(DI)]
    dve += [(f"{s}_{c}", NCH - 1) for s in ("sp_log", "sp_mask", "sp_max", "dt", "dtg") for c in range(DI)]
    pool += [(f"du_{c}", NCH - 1) for c in range(DI)]
    dve += [("dbu0_0", 0), ("dbu0_1", 0)]
    for q in range(NQ):
        i, n = divmod(q, NS)
        act += [(f"c_copy{n}", i), (f"dec{n}_0", i), (f"dec{n}_1", i)]
        pe += [(f"b{n}", i), (f"c{n}", i)]
        if q >= LAG:
            m = (q - LAG) % NS
            pe += [(f"y{m}_0", (q - LAG) // NS), (f"y{m}_1", (q - LAG) // NS)]
        if q + 1 < NQ:
            m = (q + 1) % NS
            dve += [(f"dbu{m}_0", (q + 1) // NS), (f"dbu{m}_1", (q + 1) // NS)]
        dve += [(f"st{n}_0", i), (f"st{n}_1", i)]
        pool += [(f"sc{n}_0", i), (f"sc{n}_1", i)]
        if i and n == LAG:
            dve += [("skip_0", i - 1), ("skip_1", i - 1)]
            pool += [("gated_0", i - 1), ("gated_1", i - 1)]
    for m in range(NS - LAG, NS):
        pe += [(f"y{m}_0", NCH - 1), (f"y{m}_1", NCH - 1)]
    dve += [("skip_0", NCH - 1), ("skip_1", NCH - 1)]
    pool += [("gated_0", NCH - 1), ("gated_1", NCH - 1)]
    add(pe, each_chunk("m_out"))
    add(dve, each_chunk("x_mamba"))

    ln_pe, ln_act, ln_dve = layernorm("F")
    add(pe, ln_pe, one("g_router"), [("g_turn", t) for t in range(NT)])
    add(act, ln_act, one("g_exp"), [("w_hi", k) for k in range(WD_PARTS)], each_chunk("x_hi"), [("g_turned", h) for h in range(2)])
    add(dve, ln_dve, one(*G_STEPS))
    pool += [("w_lo", k) for k in range(WD_PARTS)]
    pool += [("x_lo", i) for i in range(NCH)]
    for q in range(TURNS + LAG_E):
        i, e = divmod(q, E1 + 1)
        if q < TURNS:
            pe += [(f"hg{e}", i), (f"hu{e}", i)] + ([(f"w{e}", i)] if e < E1 else [])
            act.append((f"silu{e}", i))
            dve += [(f"hh{e}", i)] + ([(f"hw{e}", i)] if e < E1 else [])
            pool.append((f"h_lo{e}", i))
        if 1 <= q <= TURNS:
            act.append((f"h_hi{(q - 1) % (E1 + 1)}", (q - 1) // (E1 + 1)))
        if q >= LAG_E:
            pe.append((f"hd{(q - LAG_E) % (E1 + 1)}", (q - LAG_E) // (E1 + 1)))
        if i and e == LAG_E + 1:
            dve.append(("x_out", i - 1))
    dve.append(("x_out", NCH - 1))
    return {"pe": pe, "act": act, "dve": dve, "pool": pool}


SPREAD_AT = NT - 3
R_STEPS = ["r_logit", "r_max", "r_shift", "r_sum", "r_recip", "r_prob", "r_pmax", "r_hit", "r_rank", "r_best", "r_oh",
           "r_precip", "r_scale", "r_tot", "r_cum", "r_off", "r_pos", "r_own", "r_place", "r_keep", "r_base", "r_slot", "r_kept"]
G_STEPS = ["g_one", "g_score", "g_sel"] + [f"g_top{t}" for t in range(NT)] + \
    ["g_gt", "g_eq", "g_ngt", "g_left", "g_cum", "g_le", "g_tie", "g_mask", "g_pick", "g_total", "g_inv", "g_w",
     "g_zero", "g_hi", "g_r1", "g_mid", "g_lo"]


def build(nc, X_in, vec_in, core_in, cst_in, wA_in, wmod_in, cstB_in, wB1_in, wB2_in, wC_in, sel_in, eyeb_in, wD_in, out):
    f32 = mybir.dt.float32
    bf16 = mybir.dt.bfloat16
    f32r = mybir.dt.float32r
    ALU = mybir.AluOpType
    ACT = mybir.ActivationFunctionType
    AX = mybir.AxisListType.X
    SEQ = sequences()
    count = {step: (e, k + 1) for e, steps in SEQ.items() for k, step in enumerate(steps)}
    assert len(count) == sum(map(len, SEQ.values()))
    core_at, core_n = columns(CORE)
    cst_at, cst_n = columns(CST)
    wa_at, wa_n = columns(WA)
    cb_at, cb_n = columns(CSTB)
    wc_at, wc_n = columns(WC)

    ctx = ExitStack()
    with ctx:
        def sb(name, shape, dt=f32):
            return ctx.enter_context(nc.sbuf_tensor(name, shape, dt))

        def sem(name):
            return ctx.enter_context(nc.semaphore(name))

        x_loaded, vec_loaded, core_loaded, wa_loaded, wb_loaded, wc_loaded, out_stored = map(
            sem, ["x_loaded", "vec_loaded", "core_loaded", "wa_loaded", "wb_loaded", "wc_loaded", "out_stored"])
        wd_loaded = [sem(f"wd_loaded{k}") for k in range(WD_PARTS)]
        finished = {e: sem(f"{e}_done") for e in SEQ}
        order = {e: list(steps) for e, steps in SEQ.items()}

        def upto(step, i=0):
            engine, n = count[step, i]
            return finished[engine], n

        def done(step, i=0):
            engine, n = count[step, i]
            assert order[engine].pop(0) == (step, i), (step, i)
            return finished[engine], 1

        def turn(step, q):
            return upto(step.format(q % NS), q // NS)

        def column(step, q):
            return upto(step.format(ORDER[q % DK]), q // DK)

        def expert(step, q):
            return upto(step.format(q % (E1 + 1)), q // (E1 + 1))

        X = sb("x", [P, T])
        vec = sb("vec", [P, len(VEC)])
        core = sb("core", [P, core_n])
        mod = sb("mod", [P, 12])
        mtmp = sb("mtmp", [P, 24])
        wC = sb("wC", [P, wc_n])
        sel = sb("sel", [96, 2 * NS, P], bf16)
        BC = sb("bc", [96, T], bf16)
        EYEB = sb("eyeb", [P, P], bf16)
        CARRY = sb("carry", [P, 1])
        ABASE = sb("abase", [P, DI * NS])
        with nc.sbuf_tensor("arena", [P, WD_AT], f32) as ARENA:
            pass

        def over_arena(name, at, n, dt):
            assert at + n <= ARENA_W, (name, at + n)
            with nc.sbuf_tensor(f"below_{name}", [P, at], f32), nc.sbuf_tensor(name, [P, n], dt) as t:
                return t[:]

        ps = ctx.enter_context(nc.psum_tensor("ps", [P, 8 * N], f32))

        def col(name):
            k = VEC.index(name)
            return vec[:, k:k + 1]

        def area(at, n):
            return ARENA[:, at:at + n]

        def CORE_(name):
            a, w = core_at[name]
            return core[:, a:a + w]

        def C(name, part=slice(None)):
            a, w = cst_at[name]
            return cst[part, a:a + w]

        def W(name, part=slice(None)):
            a, w = wa_at[name]
            return wA[part, a:a + w]

        def CB_(name):
            a, w = cb_at[name]
            return cstB[:, a:a + w]

        def WC_(name):
            a, w = wc_at[name]
            return wC[:, a:a + w]

        wd_flat = over_arena("wD", WD_AT, 3 * (E1 + 1) * P, f32)
        wD = wd_flat.rearrange("p (k m) -> p k m", k=3 * (E1 + 1))
        SV = T + 1
        S = area(0, DK * SV).rearrange("p (v t) -> p v t", v=DK)
        H1 = area(0, T + 1)
        XX = area(1 * 2052, T)
        M0 = area(2 * 2052, T)
        M1 = area(3 * 2052, T)
        at = DK * SV
        HLN, M2, K, R, DEC, V, G = (area(at + j * T, T) for j in range(7))
        at += 7 * T
        PR = area(at, 8 * N).rearrange("p (s t) -> p s t", s=8)
        KV = wd_flat[:, 2 * T:2 * T + 4 * N].rearrange("p (s t) -> p s t", s=4)
        v_parts = over_arena("v_parts", WD_AT, 2 * T, f32r).rearrange("p (s t) -> p s t", s=2)
        TA = area(at + 4 * N, T)
        T1, T2, T3 = K, R, DEC
        O = BONUS = M2
        GEL = PR[:, 0:4]
        at += 8 * N
        wA = area(at, wa_n)
        cst = area(at + wa_n, cst_n)
        spread_r = over_arena("spread_r", at + wa_n + cst_at["spread"][0], DK * P, f32r)
        assert at + wa_n + cst_n <= WD_AT, at + wa_n + cst_n
        wmod = area(4 * 2052, 2 * 6 * P).rearrange("p (l k) -> p l k", l=2)

        cstB = area(0, cb_n)
        assert cb_n <= 2780
        PTS = [over_arena(f"place{k}", at_k, E0 * N, f32r).rearrange("p (e t) -> p e t", e=E0) for k, at_k in enumerate((4100, 34400))]
        assert 34400 + E0 * N <= WD_AT
        WB = area(8200, 8192)
        w1B = WB[:, 0:4096].rearrange("p (e f) -> p e f", e=E0)
        w2B = WB[:, 4096:8192].rearrange("p (e f m) -> p e f m", e=E0, f=NF)
        TB, HB, SLB, SCB = DEC, V, M2, K
        DG = over_arena("slot_diags", DK * SV + 3 * T, T, f32r)
        HT = over_arena("h_turned", WD_AT, 2 * T, f32r).rearrange("p (s t) -> p s t", s=2)
        OH1 = over_arena("onehot", WD_AT + 2 * T, T, f32r).rearrange("p (s c) -> p s c", s=2)
        YB = over_arena("y", WD_AT, 2 * E0 * P, f32r).rearrange("p (s e m) -> p s e m", s=2, e=E0)
        ONES_R = over_arena("ones_r", 34100, P, f32r)
        DG2 = HLN
        at = DK * SV + 7 * T
        BUF = area(at, E0 * CAP)
        HS = area(at + 1024, 2 * N).rearrange("p (s f t) -> p s f t", s=2, f=NF)
        small = lambda k: area(2780 + k * P, P)
        small3 = lambda k: small(k).rearrange("p (t e) -> p t e", e=E0)
        tiny = lambda k: area(at + 3072 + k * NT, NT)

        ST = area(0, 32 * N).rearrange("p (k t) -> p k t", k=32)
        TE = area(8200, T)
        HC = area(10248, T)
        XBP = area(12296, DI * (T + 3)).rearrange("p (c t) -> p c t", c=DI)
        CV = area(0, DI * T).rearrange("p (c t) -> p c t", c=DI)
        at = 16400
        U, Z, DTG, DU = (area(at + j * DI * T, DI * T).rearrange("p (c t) -> p c t", c=DI) for j in range(4))
        at += 4 * DI * T
        ring = lambda buf, s: buf.rearrange("p (s t) -> p s t", s=s)
        CBR = ring(area(at, C_RING * N), C_RING)
        DECR = ring(area(at + C_RING * N, DEC_RING * N), DEC_RING)
        assert at + (C_RING + DEC_RING) * N <= ARENA_W
        DBU = ring(wd_flat[:, 0:DBU_RING * N], DBU_RING)
        PRC = ring(wd_flat[:, DBU_RING * N:(DBU_RING + PR_RING) * N], PR_RING)
        SPX = wd_flat[:, 0:DI * T].rearrange("p (c t) -> p c t", c=DI)
        R1 = area(at, T)
        DRAW = area(at + T, T)
        SPE, SPR, SPW, SPL = (area(j * DI * T, DI * T).rearrange("p (c t) -> p c t", c=DI) for j in range(4))

        TF, HD = area(0, T), area(T, T)
        SG, HH, HW = (ring(area((4 + k) * 1024, 2 * N), 2) for k in range(3))
        at = 16384
        w_parts = over_arena("w_parts", at, 2 * 3 * (E1 + 1) * P, f32r).rearrange("p (s k m) -> p s k m", s=2, k=3 * (E1 + 1))
        at += 2 * 3 * (E1 + 1) * P
        x_parts = over_arena("x_parts", at, 2 * T, f32r).rearrange("p (s t) -> p s t", s=2)
        at += 2 * T
        HWP = over_arena("h_parts", at, 8 * N, f32r).rearrange("p (s r t) -> p s r t", s=2, r=4)
        assert at + 8 * N <= ARENA_W
        wd_part = lambda k: slice(k * 3 * (E1 + 1) // WD_PARTS, (k + 1) * 3 * (E1 + 1) // WD_PARTS)
        gsmall = lambda k: area(2 * T + 6 * N + k * 256, 256)
        gsmall3 = lambda k: gsmall(k).rearrange("p (t e) -> p t e", e=E1)
        gtiny = lambda k: area(2 * T + 6 * N + 16 * 256 + k * NT, NT)
        CS = area(2 * T + 6 * N + 17 * 256, NT * 96 // 2).bitcast(bf16).rearrange("p (t r) -> p t r", t=NT)

        def ch(buf, i, off=0):
            return buf[:, i * N + off:(i + 1) * N + off]

        def half(h, i, rows=P):
            return ps[0:rows, (4 * h + i) * N:(4 * h + i + 1) * N]

        def bank(b, lo=0, hi=P):
            return ps[lo:hi, b * N:(b + 1) * N]

        modcol = lambda layer, k: mod[:, 6 * layer + k:6 * layer + k + 1]
        SA, CA, GA, SB_, CB, GB = range(6)

        block = ctx.enter_context(nc.Block())

        def bcast(col2, e):
            return col2.unsqueeze(2).to_broadcast([P, col2.shape[1], e])

        def expert_b1(e, f):
            a = cb_at["b1"][0] + e * NF + f
            return cstB[:, a:a + 1]

        @block.sync
        def _(sp):
            sp.dma_start(X[:], X_in).then_inc(x_loaded, 16)
            sp.dma_start(vec[:], vec_in).then_inc(vec_loaded, 16)
            sp.dma_start(wmod, wmod_in).then_inc(vec_loaded, 16)
            sp.dma_start(core[:], core_in).then_inc(core_loaded, 16)
            sp.dma_start(cst, cst_in).then_inc(core_loaded, 16)
            sp.dma_start(wA, wA_in).then_inc(wa_loaded, 16)
            sp.dma_start(wC[:], wC_in).then_inc(wc_loaded, 16)
            sp.dma_start(EYEB[:], eyeb_in).then_inc(wc_loaded, 16)
            sp.dma_start(sel[:], sel_in).then_inc(wc_loaded, 16)
            sp.wait_ge(*upto("prod7", NCH - 1))
            sp.wait_ge(*upto("o", NCH - 1))
            sp.dma_start(cstB, cstB_in).then_inc(wb_loaded, 16)
            sp.dma_start(w1B, wB1_in).then_inc(wb_loaded, 16)
            sp.dma_start(w2B, wB2_in).then_inc(wb_loaded, 16)
            sp.wait_ge(*upto(f"y{NS - 1}_1", NCH - 1))
            for k in range(WD_PARTS):
                sp.dma_start(wD[:, wd_part(k), :], wD_in[:, wd_part(k), :]).then_inc(wd_loaded[k], 16)
            for i in range(NCH):
                sp.wait_ge(*upto("x_out", i))
                sp.dma_start(out[:, i * N:(i + 1) * N], X[:, i * N:(i + 1) * N]).then_inc(out_stored, 16)
            sp.wait_ge(out_stored, 16 * NCH)

        @block.tensor
        def _(pe):
            mm = nc.tensor.matmul

            def sweep(step, lhsT, rhs, h, waits, rows=P, parts=P):
                for i in range(NCH):
                    for w in waits:
                        pe.wait_ge(*upto(w, i))
                    mm(half(h, i, rows), lhsT, ch(rhs, i)[0:parts], start=True, stop=True).then_inc(*done(step, i))

            pe.wait_ge(vec_loaded, 32)
            pe.wait_ge(*upto("c_silu"))
            for layer in range(2):
                for k in range(6):
                    j = 6 * layer + k
                    last = mm(ps[:, 7 * N + j:7 * N + j + 1], wmod[:, layer, k * P:(k + 1) * P],
                              mtmp[:, 4 + layer:5 + layer], start=True, stop=True)
            last.then_inc(*done("mod"))
            pe.wait_ge(core_loaded, 32)
            pe.wait_ge(x_loaded, 16)
            sweep("centreA", CORE_("centre"), X, 0, [])
            pe.wait_ge(*upto("mod_copy"))
            sweep("varA", CORE_("mean"), T1, 1, ["sqA"])
            sweep("msB", CORE_("mean"), T2, 0, ["sqB", "normA"])
            pe.wait_ge(wa_loaded, 16)
            sweep("r", W("Wr"), M0, 1, ["mix_r", "lnA"])
            sweep("k", W("Wk"), M1, 0, ["mix_k", "lnB"])
            sweep("v", W("Wv"), M2, 1, ["mix_v", "r_copy"])
            sweep("lora_a", W("wA"), M0, 0, ["mix_w", "k_copy"], rows=LORA)
            sweep("g", W("Wg"), M1, 1, ["mix_g", "v_copy"])
            sweep("lora_b", W("wB", slice(0, LORA)), TA, 0, ["lora_tanh"], parts=LORA)
            sweep("head_ruk", C("head_sum"), XX, 1, ["ruk", "g_silu"])

            pe.wait_ge(*upto("bonus", NCH - 1))
            pe.wait_ge(*upto("w_exp", NCH - 1))
            pe.wait_ge(*upto("spread_r"))
            for q in range(NR + LAG_R - 1):
                i, v = q // DK, ORDER[q % DK]
                if q < NR:
                    if q >= 4:
                        pe.wait_ge(*column("kv{}", q - 4))
                    for part, ready in enumerate(("v_hi", "v_lo")):
                        pe.wait_ge(*upto(ready, i))
                        last = mm(bank(4 + q % 4), spread_r[:, v * P:(v + 1) * P], ch(v_parts[:, part, :], i), start=(part == 0), stop=(part == 1))
                    last.then_inc(*done(f"spread{v}", i))
                if q >= LAG_R and (q - LAG_R) % 4 == 0:
                    pe.wait_ge(*column("prod{}", q - LAG_R + 3))
                    for r in range(q - LAG_R, q - LAG_R + 4):
                        i, v = r // DK, ORDER[r % DK]
                        if r % DK < 4 and i >= 2:
                            pe.wait_ge(*upto("o", i - 2))
                        a = cst_at["reduce"][0] + (v % 2) * 32
                        j = 32 * (v // 2)
                        mm(bank(i % 2, j, j + 32), cst[:, a:a + 32], PR[:, r % 8, :], start=(r % DK < 4), stop=(r % DK >= 4)).then_inc(*done(f"reduce{v}", i))

            pe.wait_ge(*upto("kv7", NCH - 1))
            sweep("gn_centred", C("gn_centre"), O, 1, ["o"])
            pe.wait_ge(*upto("o", NCH - 1))
            sweep("gn_var", C("gn_mean"), T1, 0, ["gn_sq"])
            sweep("wo", W("Wo"), O, 1, ["gn_gate"])
            sweep("msC", CORE_("mean"), T2, 0, ["sqC", "gn_err"])
            pe.wait_ge(*upto("lnC", NCH - 1))
            pe.wait_ge(*upto("x1", NCH - 1))
            for i in range(NCH):
                pe.wait_ge(*upto("normC", i))
                for f in range(NF):
                    if i:
                        pe.wait_ge(*upto(f"gelu{f}", i - 1))
                    a = wa_at["w1"][0] + f * P
                    mm(bank(4 + f), wA[:, a:a + P], ch(M0, i), start=True, stop=True).then_inc(*done(f"up{f}", i))
                for f in range(NF):
                    pe.wait_ge(*upto(f"gelu{f}", i))
                    a = wa_at["w2"][0] + f * P
                    mm(half(0, i), wA[:, a:a + P], GEL[:, f, :], start=(f == 0), stop=(f == NF - 1)).then_inc(*done(f"down{f}", i))

            pe.wait_ge(*upto("gelu3", NCH - 1))
            sweep("centreD", CORE_("centre"), X, 1, ["x_attn"])
            sweep("varD", CORE_("mean"), TB, 0, ["sqD", "ffn_sum"])
            pe.wait_ge(wb_loaded, 48)
            pe.wait_ge(*upto("modD", NCH - 1))
            pe.wait_ge(*upto("lnD", NCH - 1))
            for t in range(NT):
                last = mm(ps[:, t * E0:(t + 1) * E0], HB[:, t * P:(t + 1) * P], CB_("w_switch"), start=True, stop=True)
            last.then_inc(*done("router"))
            for t in range(NT):
                nc.tensor.transpose(ps[:, 4 * N + t * P:4 * N + (t + 1) * P], HB[:, t * P:(t + 1) * P], CORE_("eye")).then_inc(*done("h_turn", t))
            pe.wait_ge(*upto("r_oh"))
            mm(bank(1)[:, 0:P], CB_("tri"), small(3), start=True, stop=True).then_inc(*done("prefix"))
            mm(bank(2)[:, 0:P], CB_("ones"), small(3), start=True, stop=True).then_inc(*done("totals"))
            def slot_spread():
                pe.wait_ge(*upto("ones_r"))
                pe.wait_ge(*upto("h_turned_lo", NCH - 1))
                for i in range(NCH):
                    pe.wait_ge(*upto("slot_diag", 4 * i + 3))
                    mm(half(1, i), ONES_R, ch(DG, i), start=True, stop=True).then_inc(*done("slot_spread", i))

            for t in range(NT):
                if t == SPREAD_AT:
                    slot_spread()
                pe.wait_ge(*upto("onehot", t))
                pe.wait_ge(*upto("h_turned_lo", t // 4))
                for part in range(2):
                    for j in range(2):
                        last = mm(bank(3 * j), HT[:, part, t * P:(t + 1) * P], OH1[:, t % 2, j * N:(j + 1) * N],
                                  start=(t == 0 and part == 0), stop=(t == NT - 1 and part == 1))
                last.then_inc(*done("dispatch", t))
            pe.wait_ge(*upto("buf0"))
            pe.wait_ge(*upto("buf1"))

            def e_up(e):
                for f in range(NF):
                    last = mm(bank(6 + e % 2)[:, f * P:(f + 1) * P], w1B[:, e, f * P:(f + 1) * P], BUF[:, e * CAP:(e + 1) * CAP], start=True, stop=True)
                last.then_inc(*done("e_up", e))

            pe.wait_ge(*upto("slots", NCH - 1))
            e_up(0)
            e_up(1)
            for e in range(E0):
                pe.wait_ge(*upto("e_relu", e))
                if e >= 2:
                    pe.wait_ge(*upto("y_lo", e - 2))
                o = bank(2 + e % 2)[:, 0:P]
                a = cb_at["b2"][0] + e * P
                mm(o, CB_("ones")[0:1, :], cstB[0:1, a:a + P], start=True, stop=False)
                for f in range(NF):
                    last = mm(o, HS[:, e % 2, f, :], w2B[:, e, f, :], start=False, stop=(f == NF - 1))
                last.then_inc(*done("e_down", e))
                if e + 2 < E0:
                    e_up(e + 2)
                if e < NCH:
                    pe.wait_ge(*upto("scale_diag", 4 * e + 3))
                    if e >= 2:
                        pe.wait_ge(*upto("scales", e - 2))
                    mm(bank(4 + e % 2), CB_("ones"), ch(DG2, e), start=True, stop=True).then_inc(*done("scale_spread", e))
            pe.wait_ge(*upto("y_lo", E0 - 1))
            for i in range(NCH):
                for e in range(E0):
                    pe.wait_ge(*upto(f"place{e}", i))
                    for part in range(2):
                        last = mm(half(0, i), YB[:, part, e, :], PTS[i % 2][:, e, :], start=(e == 0 and part == 0), stop=(e == E0 - 1 and part == 1))
                    last.then_inc(*done(f"combine{e}", i))

            sweep("centreE", CORE_("centre"), X, 1, ["x_moe", "scales"])
            sweep("varE", CORE_("mean"), TE, 0, ["sqE", "moe_sum"])
            pe.wait_ge(wc_loaded, 48)
            prev = {0: "lnE", 1: "normE"}
            a = wc_at["in"][0]
            for k, step in enumerate(["xb0", "xb1", "z0", "z1"]):
                h = 1 - k % 2
                sweep(step, wC[:, a + k * P:a + (k + 1) * P], HC, h, [prev[h], "modE"])
                prev[h] = step + ("_copy" if k < 2 else "_silu")

            def x_proj(step, h, i, col0, rows, waits):
                for w in waits:
                    pe.wait_ge(*upto(w, i))
                for c in range(DI):
                    b = wc_at["xp"][0] + c * XPW + col0
                    last = mm(half(h, i, rows), wC[:, b:b + rows], ch(U[:, c, :], i), start=(c == 0), stop=(c == DI - 1))
                last.then_inc(*done(step, i))

            for i in range(NCH):
                x_proj("bc", 1, i, DI * P, BC3 + DTR, ["z0_silu", "u1"])
                x_proj("gate0", 0, i, 0, P, ["z1_silu"])
            for i in range(NCH):
                x_proj("gate1", 1, i, P, P, ["dt_raw_copy", "bc_r1"])
            a = wc_at["dtp"][0]
            for i in range(NCH):
                for c, w in enumerate(("gate0_tanh", "gate1_tanh")):
                    pe.wait_ge(*upto(w, i))
                    mm(half(c, i), wC[BC3:BC3 + DTR, a + c * P:a + (c + 1) * P], ch(DRAW, i)[BC3:BC3 + DTR],
                       start=True, stop=True).then_inc(*done(f"dt{c}", i))

            def y_sum(q):
                i, n = divmod(q, NS)
                for c in range(DI):
                    if n == 0 and i >= 2:
                        pe.wait_ge(*upto(f"skip_{c}", i - 2))
                    pe.wait_ge(*upto(f"sc{n}_{c}", i))
                    mm(bank(c + 2 * (i % 2)), CORE_("eye"), PRC[:, (2 * q + c) % PR_RING, :], start=(n == 0), stop=(n == NS - 1)).then_inc(*done(f"y{n}_{c}", i))

            pe.wait_ge(*upto("sp_relu_1", NCH - 1))
            pe.wait_ge(*upto("bc_lo", NCH - 1))
            for q in range(NQ):
                i, n = divmod(q, NS)
                for kind, b, last_use, row in (("b", 4, "dbu{}_1", n), ("c", 6, "c_copy{}", NS + n)):
                    if q >= 2:
                        pe.wait_ge(*turn(last_use, q - 2))
                    mm(bank(b + q % 2), sel[:, row, :], BC[:, i * N:(i + 1) * N], start=True, stop=True).then_inc(*done(f"{kind}{n}", i))
                if q >= LAG:
                    y_sum(q - LAG)
            for q in range(NQ - LAG, NQ):
                y_sum(q)
            pe.wait_ge(*upto(f"dbu{NS - 1}_1", NCH - 1))
            pe.wait_ge(*upto(f"c_copy{NS - 1}", NCH - 1))
            a = wc_at["out"][0]
            for i in range(NCH):
                for c in range(DI):
                    pe.wait_ge(*upto(f"gated_{c}", i))
                    last = mm(half(1, i), wC[:, a + c * P:a + (c + 1) * P], ch(U[:, c, :], i), start=(c == 0), stop=(c == DI - 1))
                last.then_inc(*done("m_out", i))

            pe.wait_ge(*upto("skip_1", NCH - 1))
            sweep("centreF", CORE_("centre"), X, 0, ["x_mamba"])
            sweep("varF", CORE_("mean"), TF, 1, ["sqF"])
            pe.wait_ge(*upto("modF", NCH - 1))
            for t in range(NT):
                last = mm(ps[:, t * E1:(t + 1) * E1], HD[:, t * P:(t + 1) * P], WC_("gate"), start=True, stop=True)
            last.then_inc(*done("g_router"))
            pe.wait_ge(*upto("g_lo"))
            for t in range(NT):
                o = ps[0:96, 2 * N:4 * N].bitcast(bf16)[:, t * P:(t + 1) * P]
                nc.tensor.transpose(o, CS[:, t, :], EYEB[:]).then_inc(*done("g_turn", t))
            pe.wait_ge(*upto("g_turned", 1))
            pe.wait_ge(*upto("lnF", NCH - 1))
            def product(out, k, x, wait_lo, start=True, stop=True):
                for wp, xp, last in ((0, 0, False), (1, 0, False), (0, 1, True)):
                    if last and wait_lo:
                        pe.wait_ge(*upto(*wait_lo))
                    r = mm(out, w_parts[:, wp, k, :], x[xp], start=start and (wp, xp) == (0, 0), stop=stop and last)
                return r

            def down(q):
                i, e = divmod(q, E1 + 1)
                if e == 0 and i >= 2:
                    pe.wait_ge(*upto("x_out", i - 2))
                pe.wait_ge(*upto(f"h_hi{e}", i))
                product(bank(6 + i % 2), 3 * e + 2, [HWP[:, p, q % 4, :] for p in range(2)], (f"h_lo{e}", i),
                        start=(e == 0), stop=(e == E1)).then_inc(*done(f"hd{e}", i))

            pe.wait_ge(*upto("w_lo", WD_PARTS - 1))
            for q in range(TURNS):
                i, e = divmod(q, E1 + 1)
                k = q % 2
                x = [ch(x_parts[:, p, :], i) for p in range(2)]
                pe.wait_ge(*upto("x_lo", i))
                if q >= 2:
                    pe.wait_ge(*expert("silu{}", q - 2))
                product(bank(0 + k), 3 * e, x, None).then_inc(*done(f"hg{e}", i))
                if q >= 2:
                    pe.wait_ge(*expert("hh{}", q - 2))
                product(bank(2 + k), 3 * e + 1, x, None).then_inc(*done(f"hu{e}", i))
                if e < E1:
                    if q >= 2:
                        pe.wait_ge(*expert("hw{}" if (q - 2) % (E1 + 1) < E1 else "hh{}", q - 2))
                    mm(bank(4 + k), sel[:, e, :], BC[:, i * N:(i + 1) * N], start=True, stop=True).then_inc(*done(f"w{e}", i))
                if q >= LAG_E:
                    down(q - LAG_E)
            for q in range(TURNS - LAG_E, TURNS):
                down(q)

        @block.scalar
        def _(act):
            A = nc.scalar.activation

            def square(step, src, dst, waits):
                for i in range(NCH):
                    for w in waits:
                        act.wait_ge(*upto(w, i))
                    A(ch(dst, i), src(i), ACT.Square).then_inc(*done(step, i))

            def rsqrt(k, h, buf, eps, waits):
                for i in range(NCH):
                    for w in waits:
                        act.wait_ge(*upto(w, i))
                    A(ch(buf, i), half(h, i), ACT.Ln, bias=eps).then_inc(*done(f"ln{k}", i))
                    act.wait_ge(*upto(f"ln{k}", i))
                    A(ch(buf, i), ch(buf, i), ACT.Exp, scale=-0.5).then_inc(*done(f"rs{k}", i))

            def evict(step, h, dst, func, waits, rows=P, scale=1.0):
                for i in range(NCH):
                    for w in waits:
                        act.wait_ge(*upto(w, i))
                    A(ch(dst, i)[0:rows], half(h, i, rows), func, scale=scale).then_inc(*done(step, i))

            nc.scalar.preload_act_table_set("natural_log_exp_and_others")
            act.wait_ge(vec_loaded, 32)
            A(mtmp[:, 0:2], vec[:, VEC.index("c0"):VEC.index("c1") + 1], ACT.Exp, scale=-1.0).then_inc(*done("c_exp"))
            square("sqA", lambda i: half(0, i), T1, ["centreA"])
            rsqrt("A", 1, T1, col("eps5"), ["varA"])
            square("sqB", lambda i: ch(HLN, i), T2, ["modA"])
            rsqrt("B", 0, T2, col("eps6"), ["msB"])
            act.wait_ge(*upto("normB", NCH - 1))
            evict("r_copy", 1, R, ACT.Copy, ["r"])
            evict("k_copy", 0, K, ACT.Copy, ["k"])
            evict("v_copy", 1, V, ACT.Copy, ["v"])
            nc.scalar.preload_act_table_set("silu_and_others")
            evict("lora_tanh", 0, TA, ACT.Tanh, ["lora_a"], rows=LORA)
            evict("g_silu", 1, G, ACT.Silu, ["g"])
            A(spread_r, C("spread"), ACT.Copy).then_inc(*done("spread_r"))
            for i in range(NCH):
                A(ch(v_parts[:, 0, :], i), ch(V, i), ACT.Copy).then_inc(*done("v_hi", i))
            nc.scalar.preload_act_table_set("natural_log_exp_and_others")
            for i in range(NCH):
                act.wait_ge(*upto("lora_b", i))
                A(ch(DEC, i), half(0, i), ACT.Exp, bias=col("w0")).then_inc(*done("w_exp", i))
                act.wait_ge(*upto("w_exp", i))
                A(ch(DEC, i), ch(DEC, i), ACT.Exp, scale=-1.0).then_inc(*done("decay", i))
            square("gn_sq", lambda i: half(1, i), T1, ["gn_centred"])
            for i in range(NCH):
                act.wait_ge(*upto("gn_var", i))
                A(ch(T1, i), half(0, i), ACT.Ln, bias=col("eps5")).then_inc(*done("gn_ln", i))
                act.wait_ge(*upto("gn_ln", i))
                A(ch(T1, i), ch(T1, i), ACT.Exp, scale=-0.5).then_inc(*done("gn_rs", i))
                act.wait_ge(*upto("gn_rs", i))
                A(ch(T3, i), ch(T1, i), ACT.Square).then_inc(*done("gn_rs2", i))
            square("sqC", lambda i: ch(HLN, i), T2, ["x1"])
            rsqrt("C", 0, T2, col("eps6"), ["msC"])
            nc.scalar.preload_act_table_set("gelu_and_others")
            for i in range(NCH):
                for f in range(NF):
                    act.wait_ge(*upto(f"up{f}", i))
                    if i:
                        act.wait_ge(*upto(f"down{f}", i - 1))
                    A(GEL[:, f, :], bank(4 + f), ACT.Gelu).then_inc(*done(f"gelu{f}", i))
            nc.scalar.preload_act_table_set("natural_log_exp_and_others")

            square("sqD", lambda i: half(1, i), TB, ["centreD"])
            rsqrt("D", 0, TB, col("eps5"), ["varD"])
            act.wait_ge(*upto("r_shift"))
            A(small(1), small(0), ACT.Exp).then_inc(*done("r_exp"))
            for q in range(NCH):
                act.wait_ge(*upto("h_turn", 4 * q + 3))
                A(ch(HT[:, 0, :], q), half(1, q), ACT.Copy).then_inc(*done("h_turned", q))
            A(ONES_R, CB_("ones"), ACT.Copy).then_inc(*done("ones_r"))
            act.wait_ge(*upto("r_kept"))
            for t in range(NT):
                A(DG[:, t * P:(t + 1) * P], CORE_("eye"), ACT.Copy, scale=tiny(9)[:, t:t + 1]).then_inc(*done("slot_diag", t))
            evict("slots", 1, SLB, ACT.Copy, ["slot_spread"])
            act.wait_ge(*upto("r_scale"))
            for t in range(NT):
                A(DG2[:, t * P:(t + 1) * P], CORE_("eye"), ACT.Copy, scale=tiny(4)[:, t:t + 1]).then_inc(*done("scale_diag", t))
            act.wait_ge(*upto("dispatch", NT - 1))
            A(BUF[:, 0:N], bank(0), ACT.Copy).then_inc(*done("buf0"))

            def e_relu(e):
                act.wait_ge(*upto("e_up", e))
                if e >= 2:
                    act.wait_ge(*upto("e_down", e - 2))
                for f in range(NF):
                    last = A(HS[:, e % 2, f, :], bank(6 + e % 2)[:, f * P:(f + 1) * P], ACT.Relu, bias=expert_b1(e, f))
                last.then_inc(*done("e_relu", e))

            e_relu(1)
            for e in range(E0):
                act.wait_ge(*upto("e_down", e))
                A(YB[:, 0, e, :], bank(2 + e % 2)[:, 0:P], ACT.Copy).then_inc(*done("y_hi", e))
                if e + 2 < E0 and e % 2:
                    e_relu(e + 2)
                if e < NCH:
                    act.wait_ge(*upto("scale_spread", e))
                    A(ch(SCB, e), bank(4 + e % 2), ACT.Copy, scale=modcol(0, GB)).then_inc(*done("scales", e))

            square("sqE", lambda i: half(1, i), TE, ["centreE"])
            rsqrt("E", 0, TE, col("eps5"), ["varE"])
            nc.scalar.preload_act_table_set("silu_and_others")
            for c in range(DI):
                for i in range(NCH):
                    act.wait_ge(*upto(f"xb{c}", i))
                    A(XBP[:, c, i * N + 3:(i + 1) * N + 3], half(1 - c, i), ACT.Copy).then_inc(*done(f"xb{c}_copy", i))
            act.wait_ge(*upto("x_moe", NCH - 1))
            for c in range(DI):
                evict(f"z{c}_silu", 1 - c, Z[:, c, :], ACT.Silu, [f"z{c}"])
            def proj_out(i):
                act.wait_ge(*upto("bc", i))
                A(ch(BC, i), half(1, i, BC3), ACT.Copy).then_inc(*done("bc_hi", i))
                A(ch(DRAW, i)[BC3:BC3 + DTR], ps[BC3:BC3 + DTR, (4 + i) * N:(5 + i) * N], ACT.Copy).then_inc(*done("dt_raw_copy", i))
                act.wait_ge(*upto("gate0", i))
                A(ch(DTG[:, 0, :], i), half(0, i), ACT.Tanh, scale=0.5).then_inc(*done("gate0_tanh", i))

            for i in range(NCH):
                for c in range(DI):
                    act.wait_ge(*upto(f"conv{c}_{KC - 1}", i))
                    A(ch(U[:, c, :], i), ch(CV[:, c, :], i), ACT.Silu).then_inc(*done(f"u{c}", i))
                if i:
                    proj_out(i - 1)
            proj_out(NCH - 1)
            for i in range(NCH):
                act.wait_ge(*upto("bc_r1", i))
                A(ch(BC, i)[0:64], ch(R1, i)[0:64], ACT.Copy).then_inc(*done("bc_mid", i))
            evict("gate1_tanh", 1, DTG[:, 1, :], ACT.Tanh, ["gate1"], scale=0.5)
            nc.scalar.preload_act_table_set("natural_log_exp_and_others")
            a0 = VEC.index("A0_0")
            A(ABASE[:], vec[:, a0:a0 + DI * NS], ACT.Exp).then_inc(*done("a_exp"))

            def sp_ln(i):
                for c in range(DI):
                    act.wait_ge(*upto(f"sp_w_{c}", i))
                    A(ch(SPL[:, c, :], i), ch(SPW[:, c, :], i), ACT.Ln).then_inc(*done(f"sp_ln_{c}", i))

            for i in range(NCH):
                for c in range(DI):
                    act.wait_ge(*upto(f"dt{c}", i))
                    A(ch(SPE[:, c, :], i), half(c, i), ACT.Abs, bias=col(f"dt_b{c}")).then_inc(*done(f"sp_abs_{c}", i))
                    act.wait_ge(*upto(f"sp_abs_{c}", i))
                    A(ch(SPE[:, c, :], i), ch(SPE[:, c, :], i), ACT.Exp, scale=-1.0).then_inc(*done(f"sp_e_{c}", i))
                    A(ch(SPR[:, c, :], i), half(c, i), ACT.Relu, bias=col(f"dt_b{c}")).then_inc(*done(f"sp_relu_{c}", i))
                    act.wait_ge(*upto(f"sp_e_{c}", i))
                    A(ch(SPW[:, c, :], i), ch(SPE[:, c, :], i), ACT.Identity, bias=1.0).then_inc(*done(f"sp_w_{c}", i))
                if i:
                    sp_ln(i - 1)
            sp_ln(NCH - 1)
            act.wait_ge(*upto("a_neg"))
            act.wait_ge(*upto("bc_lo", NCH - 1))
            act.wait_ge(*upto("dt1", NCH - 1))
            for q in range(NQ):
                i, n = divmod(q, NS)
                act.wait_ge(*upto(f"c{n}", i))
                if q >= C_RING:
                    act.wait_ge(*turn("sc{}_1", q - C_RING))
                A(CBR[:, q % C_RING, :], bank(6 + q % 2), ACT.Copy).then_inc(*done(f"c_copy{n}", i))
                for c in range(DI):
                    if q >= DEC_RING // DI:
                        act.wait_ge(*turn(f"st{{}}_{c}", q - DEC_RING // DI))
                    if n == 0:
                        act.wait_ge(*upto(f"dtg_{c}", i))
                    A(DECR[:, (2 * q + c) % DEC_RING, :], ch(DTG[:, c, :], i), ACT.Exp,
                      scale=ABASE[:, c * NS + n:c * NS + n + 1]).then_inc(*done(f"dec{n}_{c}", i))

            square("sqF", lambda i: half(0, i), TF, ["centreF"])
            rsqrt("F", 1, TF, col("eps5"), ["varF"])
            act.wait_ge(*upto("g_router"))
            A(gsmall(0), ps[:, 0:NT * E1], ACT.Exp, scale=-1.0).then_inc(*done("g_exp"))
            nc.scalar.preload_act_table_set("silu_and_others")
            for k in range(WD_PARTS):
                act.wait_ge(wd_loaded[k], 16)
                A(w_parts[:, 0, wd_part(k), :], wD[:, wd_part(k), :], ACT.Copy).then_inc(*done("w_hi", k))
            for i in range(NCH):
                act.wait_ge(*upto("modF", i))
                A(ch(x_parts[:, 0, :], i), ch(HD, i), ACT.Copy).then_inc(*done("x_hi", i))
            for j in range(2):
                act.wait_ge(*upto("g_turn", 8 * j + 7))
                A(BC[:, j * 2 * N:(j + 1) * 2 * N], ps[0:96, 2 * N:4 * N].bitcast(bf16)[:, j * 2 * N:(j + 1) * 2 * N], ACT.Copy).then_inc(*done("g_turned", j))

            def h_hi(q):
                i, e = divmod(q, E1 + 1)
                act.wait_ge(*upto(f"hw{e}" if e < E1 else f"hh{e}", i))
                if q >= 4:
                    act.wait_ge(*expert("hd{}", q - 4))
                A(HWP[:, 0, q % 4, :], (HW if e < E1 else HH)[:, q % 2, :], ACT.Copy).then_inc(*done(f"h_hi{e}", i))

            for q in range(TURNS):
                i, e = divmod(q, E1 + 1)
                act.wait_ge(*upto(f"hg{e}", i))
                if q >= 2:
                    act.wait_ge(*expert("hh{}", q - 2))
                A(SG[:, q % 2, :], bank(q % 2), ACT.Silu).then_inc(*done(f"silu{e}", i))
                if q:
                    h_hi(q - 1)
            h_hi(TURNS - 1)

        @block.vector
        def _(dve):
            tt, ts, stt = nc.vector.tensor_tensor, nc.vector.tensor_scalar, nc.vector.scalar_tensor_tensor
            red = nc.vector.tensor_reduce

            def skip(i):
                for c in range(DI):
                    dve.wait_ge(*upto(f"y{NS - 1}_{c}", i))
                    stt(ch(U[:, c, :], i), ch(U[:, c, :], i), col(f"D{c}"), bank(c + 2 * (i % 2)), ALU.mult, ALU.add).then_inc(*done(f"skip_{c}", i))

            dve.wait_ge(*upto("c_exp"))
            ts(mtmp[:, 2:4], mtmp[:, 0:2], 1.0, None, ALU.add).then_inc(*done("c_one"))
            dve.wait_ge(*upto("c_one"))
            nc.vector.reciprocal(mtmp[:, 0:2], mtmp[:, 2:4]).then_inc(*done("c_recip"))
            dve.wait_ge(*upto("c_recip"))
            tt(mtmp[:, 4:6], mtmp[:, 0:2], vec[:, VEC.index("c0"):VEC.index("c1") + 1], ALU.mult).then_inc(*done("c_silu"))
            dve.wait_ge(*upto("mod"))
            nc.vector.tensor_copy(mod[:], ps[:, 7 * N:7 * N + 12]).then_inc(*done("mod_copy"))
            dve.wait_ge(*upto("mod_copy"))
            m3 = mod[:].rearrange("p (k s) -> p k s", s=3)
            g3 = mtmp[:, 8:12]
            a3 = mtmp[:, 12:16]
            s3 = mtmp[:, 16:20]
            ts(m3[:, :, 1], m3[:, :, 1], 1.0, None, ALU.add).then_inc(*done("mod_ca"))
            ts(g3, m3[:, :, 2], 0.0, None, ALU.is_ge).then_inc(*done("mod_sign"))
            dve.wait_ge(*upto("mod_sign"))
            ts(s3, g3, 2.0, -1.0, ALU.mult, ALU.add).then_inc(*done("mod_sign2"))
            stt(a3, m3[:, :, 2], -1.0, m3[:, :, 2], ALU.mult, ALU.max).then_inc(*done("mod_abs"))
            dve.wait_ge(*upto("mod_abs"))
            ts(a3, a3, GATE_FLOOR, None, ALU.max).then_inc(*done("mod_floor"))
            dve.wait_ge(*upto("mod_floor"))
            tt(m3[:, :, 2], s3, a3, ALU.mult).then_inc(*done("mod_gate"))
            dve.wait_ge(*upto("mod_gate"))

            def norm(k, h, dst, buf, layer, scale, shift, waits=()):
                for i in range(NCH):
                    dve.wait_ge(*upto(f"rs{k}", i))
                    for w in waits:
                        dve.wait_ge(*upto(w, i))
                    tt(ch(dst, i), half(h, i), ch(buf, i), ALU.mult).then_inc(*done(f"norm{k}", i))
                    dve.wait_ge(*upto(f"norm{k}", i))
                    ts(ch(dst, i), ch(dst, i), modcol(layer, scale), modcol(layer, shift), ALU.mult, ALU.add).then_inc(*done(f"mod{k}", i))

            norm("A", 0, HLN, T1, 0, CA, SA)
            dve.wait_ge(*upto("h1_zero"))
            for i in range(NCH):
                dve.wait_ge(*upto("rsB", i))
                stt(ch(H1, i, 1), ch(HLN, i), col("ln1_w"), ch(T2, i), ALU.mult, ALU.mult).then_inc(*done("normB", i))
            for i in range(NCH):
                dve.wait_ge(*upto("normB", i))
                tt(ch(XX, i), ch(H1, i), ch(H1, i, 1), ALU.subtract).then_inc(*done("xx", i))

            def mix(step, mu, dst, waits):
                for i in range(NCH):
                    dve.wait_ge(*upto("xx", i))
                    for w in waits:
                        dve.wait_ge(*upto(w, i))
                    stt(ch(dst, i), ch(XX, i), col(mu), ch(H1, i, 1), ALU.mult, ALU.add).then_inc(*done(step, i))

            mix("mix_r", "mu_r", M0, [])
            dve.wait_ge(*upto("mod"))
            mix("mix_k", "mu_k", M1, [])
            mix("mix_v", "mu_v", M2, [])
            mix("mix_w", "mu_w", M0, ["r"])
            mix("mix_g", "mu_g", M1, ["k"])
            for i in range(NCH):
                dve.wait_ge(*upto("k_copy", i))
                dve.wait_ge(*upto("mix_g", i))
                stt(ch(XX, i), ch(R, i), col("u"), ch(K, i), ALU.mult, ALU.mult).then_inc(*done("ruk", i))
            for i in range(NCH):
                dve.wait_ge(*upto("head_ruk", i))
                tt(ch(BONUS, i), half(1, i), ch(V, i), ALU.mult).then_inc(*done("bonus", i))
            nc.vector.memset(S[:, :, 0:1], 0.0).then_inc(*done("s_zero"))
            dve.wait_ge(*upto("s_zero"))

            def kv(q):
                i, v = q // DK, ORDER[q % DK]
                dve.wait_ge(*upto(f"spread{v}", i))
                if q >= 4:
                    dve.wait_ge(*column("scan{}", q - 4))
                tt(KV[:, q % 4, :], bank(4 + q % 4), ch(K, i), ALU.mult).then_inc(*done(f"kv{v}", i))

            def o(i):
                dve.wait_ge(*upto(f"reduce{ORDER[-1]}", i))
                tt(ch(O, i), bank(i % 2), ch(BONUS, i), ALU.add).then_inc(*done("o", i))

            kv(0)
            for q in range(NR):
                i, v = q // DK, ORDER[q % DK]
                if q + 1 < NR:
                    kv(q + 1)
                if q % DK == 0:
                    dve.wait_ge(*upto("decay", i))
                dve.wait_ge(*upto(f"kv{v}", i))
                nc.vector.tensor_tensor_scan(S[:, v, i * N + 1:(i + 1) * N + 1], ch(DEC, i), KV[:, q % 4, :],
                                             S[:, v, i * N:i * N + 1], ALU.mult, ALU.add).then_inc(*done(f"scan{v}", i))
                if i and q % DK == DK - 1:
                    o(i - 1)
            o(NCH - 1)
            for i in range(NCH):
                dve.wait_ge(*upto("gn_rs2", i))
                stt(ch(T3, i), half(0, i), EPS_GN, ch(T3, i), ALU.add, ALU.mult).then_inc(*done("gn_err", i))
                dve.wait_ge(*upto("gn_err", i))
                ts(ch(T3, i), ch(T3, i), -0.5, 1.5, ALU.mult, ALU.add).then_inc(*done("gn_half", i))
                dve.wait_ge(*upto("gn_half", i))
                tt(ch(T1, i), ch(T1, i), ch(T3, i), ALU.mult).then_inc(*done("gn_rsqrt", i))
                dve.wait_ge(*upto("gn_rsqrt", i))
                tt(ch(O, i), half(1, i), ch(T1, i), ALU.mult).then_inc(*done("gn_norm", i))
                dve.wait_ge(*upto("gn_norm", i))
                ts(ch(O, i), ch(O, i), col("gn_w"), col("gn_b"), ALU.mult, ALU.add).then_inc(*done("gn_affine", i))
                dve.wait_ge(*upto("gn_affine", i))
                tt(ch(O, i), ch(O, i), ch(G, i), ALU.mult).then_inc(*done("gn_gate", i))
            for i in range(NCH):
                dve.wait_ge(*upto("wo", i))
                tt(ch(HLN, i), half(1, i), ch(HLN, i), ALU.add).then_inc(*done("x1", i))
            for i in range(NCH):
                dve.wait_ge(*upto("rsC", i))
                stt(ch(M0, i), ch(HLN, i), col("ln2_w"), ch(T2, i), ALU.mult, ALU.mult).then_inc(*done("normC", i))
            for i in range(NCH):
                dve.wait_ge(*upto("down3", i))
                tt(ch(HLN, i), half(0, i), ch(HLN, i), ALU.add).then_inc(*done("ffn_sum", i))
                dve.wait_ge(*upto("ffn_sum", i))
                stt(ch(X, i), ch(HLN, i), modcol(0, GA), ch(X, i), ALU.mult, ALU.add).then_inc(*done("x_attn", i))

            norm("D", 1, HB, TB, 0, CB, SB_)
            steps = iter(R_STEPS)
            state = {"last": None}

            def step(op, *args, **kw):
                name = next(state["names"])
                if state["last"]:
                    dve.wait_ge(*upto(state["last"]))
                for w in kw.pop("waits", []):
                    dve.wait_ge(*upto(*w))
                op(*args, **kw).then_inc(*done(name))
                state["last"] = name

            L_, E_, PR_, OH_, RK_, CU_, TO_ = (small3(k) for k in (0, 1, 2, 3, 4, 5, 6))
            flat = small
            MX, SM, RC, PM, SC, BEST, POS, KEEP, BASE, SLOT = (tiny(k) for k in (0, 1, 2, 3, 4, 5, 6, 7, 8, 9))
            state["names"] = steps
            dve.wait_ge(wb_loaded, 48)
            step(tt, flat(0), ps[:, 0:NT * E0], CB_("b_switch"), ALU.add, waits=[("router",)])
            step(red, MX, L_, AX, ALU.max)
            step(tt, L_, L_, bcast(MX, E0), ALU.subtract)
            step(red, SM, E_, AX, ALU.add, waits=[("r_exp",)])
            step(nc.vector.reciprocal, RC, SM)
            step(tt, PR_, E_, bcast(RC, E0), ALU.mult)
            step(red, PM, PR_, AX, ALU.max)
            step(tt, RK_, PR_, bcast(PM, E0), ALU.is_equal)
            step(tt, flat(4), flat(4), CB_("rank"), ALU.mult)
            step(red, BEST, RK_, AX, ALU.max)
            step(tt, OH_, CB_("rank").rearrange("p (t e) -> p t e", e=E0), bcast(BEST, E0), ALU.is_equal)
            step(nc.vector.reciprocal, RC, PM)
            step(tt, SC, PM, RC, ALU.mult)
            step(nc.vector.tensor_copy, TO_.rearrange("p t e -> p (t e)").rearrange("p (e t) -> p e t", e=E0),
                 bank(2)[:, 0:P].rearrange("p (t e) -> p e t", e=E0), waits=[("totals",)])
            step(nc.vector.tensor_tensor_scan, flat(5), CB_("seg"), flat(6), 0.0, ALU.mult, ALU.add)
            step(tt, flat(5), flat(5), flat(6), ALU.subtract)
            step(tt, RK_, bank(1)[:, 0:P].rearrange("p (t e) -> p t e", e=E0), flat(5).rearrange("p (e t) -> p t e", e=E0), ALU.add)
            step(tt, RK_, RK_, OH_, ALU.mult)
            step(red, POS, RK_, AX, ALU.add)
            step(ts, KEEP, POS, float(CAP), None, ALU.is_le)
            step(ts, BASE, BEST, -float(CAP), float(E0 * CAP), ALU.mult, ALU.add)
            step(tt, SLOT, BASE, POS, ALU.add)
            step(tt, SLOT, SLOT, KEEP, ALU.mult)
            dve.wait_ge(*upto("r_kept"))
            for t in range(NT):
                if t % 4 == 0:
                    i = t // 4
                    dve.wait_ge(*upto("h_turned", i))
                    tt(ch(HT[:, 1, :], i), half(1, i), ch(HT[:, 0, :], i).bitcast(f32), ALU.subtract).then_inc(*done("h_turned_lo", i))
                if t >= 2:
                    dve.wait_ge(*upto("dispatch", t - 2))
                ts(OH1[:, t % 2, :], CB_("iota"), SLOT[:, t:t + 1], None, ALU.is_equal).then_inc(*done("onehot", t))
            dve.wait_ge(*upto("dispatch", NT - 1))
            nc.vector.tensor_copy(BUF[:, N:2 * N], bank(3)).then_inc(*done("buf1"))

            def e_relu(e):
                dve.wait_ge(*upto("e_up", e))
                if e >= 2:
                    dve.wait_ge(*upto("e_down", e - 2))
                for f in range(NF):
                    last = ts(HS[:, e % 2, f, :], bank(6 + e % 2)[:, f * P:(f + 1) * P], expert_b1(e, f), 0.0, ALU.add, ALU.max)
                last.then_inc(*done("e_relu", e))

            def place(e, i):
                dve.wait_ge(*upto("slots", i))
                if i >= 2:
                    dve.wait_ge(*upto(f"combine{e}", i - 2))
                ts(PTS[i % 2][:, e, :], ch(SLB, i), CB_("iota_p")[:, e:e + 1], None, ALU.is_equal).then_inc(*done(f"place{e}", i))

            e_relu(0)
            for e in range(E0):
                for j in range(2):
                    place((2 * e + j) % E0, (2 * e + j) // E0)
                dve.wait_ge(*upto("y_hi", e))
                tt(YB[:, 1, e, :], bank(2 + e % 2)[:, 0:P], YB[:, 0, e, :].bitcast(f32), ALU.subtract).then_inc(*done("y_lo", e))
                if e + 2 < E0 and e % 2 == 0:
                    e_relu(e + 2)
                if e < NCH:
                    stt(ch(HB, e), ch(SLB, e), 0.5, ch(HB, e), ALU.is_lt, ALU.mult).then_inc(*done("kept_x", e))
            for i in range(NCH):
                dve.wait_ge(*upto("kept_x", i))
                dve.wait_ge(*upto(f"combine{E0 - 1}", i))
                tt(ch(HB, i), half(0, i), ch(HB, i), ALU.add).then_inc(*done("moe_sum", i))
                dve.wait_ge(*upto("moe_sum", i))
                dve.wait_ge(*upto("scales", i))
                tt(ch(HB, i), ch(HB, i), ch(SCB, i), ALU.mult).then_inc(*done("moe_scaled", i))
                if i + 2 < NCH:
                    for e in range(E0):
                        place(e, i + 2)

            norm("E", 1, HC, TE, 1, CA, SA)
            nc.vector.memset(XBP[:, :, 0:3], 0.0).then_inc(*done("xb_zero"))
            dve.wait_ge(*upto("xb_zero"))
            def bc_r1(i):
                dve.wait_ge(*upto("bc_hi", i))
                tt(ch(R1, i)[0:BC3], half(1, i, BC3), ch(BC, i), ALU.subtract).then_inc(*done("bc_r1", i))

            for i in range(NCH):
                for c in range(DI):
                    dve.wait_ge(*upto(f"xb{c}_copy", i))
                    for j in range(KC):
                        src = XBP[:, c, i * N + j:(i + 1) * N + j]
                        if j == 0:
                            ts(ch(CV[:, c, :], i), src, col(f"cw{c}_0"), col(f"cb{c}"), ALU.mult, ALU.add).then_inc(*done(f"conv{c}_0", i))
                        else:
                            dve.wait_ge(*upto(f"conv{c}_{j - 1}", i))
                            stt(ch(CV[:, c, :], i), src, col(f"cw{c}_{j}"), ch(CV[:, c, :], i), ALU.mult, ALU.add).then_inc(*done(f"conv{c}_{j}", i))
                if i:
                    bc_r1(i - 1)
            bc_r1(NCH - 1)
            dve.wait_ge(*upto("a_exp"))
            ts(ABASE[:], ABASE[:], -0.5, None, ALU.mult).then_inc(*done("a_neg"))
            nc.vector.memset(CARRY[:], 0.0).then_inc(*done("st_zero"))

            def dt_of(i):
                for c in range(DI):
                    dve.wait_ge(*upto(f"sp_ln_{c}", i))
                    dve.wait_ge(*upto(f"sp_r_{c}", i))
                    tt(ch(SPL[:, c, :], i), ch(SPL[:, c, :], i), ch(SPX[:, c, :], i), ALU.subtract).then_inc(*done(f"sp_log_{c}", i))
                for c in range(DI):
                    dve.wait_ge(*upto(f"sp_log_{c}", i))
                    stt(ch(SPL[:, c, :], i), ch(SPE[:, c, :], i), E_SMALL, ch(SPL[:, c, :], i), ALU.is_gt, ALU.mult).then_inc(*done(f"sp_mask_{c}", i))
                for c in range(DI):
                    dve.wait_ge(*upto(f"sp_mask_{c}", i))
                    dve.wait_ge(*upto(f"sp_lo_{c}", i))
                    tt(ch(SPL[:, c, :], i), ch(SPL[:, c, :], i), ch(DU[:, c, :], i), ALU.max).then_inc(*done(f"sp_max_{c}", i))
                for c in range(DI):
                    dve.wait_ge(*upto(f"sp_relu_{c}", i))
                    dve.wait_ge(*upto(f"sp_max_{c}", i))
                    tt(ch(SPR[:, c, :], i), ch(SPR[:, c, :], i), ch(SPL[:, c, :], i), ALU.add).then_inc(*done(f"dt_{c}", i))
                for c in range(DI):
                    dve.wait_ge(*upto(f"dt_{c}", i))
                    stt(ch(DTG[:, c, :], i), ch(DTG[:, c, :], i), 2.0, ch(SPR[:, c, :], i), ALU.add, ALU.mult).then_inc(*done(f"dtg_{c}", i))

            for i in range(NCH):
                for c in range(DI):
                    dve.wait_ge(*upto(f"sp_w_{c}", i))
                    stt(ch(SPX[:, c, :], i), ch(SPW[:, c, :], i), -1.0, ch(SPE[:, c, :], i), ALU.add, ALU.subtract).then_inc(*done(f"sp_r_{c}", i))
                if i:
                    dt_of(i - 1)
            dt_of(NCH - 1)

            def dbu(q):
                i, n = divmod(q, NS)
                for c in range(DI):
                    dve.wait_ge(*upto(f"b{n}", i))
                    if n == 0:
                        dve.wait_ge(*upto(f"du_{c}", i))
                    if q >= DBU_RING // DI:
                        dve.wait_ge(*turn(f"st{{}}_{c}", q - DBU_RING // DI))
                    tt(DBU[:, (2 * q + c) % DBU_RING, :], bank(4 + q % 2), ch(DU[:, c, :], i), ALU.mult).then_inc(*done(f"dbu{n}_{c}", i))

            dbu(0)
            for q in range(NQ):
                i, n = divmod(q, NS)
                if q + 1 < NQ:
                    dbu(q + 1)
                if q == 0:
                    dve.wait_ge(*upto("du_1", NCH - 1))
                for c in range(DI):
                    k = 2 * n + c
                    dve.wait_ge(*upto(f"dec{n}_{c}", i))
                    dve.wait_ge(*upto(f"dbu{n}_{c}", i))
                    if i:
                        dve.wait_ge(*upto(f"sc{n}_{c}", i - 1))
                    first = ST[:, k, N - 1:N] if i else CARRY[:]
                    nc.vector.tensor_tensor_scan(ST[:, k, :], DECR[:, (2 * q + c) % DEC_RING, :], DBU[:, (2 * q + c) % DBU_RING, :], first,
                                                 ALU.mult, ALU.add).then_inc(*done(f"st{n}_{c}", i))
                if i and n == LAG:
                    skip(i - 1)
            skip(NCH - 1)
            for i in range(NCH):
                dve.wait_ge(*upto("m_out", i))
                stt(ch(X, i), half(1, i), modcol(1, GA), ch(X, i), ALU.mult, ALU.add).then_inc(*done("x_mamba", i))

            norm("F", 0, HD, TF, 1, CB, SB_)
            state["names"], state["last"] = iter(G_STEPS), None
            g, g3 = gsmall, gsmall3
            M8 = area(2 * T + 6 * N + 12 * 256, NT * 8).rearrange("p (t k) -> p t k", k=8)
            THR = M8[:, :, 7]
            NG, LEFT, TOT, INV = (gtiny(k) for k in range(4))
            step(ts, g(1), g(0), 1.0, None, ALU.add, waits=[("g_exp",)])
            step(nc.vector.reciprocal, g(2), g(1))
            step(tt, g(3), g(2), WC_("g_bias"), ALU.add)
            for t in range(NT):
                step(nc.vector.max, M8[:, t, :], g3(3)[:, t, :])
            step(tt, g3(4), g3(3), bcast(THR, E1), ALU.is_gt)
            step(tt, g3(5), g3(3), bcast(THR, E1), ALU.is_equal)
            step(red, NG, g3(4), AX, ALU.add)
            step(ts, LEFT, NG, -1.0, float(TOPK), ALU.mult, ALU.add)
            step(nc.vector.tensor_tensor_scan, g(6), WC_("g_seg"), g(5), 0.0, ALU.mult, ALU.add)
            step(tt, g3(6), g3(6), bcast(LEFT, E1), ALU.is_le)
            step(tt, g(6), g(6), g(5), ALU.mult)
            step(tt, g(6), g(6), g(4), ALU.add)
            step(tt, g(6), g(6), g(2), ALU.mult)
            step(red, TOT, g3(6), AX, ALU.add)
            step(nc.vector.reciprocal, INV, TOT)
            step(stt, g3(7), g3(6), ROUTE_SCALE, bcast(INV, E1), ALU.mult, ALU.mult)
            step(nc.vector.memset, CS, 0.0)
            step(nc.vector.tensor_copy, CS[:, :, 0:E1], g3(7))
            step(tt, g3(8), g3(7), CS[:, :, 0:E1], ALU.subtract)
            step(nc.vector.tensor_copy, CS[:, :, 32:32 + E1], g3(8))
            step(tt, CS[:, :, 64:64 + E1], g3(8), CS[:, :, 32:32 + E1], ALU.subtract)
            def x_out(i):
                dve.wait_ge(*upto(f"hd{E1}", i))
                stt(ch(X, i), bank(6 + i % 2), modcol(1, GB), ch(X, i), ALU.mult, ALU.add).then_inc(*done("x_out", i))

            for q in range(TURNS):
                i, e = divmod(q, E1 + 1)
                k = q % 2
                dve.wait_ge(*upto(f"silu{e}", i))
                dve.wait_ge(*upto(f"hu{e}", i))
                if q >= 2:
                    dve.wait_ge(*expert("h_lo{}", q - 2))
                tt(HH[:, k, :], bank(2 + k), SG[:, k, :], ALU.mult).then_inc(*done(f"hh{e}", i))
                if e < E1:
                    dve.wait_ge(*upto(f"hh{e}", i))
                    dve.wait_ge(*upto(f"w{e}", i))
                    tt(HW[:, k, :], bank(4 + k), HH[:, k, :], ALU.mult).then_inc(*done(f"hw{e}", i))
                if i and e == LAG_E + 1:
                    x_out(i - 1)
            x_out(NCH - 1)

        @block.gpsimd
        def _(pool):
            mul = lambda o, a, b: nc.gpsimd.tensor_tensor(o, a, b, ALU.mult)
            nc.gpsimd.memset(H1[:, 0:1], 0.0).then_inc(*done("h1_zero"))
            for i in range(NCH):
                pool.wait_ge(*upto("v_hi", i))
                nc.gpsimd.tensor_tensor(ch(v_parts[:, 1, :], i), ch(V, i), ch(v_parts[:, 0, :], i).bitcast(f32), ALU.subtract).then_inc(*done("v_lo", i))
            for q in range(NR):
                i, v = q // DK, ORDER[q % DK]
                pool.wait_ge(*upto(f"scan{v}", i))
                if q >= 8:
                    pool.wait_ge(*column("reduce{}", q - 8))
                mul(PR[:, q % 8, :], S[:, v, i * N:(i + 1) * N], ch(R, i)).then_inc(*done(f"prod{v}", i))
            for i in range(NCH):
                pool.wait_ge(*upto("moe_scaled", i))
                nc.gpsimd.tensor_tensor(ch(X, i), ch(HB, i), ch(X, i), ALU.add).then_inc(*done("x_moe", i))
            for i in range(NCH):
                pool.wait_ge(*upto("bc_mid", i))
                nc.gpsimd.tensor_tensor(ch(BC, i)[0:32], ch(R1, i)[0:32], ch(BC, i)[0:32], ALU.subtract).then_inc(*done("bc_lo", i))

            def du(i):
                for c in range(DI):
                    pool.wait_ge(*upto(f"dt_{c}", i))
                    mul(ch(DU[:, c, :], i), ch(U[:, c, :], i), ch(SPR[:, c, :], i)).then_inc(*done(f"du_{c}", i))

            for i in range(NCH):
                for c in range(DI):
                    pool.wait_ge(*upto(f"sp_e_{c}", i))
                    nc.gpsimd.tensor_scalar(ch(DU[:, c, :], i), ch(SPE[:, c, :], i), -0.5, 1.0, ALU.mult, ALU.add).then_inc(*done(f"sp_p_{c}", i))
                    pool.wait_ge(*upto(f"sp_p_{c}", i))
                    mul(ch(DU[:, c, :], i), ch(DU[:, c, :], i), ch(SPE[:, c, :], i)).then_inc(*done(f"sp_lo_{c}", i))
                if i:
                    du(i - 1)
            du(NCH - 1)

            def gated(i):
                for c in range(DI):
                    pool.wait_ge(*upto(f"skip_{c}", i))
                    mul(ch(U[:, c, :], i), ch(U[:, c, :], i), ch(Z[:, c, :], i)).then_inc(*done(f"gated_{c}", i))

            for q in range(NQ):
                i, n = divmod(q, NS)
                for c in range(DI):
                    pool.wait_ge(*upto(f"st{n}_{c}", i))
                    pool.wait_ge(*upto(f"c_copy{n}", i))
                    if q >= LAG:
                        pool.wait_ge(*turn(f"y{{}}_{c}", q - LAG))
                    mul(PRC[:, (2 * q + c) % PR_RING, :], ST[:, 2 * n + c, :], CBR[:, q % C_RING, :]).then_inc(*done(f"sc{n}_{c}", i))
                if i and n == LAG:
                    gated(i - 1)
            gated(NCH - 1)

            for k in range(WD_PARTS):
                pool.wait_ge(*upto("w_hi", k))
                nc.gpsimd.tensor_tensor(w_parts[:, 1, wd_part(k), :], wD[:, wd_part(k), :], w_parts[:, 0, wd_part(k), :].bitcast(f32),
                                        ALU.subtract).then_inc(*done("w_lo", k))
            for i in range(NCH):
                pool.wait_ge(*upto("x_hi", i))
                nc.gpsimd.tensor_tensor(ch(x_parts[:, 1, :], i), ch(HD, i), ch(x_parts[:, 0, :], i).bitcast(f32), ALU.subtract).then_inc(*done("x_lo", i))
            for q in range(TURNS):
                i, e = divmod(q, E1 + 1)
                pool.wait_ge(*upto(f"h_hi{e}", i))
                if q >= 4:
                    pool.wait_ge(*expert("hd{}", q - 4))
                nc.gpsimd.tensor_tensor(HWP[:, 1, q % 4, :], (HW if e < E1 else HH)[:, q % 2, :], HWP[:, 0, q % 4, :].bitcast(f32),
                                        ALU.subtract).then_inc(*done(f"h_lo{e}", i))
        assert not any(order.values()), {k: v[:3] for k, v in order.items()}


def kernel(**inputs):
    import numpy as np
    import concourse.bacc as bacc
    from concourse.bass_utils import run_bass_kernel_spmd

    a = {k: np.asarray(v) for k, v in inputs.items()}

    def by_value(w, axis):
        s = w.shape
        return np.moveaxis(w.reshape(s[:axis] + (H, DK) + s[axis + 1:]), axis, axis + 1).reshape(s)

    L0 = {k[8:]: v for k, v in a.items() if k.startswith("L0_attn_")}
    vecs = dict(L0, u=L0["u"].reshape(-1), gn_w=by_value(L0["gn_w"].reshape(-1), 0), gn_b=by_value(L0["gn_b"].reshape(-1), 0),
                c0=a["L0_c"][0], c1=a["L1_c"][0], eps5=np.full(P, 1e-5, np.float32), eps6=np.full(P, 1e-6, np.float32))
    x = np.ascontiguousarray(L0["x"][0].T)
    w = dict(L0, Wv=by_value(L0["Wv"], 1), Wg=by_value(L0["Wg"], 1), Wo=by_value(L0["Wo"], 0),
             wB=np.concatenate([L0["wB"], L0["wB"]]), w1=L0["ffn_w1"],
             w2=L0["ffn_w2"].reshape(NF, P, P).transpose(1, 0, 2).reshape(P, F))
    wA = np.concatenate([w[n] for n in WA], 1)
    wmod = np.stack([a["L0_wmod"], a["L1_wmod"]], 1)
    F0 = {k[7:]: v for k, v in a.items() if k.startswith("L0_ffn_")}
    M = {k[8:]: v for k, v in a.items() if k.startswith("L1_attn_")}
    F1 = {k[7:]: v for k, v in a.items() if k.startswith("L1_ffn_")}
    w1B = F0["w1"].transpose(1, 0, 2)
    w2B = F0["w2"].reshape(E0, NF, P, P).transpose(2, 0, 1, 3).reshape(P, E0, NF, P)
    xp = M["x_proj_w"].T.reshape(DI, P, -1)
    dt_c, bc_c, gate_c = xp[:, :, :DTR], xp[:, :, DTR:DTR + 2 * NS], xp[:, :, DTR + 2 * NS:]
    xp = np.concatenate([gate_c, bc_c, bc_c, bc_c, dt_c], 2).transpose(1, 0, 2).reshape(P, -1)
    dtp = np.zeros((P, DI * P), np.float32)
    dtp[BC3:BC3 + DTR] = M["dt_proj_w"].T
    wc = {"in": M["in_proj_w"].T, "xp": xp, "dtp": dtp, "out": M["out_proj_w"].T.reshape(DI, P, P).transpose(1, 0, 2).reshape(P, -1),
          "gate": F1["gate_w"].T, "g_bias": np.broadcast_to(np.tile(F1["expert_bias"], NT), (P, NT * E1)),
          "g_seg": np.broadcast_to(np.tile(np.arange(E1) > 0, NT), (P, NT * E1)).astype(np.float32)}
    wC = np.concatenate([wc[n] for n in WC], 1)
    shared = [F1["shared_gate_w"][None], F1["shared_up_w"][None], F1["shared_down_w"][None]]
    wD = np.stack([np.concatenate([F1[n], sh]) for n, sh in zip(["w_gate", "w_up", "w_down"], shared)], 1)
    wD = wD.transpose(3, 0, 1, 2).reshape(P, 3 * (E1 + 1), P)
    for c in range(DI):
        part = slice(c * P, (c + 1) * P)
        vecs.update({f"dt_b{c}": M["dt_proj_b"][part], f"D{c}": M["D_param"][part], f"cb{c}": M["conv_b"][part]})
        vecs.update({f"cw{c}_{j}": M["conv_w"][part, 0, j] for j in range(KC)})
        vecs.update({f"A{c}_{n}": M["A_log"][part, n] for n in range(NS)})
    vec = np.stack([vecs[n] for n in VEC], 1)

    eye = np.eye(P, dtype=np.float32)
    head_k = np.arange(P) // DK
    head_v = np.arange(P) % H
    gn_mean = (head_v[:, None] == head_v[None]).astype(np.float32) / DK
    reduce = np.zeros((P, 2, 32), np.float32)
    spread = np.zeros((P, DK, P), np.float32)
    for b in range(2):
        reduce[:, b, b * H:(b + 1) * H] = head_k[:, None] == np.arange(H)[None]
    for v in range(DK):
        spread[v * H:(v + 1) * H, v] = np.arange(H)[:, None] == head_k[None]
    c = {"head_sum": head_k[:, None] == head_v[None],
         "gn_mean": gn_mean, "gn_centre": eye - gn_mean, "reduce": reduce.reshape(P, -1), "spread": spread.reshape(P, -1)}
    cst = np.concatenate([c[n].astype(np.float32) for n in CST], 1)
    c = {"centre": eye - 1.0 / P, "mean": np.full((P, P), 1.0 / P), "eye": eye}
    core = np.concatenate([c[n].astype(np.float32) for n in CORE], 1)
    row = lambda v: np.broadcast_to(np.asarray(v, np.float32).reshape(1, -1), (P, np.size(v)))
    experts = np.arange(E0)
    slots = 1 + np.arange(P)[:, None] + CAP * experts[None]
    c = {"iota": row(1 + np.arange(E0 * CAP)), "tri": np.triu(np.ones((P, P))), "ones": np.ones((P, P)),
         "rank": row(np.tile(E0 - experts, NT)), "seg": row(np.tile(np.arange(NT) > 0, E0)), 
         "iota_p": slots, "b_switch": row(np.tile(F0["b_switch"], NT)), "w_switch": F0["w_switch"],
         "b1": F0["b1"].reshape(E0, NF, P).transpose(2, 0, 1).reshape(P, -1), "b2": row(F0["b2"].reshape(-1))}
    cstB = np.concatenate([c[n].astype(np.float32) for n in CSTB], 1)
    bf = mybir.dt.np(mybir.dt.bfloat16)
    sel = np.zeros((3, 2 * NS, 2 * NS, P), np.float32)
    sel[:, np.arange(2 * NS), np.arange(2 * NS)] = 1
    sel = sel.reshape(96, 2 * NS, P).astype(bf)

    nc = bacc.Bacc("TRN2", target_bir_lowering=False, num_devices=1)
    arrays = {"x": x, "vec": vec, "core": core, "cst": cst, "wA": wA, "wmod": wmod, "cstB": cstB, "wB1": w1B, "wB2": w2B, "wC": wC,
              "sel": sel, "eyeb": eye.astype(bf), "wD": wD}
    aps = []
    for name, v in arrays.items():
        arrays[name] = v = np.ascontiguousarray(v)
        aps.append(nc.dram_tensor(f"in_{name}", v.shape, mybir.dt.from_np(v.dtype), kind="ExternalInput").ap())
    o = nc.dram_tensor("out_x", (P, T), mybir.dt.float32, kind="ExternalOutput").ap()
    build(nc, *aps, o)
    r = run_bass_kernel_spmd(nc, [{f"in_{k}": v for k, v in arrays.items()}], core_ids=[0])
    return np.ascontiguousarray(r.results[0]["out_x"].T)[None]
```

```python
from contextlib import ExitStack

import concourse.bass as bass
from concourse import mybir

P = 128
T = 2048
N = 512
NCH = T // N
WD_AT = 38600
ARENA_W = WD_AT + 3 * 17 * P
NT = T // P
H, DK = 16, 8
LORA = 64
F = 512
NF = F // P
E0 = 8
CAP = int(0.5 * T / E0)
EPS_LN, EPS_RMS, EPS_GN = 1e-5, 1e-6, 1e-5
GATE_FLOOR = 0.25

NS = 16
DI = 2
KC = 4
DTR = 8
E1, TOPK = 16, 8
NQ = NCH * NS
E_SMALL = 1e-3
TURNS = NCH * (E1 + 1)
LAG = 4
SIDE = {"pe": {10: ["m_out"], 13: ["centreF"], 15: ["varF"], 18: ["g_router"]},
        "act": {14: ["sqF"], 16: ["lnF", "rsF"], 19: ["g_exp", "x_hi"]},
        "dve": {4: ["skip_0", "skip_1"], 10: ["x_mamba"], 15: ["normF", "modF"]},
        "pool": {5: ["gated_0", "gated_1"]}}
ALL_TURNS = NQ + max(max(side) for side in SIDE.values()) + 1


def side_steps(engine, q):
    return [(q - (i + 1) * NS, i) for i in range(NCH) if q - (i + 1) * NS in SIDE[engine]]


LAG_E = 2
WD_PARTS = 4
C_RING, DEC_RING, DBU_RING, PR_RING = 4, 4, 6, 2 * LAG
ROUTE_SCALE = 2.826
VEC = ["ln1_w", "mu_r", "mu_k", "mu_v", "mu_w", "mu_g", "w0", "u", "gn_w", "gn_b", "ln2_w",
       "c0", "c1", "eps5", "eps6",
       "dt_b0", "dt_b1", "D0", "D1", "cb0", "cb1"] + [f"cw{c}_{j}" for c in range(DI) for j in range(KC)] + \
    [f"A{c}_{n}" for c in range(DI) for n in range(NS)]
CORE = {"centre": P, "mean": P, "eye": P}
CST = {"head_sum": P, "gn_mean": P, "gn_centre": P, "reduce": 2 * 32, "spread": DK * P}
CSTB = {"iota": E0 * CAP, "tri": P, "ones": P, "rank": NT * E0, "seg": NT * E0, "iota_p": E0, "b_switch": NT * E0,
        "w_switch": E0, "b1": E0 * NF, "b2": E0 * P}
WC = {"in": 2 * DI * P, "xp": DI * (DI * P + 3 * 2 * NS + DTR), "dtp": DI * P, "out": DI * P, "gate": E1, "g_bias": NT * E1, "g_seg": NT * E1}
BC3 = 3 * 2 * NS
XPW = DI * P + 3 * 2 * NS + DTR
WA = {"Wr": P, "Wk": P, "Wv": P, "Wg": P, "Wo": P, "wA": LORA, "wB": P, "w1": F, "w2": F}


def columns(widths):
    at, out = 0, {}
    for name, w in widths.items():
        out[name] = (at, w)
        at += w
    return out, at


def each_chunk(*steps):
    return [(s, i) for i in range(NCH) for s in steps]


def layernorm(k):
    return ([(f"centre{k}", i) for i in range(NCH)] + [(f"var{k}", i) for i in range(NCH)],
            [(f"sq{k}", i) for i in range(NCH)] + each_chunk(f"ln{k}", f"rs{k}"),
            each_chunk(f"norm{k}", f"mod{k}"))


def rmsnorm(k):
    return (each_chunk(f"ms{k}"), [(f"sq{k}", i) for i in range(NCH)] + each_chunk(f"ln{k}", f"rs{k}"),
            each_chunk(f"norm{k}"))


ORDER = [0, 2, 4, 6, 1, 3, 5, 7]
NR = NCH * DK
LAG_R = 9


def one(*steps):
    return [(s, 0) for s in steps]


def sequences():
    pe, act, dve, pool = [], [], [], []
    engines = {"pe": pe, "act": act, "dve": dve, "pool": pool}

    def add(to, *parts):
        for part in parts:
            to.extend(part)

    ln_pe, ln_act, ln_dve = layernorm("A")
    rm_pe, rm_act, rm_dve = rmsnorm("B")
    add(pe, ln_pe[:-1], one("mod"), ln_pe[-1:], rm_pe, *(each_chunk(s) for s in ["r", "k", "v", "lora_a", "g", "lora_b", "head_ruk"]))
    add(act, one("c_exp"), ln_act, rm_act, *(each_chunk(s) for s in ["r_copy", "k_copy", "v_copy", "lora_tanh", "g_silu"]), one("spread_r"), each_chunk("v_hi"),
        each_chunk("w_exp", "decay"))
    add(dve, one("c_one", "c_recip", "c_silu", "mod_copy", "mod_ca", "mod_sign", "mod_sign2", "mod_abs", "mod_floor", "mod_gate"),
        ln_dve, rm_dve, *(each_chunk(s) for s in ["xx", "mix_r", "mix_k", "mix_v", "mix_w", "mix_g", "ruk", "bonus"]), one("s_zero"))
    add(pool, one("h1_zero"))
    add(pool, each_chunk("v_lo"))
    dve.append(("kv0", 0))
    for q in range(NR + LAG_R - 1):
        i, k = divmod(q, DK)
        if q < NR:
            pe.append((f"spread{ORDER[k]}", i))
            if q + 1 < NR:
                dve.append((f"kv{ORDER[(q + 1) % DK]}", (q + 1) // DK))
            dve.append((f"scan{ORDER[k]}", i))
            pool.append((f"prod{ORDER[k]}", i))
            if i and k == DK - 1:
                dve.append(("o", i - 1))
        if q >= LAG_R and (q - LAG_R) % 4 == 0:
            pe += [(f"reduce{ORDER[(q - LAG_R + j) % DK]}", (q - LAG_R) // DK) for j in range(4)]
    dve.append(("o", NCH - 1))
    rm_pe, rm_act, rm_dve = rmsnorm("C")
    add(pool, one("f_w_hi", "f_w_lo"), each_chunk("gn_gate"))
    add(pe, each_chunk("gn_centred"), each_chunk("gn_var"), each_chunk("wo"), rm_pe)
    add(act, each_chunk("gn_sq"), 
        *([(s, i) for s in ("gn_ln", "gn_rs", "gn_rs2")] + ([("gn_affine", i - 1)] if i else []) for i in range(NCH)), [("gn_affine", NCH - 1)], rm_act[:4], *([("lnC", i), ("rsC", i)] + ([("f_x_hi", i - 1)] if i else []) for i in range(NCH)), [("f_x_hi", NCH - 1)])
    add(dve, each_chunk("gn_err", "gn_half", "gn_rsqrt", "gn_norm"), each_chunk("x1"), rm_dve)
    add(pool, each_chunk("f_x_lo"))
    ln_pe, ln_act, ln_dve = layernorm("D")
    for i in range(NCH + 1):
        if i < NCH:
            pe += [(f"up{f}", i) for f in range(NF)]
            act += [(s, i) for s in ("gelu0", "gelu1", "f_hi0", "gelu2", "f_hi1", "gelu3", "f_hi2", "f_hi3")]
            pool += [("f_lo0", i), ("f_lo2", i)]
            dve += [("f_lo1", i), ("f_lo3", i)]
        if i:
            pe += [(f"down{f}", i - 1) for f in range(NF)]
            dve += [("ffn_sum", i - 1), ("x_attn", i - 1)]
        if i >= 2:
            pe.append(("centreD", i - 2))
    add(pe, [("varD", 0), ("varD", 1), ("centreD", NCH - 1), ("varD", 2), ("varD", 3)])

    add(pe, one("router"), [("h_turn", t) for t in range(NT)], one("prefix", "totals"),
        [("dispatch", t) for t in range(SPREAD_AT)], each_chunk("slot_spread"), [("dispatch", t) for t in range(SPREAD_AT, NT)], [("e_up", 0), ("e_up", 1)])
    add(act, ln_act, one("r_exp"), [("h_turned", q) for q in range(NCH)], one("ones_r"),
        [("slot_diag", t) for t in range(NT)], [("scale_diag", t) for t in range(NT)], each_chunk("slots"), one("buf0"), [("e_relu", 1)])
    add(dve, ln_dve, one(*R_STEPS), *([("h_turned_lo", i)] + [("onehot", 4 * i + j) for j in range(4)] for i in range(NCH)), one("buf1"),
        [("e_relu", 0)])
    for e in range(E0):
        pe += [("e_down", e)] + ([("e_up", e + 2)] if e + 2 < E0 else []) + ([("scale_spread", e)] if e < NCH else [])
        act += [("y_hi", e)] + ([("e_relu", e + 2)] if e + 2 < E0 and e % 2 else []) + ([("scales", e)] if e < NCH else [])
        dve += [(f"place{(2 * e + j) % E0}", (2 * e + j) // E0) for j in range(2)] + \
            [("y_lo", e)] + ([("e_relu", e + 2)] if e + 2 < E0 and e % 2 == 0 else []) + ([("kept_x", e)] if e < NCH else [])
    for i in range(NCH):
        pe += [(f"combine{e}", i) for e in range(E0)]
        dve += [("moe_sum", i), ("moe_scaled", i)] + [(f"place{e}", i + 2) for e in range(E0) if i + 2 < NCH]
        pool.append(("x_moe", i))

    ln_pe, ln_act, ln_dve = layernorm("E")
    add(pe, ln_pe, *(each_chunk(s) for s in ["xb0", "xb1"]),
        *([("bc", i), ("gate0", i)] + [(s, i - 1) for s in ("gate1", "dt0", "dt1") if i] for i in range(NCH)),
        [(s, NCH - 1) for s in ("gate1", "dt0", "dt1")], each_chunk("z0", "z1"))
    add(act, ln_act, *(each_chunk(s) for s in ["xb0_copy", "xb1_copy"]))
    add(dve, ln_dve, one("xb_zero"))
    add(pool, one("xp_hi", "xp_lo"))
    for i in range(NCH + 1):
        if i < NCH:
            dve += [(f"conv{c}_{j}", i) for c in range(DI) for j in range(KC)]
            pool += [("u_lo0", i), ("u_lo1", i)]
        if i:
            act += [(s, i - 1) for s in ("bc_hi", "dt_raw_copy")]
            dve.append(("bc_r1", i - 1))
            pool.append(("bc_lo", i - 1))
        if i < NCH:
            act += [("u0", i), ("u_hi0", i), ("u1", i), ("u_hi1", i)]
        if i:
            act += [("gate0_tanh", i - 1), ("bc_mid", i - 1)]
        if i >= 2:
            act.append(("gate1_tanh", i - 2))
        if i >= 3:
            act += [(f"{s}_{c}", i - 3) for c in range(DI) for s in ("sp_abs", "sp_relu")]
    act.append(("gate1_tanh", NCH - 1))
    add(act, one("a_exp"))
    add(dve, one("a_neg", "st_zero"))
    for i in range(NCH):
        if i >= NCH - 2:
            act += [(f"{s}_{c}", i) for c in range(DI) for s in ("sp_abs", "sp_relu")]
        act += [(f"{s}_{c}", i) for s in ("sp_e", "sp_w", "sp_ln") for c in range(DI)]
        dve += [(f"{s}_{c}", i) for s in ("sp_r", "sp_log", "sp_mask", "sp_max", "dt", "dtg") for c in range(DI)]
        pool += [(f"{s}_{c}", i) for c in range(DI) for s in ("sp_p", "sp_lo")]
        pool += [(f"du_{c}", i - 1) for c in range(DI) if i]
    act += each_chunk("z0_silu", "z1_silu")
    pool += [(f"du_{c}", NCH - 1) for c in range(DI)]
    dve += [("dbu0", 0)]
    for q in range(ALL_TURNS):
        i, n = divmod(q, NS)
        if q < NQ:
            act += [(f"c_copy{n}", i), (f"dec{n}_0", i), (f"dec{n}_1", i)]
            pe += [(f"b{n}", i), (f"c{n}", i)]
        if LAG <= q < NQ + LAG:
            m = (q - LAG) % NS
            pe += [(f"y{m}_0", (q - LAG) // NS), (f"y{m}_1", (q - LAG) // NS)]
        if q + 1 < NQ:
            dve += [(f"dbu{(q + 1) % NS}", (q + 1) // NS)]
        if q < NQ:
            dve += [(f"st{n}_0", i), (f"st{n}_1", i)]
            pool += [(f"sc{n}_0", i), (f"sc{n}_1", i)]
        for engine, to in engines.items():
            for d, j in side_steps(engine, q):
                to.extend((step, j) for step in SIDE[engine][d])

    add(act, [("w_hi", k) for k in range(WD_PARTS)])
    add(dve, one(*G_STEPS))
    pool += [("x_lo", 0)] + [("w_lo", k) for k in range(WD_PARTS)] + [("x_lo", i) for i in range(1, NCH)]
    for q in range(TURNS + LAG_E):
        i, e = divmod(q, E1 + 1)
        if q < TURNS:
            pe += [(f"hg{e}", i), (f"hu{e}", i)]
            if q == 1:
                pe += [("g_turn", t) for t in range(NT)] + [("w0", 0)]
            if q and e < E1:
                pe.append((f"w{e}", i))
            act.append((f"silu{e}", i))
            if q == 1:
                act += [("g_turned", h) for h in range(2)]
            dve += [(f"hh{e}", i)] + ([(f"hw{e}", i)] if e < E1 else [])
            pool.append((f"h_lo{e}", i))
        if 1 <= q <= TURNS:
            act.append((f"h_hi{(q - 1) % (E1 + 1)}", (q - 1) // (E1 + 1)))
        if q >= LAG_E:
            pe.append((f"hd{(q - LAG_E) % (E1 + 1)}", (q - LAG_E) // (E1 + 1)))
        if i and e == LAG_E + 1:
            dve.append(("x_out", i - 1))
    dve.append(("x_out", NCH - 1))
    return {"pe": pe, "act": act, "dve": dve, "pool": pool}


SPREAD_AT = NT - 3
R_STEPS = ["r_logit", "r_max", "r_shift", "r_sum", "r_recip", "r_prob", "r_pmax", "r_hit", "r_rank", "r_best", "r_oh",
           "r_precip", "r_scale", "r_tot", "r_cum", "r_off", "r_pos", "r_own", "r_place", "r_keep", "r_base", "r_slot", "r_kept"]
G_STEPS = ["g_one", "g_score", "g_sel"] + [f"g_top{t}" for t in range(NT)] + \
    ["g_gt", "g_eq", "g_ngt", "g_left", "g_cum", "g_le", "g_tie", "g_mask", "g_pick", "g_total", "g_inv", "g_w",
     "g_zero", "g_hi", "g_r1", "g_mid", "g_lo"]


def build(nc, X_in, vec_in, core_in, cst_in, wA_in, wmod_in, cstB_in, wB1_in, wB2_in, wC_in, sel_in, eyeb_in, wD_in, out):
    f32 = mybir.dt.float32
    bf16 = mybir.dt.bfloat16
    f32r = mybir.dt.float32r
    ALU = mybir.AluOpType
    ACT = mybir.ActivationFunctionType
    AX = mybir.AxisListType.X
    SEQ = sequences()
    count = {step: (e, k + 1) for e, steps in SEQ.items() for k, step in enumerate(steps)}
    assert len(count) == sum(map(len, SEQ.values()))
    core_at, core_n = columns(CORE)
    cst_at, cst_n = columns(CST)
    wa_at, wa_n = columns(WA)
    cb_at, cb_n = columns(CSTB)
    wc_at, wc_n = columns(WC)

    ctx = ExitStack()
    with ctx:
        def sb(name, shape, dt=f32):
            return ctx.enter_context(nc.sbuf_tensor(name, shape, dt))

        def sem(name):
            return ctx.enter_context(nc.semaphore(name))

        vec_loaded, core_loaded, wmod_loaded, cst_loaded, wa_loaded, cstb_loaded, wb_loaded, wc_loaded, out_stored = map(
            sem, ["vec_loaded", "core_loaded", "wmod_loaded", "cst_loaded", "wa_loaded", "cstb_loaded", "wb_loaded", "wc_loaded", "out_stored"])
        x_loaded = [sem(f"x_loaded{i}") for i in range(NCH)]
        wd_loaded = [sem(f"wd_loaded{k}") for k in range(WD_PARTS)]
        finished = {e: sem(f"{e}_done") for e in SEQ}
        order = {e: list(steps) for e, steps in SEQ.items()}

        def upto(step, i=0):
            engine, n = count[step, i]
            return finished[engine], n

        def done(step, i=0):
            engine, n = count[step, i]
            assert order[engine].pop(0) == (step, i), (step, i)
            return finished[engine], 1

        def turn(step, q):
            return upto(step.format(q % NS), q // NS)

        def column(step, q):
            return upto(step.format(ORDER[q % DK]), q // DK)

        def expert(step, q):
            return upto(step.format(q % (E1 + 1)), q // (E1 + 1))

        X = sb("x", [P, T])
        vec = sb("vec", [P, len(VEC)])
        core = sb("core", [P, core_n])
        mod = sb("mod", [P, 12])
        mtmp = sb("mtmp", [P, 24])
        wC = sb("wC", [P, wc_n])
        sel = sb("sel", [96, 2 * NS, P], bf16)
        BC = sb("bc", [96, T], bf16)
        EYEB = sb("eyeb", [P, P], bf16)
        CARRY = sb("carry", [P, 1])
        ABASE = sb("abase", [P, DI * NS])
        with nc.sbuf_tensor("arena", [P, WD_AT], f32) as ARENA:
            pass

        def over_arena(name, at, n, dt):
            assert at + n <= ARENA_W, (name, at + n)
            with nc.sbuf_tensor(f"below_{name}", [P, at], f32), nc.sbuf_tensor(name, [P, n], dt) as t:
                return t[:]

        ps = ctx.enter_context(nc.psum_tensor("ps", [P, 8 * N], f32))

        def col(name):
            k = VEC.index(name)
            return vec[:, k:k + 1]

        def area(at, n):
            return ARENA[:, at:at + n]

        def CORE_(name):
            a, w = core_at[name]
            return core[:, a:a + w]

        def C(name, part=slice(None)):
            a, w = cst_at[name]
            return cst[part, a:a + w]

        def W(name, part=slice(None)):
            a, w = wa_at[name]
            return wA[part, a:a + w]

        def CB_(name):
            a, w = cb_at[name]
            return cstB[:, a:a + w]

        def WC_(name):
            a, w = wc_at[name]
            return wC[:, a:a + w]

        wd_flat = over_arena("wD", WD_AT, 3 * (E1 + 1) * P, f32)
        wD = wd_flat.rearrange("p (k m) -> p k m", k=3 * (E1 + 1))
        SV = T + 1
        S = area(0, DK * SV).rearrange("p (v t) -> p v t", v=DK)
        H1 = area(0, T + 1)
        XX = area(1 * 2052, T)
        M0 = area(2 * 2052, T)
        M1 = area(3 * 2052, T)
        at = DK * SV
        HLN, M2, K, R, DEC, V, G = (area(at + j * T, T) for j in range(7))
        at += 7 * T
        PR = area(at, 8 * N).rearrange("p (s t) -> p s t", s=8)
        KV = wd_flat[:, 2 * T:2 * T + 4 * N].rearrange("p (s t) -> p s t", s=4)
        v_parts = over_arena("v_parts", WD_AT, 2 * T, f32r).rearrange("p (s t) -> p s t", s=2)
        TA = area(at + 4 * N, T)
        T1, T2, T3 = K, R, DEC
        O = BONUS = M2
        GEL = PR[:, 0:NF]
        f_w_parts = over_arena("f_w_parts", WD_AT, 2 * 2 * F, f32r).rearrange("p (s k) -> p s k", s=2)
        f_x_parts = over_arena("f_x_parts", WD_AT + 4 * F, 2 * T, f32r).rearrange("p (s t) -> p s t", s=2)
        f_parts = [over_arena(f"f_parts{s_}", at_, NF * N, f32r).rearrange("p (f t) -> p f t", f=NF)
                   for s_, at_ in enumerate((at + 4 * N, 2 * 2052 + T))]
        at += 8 * N
        wA = area(at, wa_n)
        cst = area(at + wa_n, cst_n)
        spread_r = over_arena("spread_r", at + wa_n + cst_at["spread"][0], DK * P, f32r)
        assert at + wa_n + cst_n <= WD_AT, at + wa_n + cst_n
        wmod = area(4 * 2052, 2 * 6 * P).rearrange("p (l k) -> p l k", l=2)

        cstB = area(0, cb_n)
        assert cb_n <= 2780
        place_at = (4100, WD_AT - E0 * N - 104)
        PTS = [over_arena(f"place{k}", at_k, E0 * N, f32r).rearrange("p (e t) -> p e t", e=E0) for k, at_k in enumerate(place_at)]
        WB = area(8200, 8192)
        w1B = WB[:, 0:4096].rearrange("p (e f) -> p e f", e=E0)
        w2B = WB[:, 4096:8192].rearrange("p (e f m) -> p e f m", e=E0, f=NF)
        TB, HB, SLB, SCB = DEC, V, M2, K
        DG = over_arena("slot_diags", DK * SV + 3 * T, T, f32r)
        HT = over_arena("h_turned", WD_AT, 2 * T, f32r).rearrange("p (s t) -> p s t", s=2)
        OH1 = over_arena("onehot", WD_AT + 2 * T, T, f32r).rearrange("p (s c) -> p s c", s=2)
        YB = over_arena("y", WD_AT, 2 * E0 * P, f32r).rearrange("p (s e m) -> p s e m", s=2, e=E0)
        ONES_R = over_arena("ones_r", place_at[1] - 300, P, f32r)
        DG2 = HLN
        at = DK * SV + 7 * T
        BUF = area(at, E0 * CAP)
        HS = area(at + 1024, 2 * N).rearrange("p (s f t) -> p s f t", s=2, f=NF)
        small = lambda k: area(2780 + k * P, P)
        small3 = lambda k: small(k).rearrange("p (t e) -> p t e", e=E0)
        tiny = lambda k: area(at + 3072 + k * NT, NT)

        ST = area(0, 32 * N).rearrange("p (k t) -> p k t", k=32)
        te_at, xbp_at, wide_at = 8184, 12296, 16400
        assert te_at + 2 * T <= xbp_at + P and xbp_at + DI * (T + 3) <= wide_at
        TE = area(te_at, T)
        HC = area(te_at + T, T)
        XBP = area(xbp_at, DI * (T + 3)).rearrange("p (c t) -> p c t", c=DI)
        CV = area(0, DI * T).rearrange("p (c t) -> p c t", c=DI)
        at = wide_at
        U, Z, DTG, DU = (area(at + j * DI * T, DI * T).rearrange("p (c t) -> p c t", c=DI) for j in range(4))
        at += 4 * DI * T
        ring = lambda buf, s: buf.rearrange("p (s t) -> p s t", s=s)
        CBR = ring(area(at, C_RING * N), C_RING)
        DBU = ring(area(at + C_RING * N, DBU_RING * N), DBU_RING)
        assert at + (C_RING + DBU_RING) * N <= WD_AT
        DECR = ring(wd_flat[:, 0:DEC_RING * N], DEC_RING)
        PRC = ring(wd_flat[:, DEC_RING * N:(DEC_RING + PR_RING) * N], PR_RING)
        u_parts = [over_arena(f"u_parts{k}", at_, DI * T, f32r).rearrange("p (c t) -> p c t", c=DI)
                   for k, at_ in enumerate((wide_at + 3 * DI * T, DI * T))]
        xp_parts = over_arena("xp_parts", at + 2 * T, 2 * DI * XPW, f32r).rearrange("p (s k) -> p s k", s=2)
        assert at + 2 * T + 2 * DI * XPW <= WD_AT
        SPX = wd_flat[:, 0:DI * T].rearrange("p (c t) -> p c t", c=DI)
        R1 = area(at, T)
        DRAW = area(at + T, T)
        SPE, SPR, SPL = (area(j * DI * T, DI * T).rearrange("p (c t) -> p c t", c=DI) for j in (0, 1, 3))
        SPW = Z

        HD, TF = Z[:, 0, :], Z[:, 1, :]
        x_parts = over_arena("x_parts", wide_at, 2 * T, f32r).rearrange("p (s t) -> p s t", s=2)
        w_parts = over_arena("w_parts", N, 2 * 3 * (E1 + 1) * P, f32r).rearrange("p (s k m) -> p s k m", s=2, k=3 * (E1 + 1))
        at = 16400 + 2 * DI * T
        HWP = over_arena("h_parts", at, 8 * N, f32r).rearrange("p (s r t) -> p s r t", s=2, r=4)
        at += DI * T
        SG, HH, HW = (ring(area(at + k * 2 * N, 2 * N), 2) for k in range(3))
        at += 6 * N
        wd_part = lambda k: slice(k * 3 * (E1 + 1) // WD_PARTS, (k + 1) * 3 * (E1 + 1) // WD_PARTS)
        part_of = lambda k: next(j for j in range(WD_PARTS) if k < wd_part(j).stop)
        gsmall = lambda k, at=at: area(at + k * 256, 256) if k else TF[:, 0:NT * E1]
        gsmall3 = lambda k: gsmall(k).rearrange("p (t e) -> p t e", e=E1)
        gtiny = lambda k, at=at: area(at + 16 * 256 + k * NT, NT)
        CS = area(at + 17 * 256, NT * 96 // 2).bitcast(bf16).rearrange("p (t r) -> p t r", t=NT)

        def ch(buf, i, off=0):
            return buf[:, i * N + off:(i + 1) * N + off]

        def half(h, i, rows=P):
            return ps[0:rows, (4 * h + i) * N:(4 * h + i + 1) * N]

        def bank(b, lo=0, hi=P):
            return ps[lo:hi, b * N:(b + 1) * N]

        modcol = lambda layer, k: mod[:, 6 * layer + k:6 * layer + k + 1]
        SA, CA, GA, SB_, CB, GB = range(6)

        block = ctx.enter_context(nc.Block())

        def bcast(col2, e):
            return col2.unsqueeze(2).to_broadcast([P, col2.shape[1], e])

        def expert_b1(e, f):
            a = cb_at["b1"][0] + e * NF + f
            return cstB[:, a:a + 1]

        @block.sync
        def _(sp):
            sp.dma_start(core[:], core_in).then_inc(core_loaded, 16)
            for i in range(NCH):
                sp.dma_start(ch(X, i), ch(X_in, i)).then_inc(x_loaded[i], 16)
                if i == 0:
                    sp.dma_start(vec[:], vec_in).then_inc(vec_loaded, 16)
            sp.dma_start(wmod, wmod_in).then_inc(wmod_loaded, 16)
            sp.dma_start(cst, cst_in).then_inc(cst_loaded, 16)
            sp.dma_start(wA, wA_in).then_inc(wa_loaded, 16)
            sp.dma_start(wC[:], wC_in).then_inc(wc_loaded, 16)
            sp.dma_start(EYEB[:], eyeb_in).then_inc(wc_loaded, 16)
            sp.dma_start(sel[:], sel_in).then_inc(wc_loaded, 16)
            sp.wait_ge(*upto("prod7", NCH - 1))
            sp.wait_ge(*upto("o", NCH - 1))
            sp.dma_start(cstB, cstB_in).then_inc(cstb_loaded, 16)
            sp.dma_start(w1B, wB1_in).then_inc(wb_loaded, 16)
            sp.dma_start(w2B, wB2_in).then_inc(wb_loaded, 16)
            sp.wait_ge(*upto(f"y{NS - 1}_1", NCH - 1))
            for k in range(WD_PARTS):
                sp.dma_start(wD[:, wd_part(k), :], wD_in[:, wd_part(k), :]).then_inc(wd_loaded[k], 16)
            for i in range(NCH):
                sp.wait_ge(*upto("x_out", i))
                sp.dma_start(out[:, i * N:(i + 1) * N], X[:, i * N:(i + 1) * N]).then_inc(out_stored, 16)
            sp.wait_ge(out_stored, 16 * NCH)

        @block.tensor
        def _(pe):
            mm = nc.tensor.matmul

            def sweep(step, lhsT, rhs, h, waits, rows=P, parts=P):
                for i in range(NCH):
                    for w in waits:
                        pe.wait_ge(*upto(w, i))
                    mm(half(h, i, rows), lhsT, ch(rhs, i)[0:parts], start=True, stop=True).then_inc(*done(step, i))

            pe.wait_ge(core_loaded, 16)
            for i in range(NCH):
                pe.wait_ge(x_loaded[i], 16)
                mm(half(0, i), CORE_("centre"), ch(X, i), start=True, stop=True).then_inc(*done("centreA", i))
            for i in range(NCH - 1):
                pe.wait_ge(*upto("sqA", i))
                mm(half(1, i), CORE_("mean"), ch(T1, i), start=True, stop=True).then_inc(*done("varA", i))
            pe.wait_ge(wmod_loaded, 16)
            pe.wait_ge(*upto("c_silu"))
            for layer in range(2):
                for k in range(6):
                    j = 6 * layer + k
                    last = mm(ps[:, 7 * N + j:7 * N + j + 1], wmod[:, layer, k * P:(k + 1) * P],
                              mtmp[:, 4 + layer:5 + layer], start=True, stop=True)
            last.then_inc(*done("mod"))
            pe.wait_ge(*upto("mod_copy"))
            pe.wait_ge(*upto("sqA", NCH - 1))
            mm(half(1, NCH - 1), CORE_("mean"), ch(T1, NCH - 1), start=True, stop=True).then_inc(*done("varA", NCH - 1))
            sweep("msB", CORE_("mean"), T2, 0, ["sqB", "normA"])
            pe.wait_ge(wa_loaded, 16)
            pe.wait_ge(cst_loaded, 16)
            sweep("r", W("Wr"), M0, 1, ["mix_r", "lnA"])
            sweep("k", W("Wk"), M1, 0, ["mix_k", "lnB"])
            sweep("v", W("Wv"), M2, 1, ["mix_v", "r_copy"])
            sweep("lora_a", W("wA"), M0, 0, ["mix_w", "k_copy"], rows=LORA)
            sweep("g", W("Wg"), M1, 1, ["mix_g", "v_copy"])
            sweep("lora_b", W("wB", slice(0, LORA)), TA, 0, ["lora_tanh"], parts=LORA)
            sweep("head_ruk", C("head_sum"), XX, 1, ["ruk", "g_silu"])

            pe.wait_ge(*upto("bonus", NCH - 1))
            pe.wait_ge(*upto("w_exp", NCH - 1))
            pe.wait_ge(*upto("spread_r"))
            for q in range(NR + LAG_R - 1):
                i, v = q // DK, ORDER[q % DK]
                if q < NR:
                    if q >= 4:
                        pe.wait_ge(*column("kv{}", q - 4))
                    for part, ready in enumerate(("v_hi", "v_lo")):
                        pe.wait_ge(*upto(ready, i))
                        last = mm(bank(4 + q % 4), spread_r[:, v * P:(v + 1) * P], ch(v_parts[:, part, :], i), start=(part == 0), stop=(part == 1))
                    last.then_inc(*done(f"spread{v}", i))
                if q >= LAG_R and (q - LAG_R) % 4 == 0:
                    pe.wait_ge(*column("prod{}", q - LAG_R + 3))
                    for r in range(q - LAG_R, q - LAG_R + 4):
                        i, v = r // DK, ORDER[r % DK]
                        if r % DK < 4 and i >= 2:
                            pe.wait_ge(*upto("o", i - 2))
                        a = cst_at["reduce"][0] + (v % 2) * 32
                        j = 32 * (v // 2)
                        mm(bank(i % 2, j, j + 32), cst[:, a:a + 32], PR[:, r % 8, :], start=(r % DK < 4), stop=(r % DK >= 4)).then_inc(*done(f"reduce{v}", i))

            pe.wait_ge(*upto("kv7", NCH - 1))
            sweep("gn_centred", C("gn_centre"), O, 1, ["o"])
            pe.wait_ge(*upto("o", NCH - 1))
            sweep("gn_var", C("gn_mean"), T1, 0, ["gn_sq"])
            sweep("wo", W("Wo"), O, 1, ["gn_gate"])
            sweep("msC", CORE_("mean"), T2, 0, ["sqC", "gn_err"])
            pe.wait_ge(*upto("lnC", NCH - 1))
            pe.wait_ge(*upto("x1", NCH - 1))
            pe.wait_ge(*upto("f_w_lo"))

            def by_parts(out, w, x, x_lo_ready, start=True, stop=True):
                mm(out, w[0], x[0], start=start, stop=False)
                mm(out, w[1], x[0], start=False, stop=False)
                pe.wait_ge(*upto(*x_lo_ready))
                return mm(out, w[0], x[1], start=False, stop=stop)

            def centre_d(i):
                pe.wait_ge(*upto("x_attn", i))
                mm(half(0, i), CORE_("centre"), ch(X, i), start=True, stop=True).then_inc(*done("centreD", i))

            def var_d(i):
                if i == 0:
                    pe.wait_ge(*upto("gelu3", NCH - 1))
                pe.wait_ge(*upto("sqD", i))
                mm(half(1, i), CORE_("mean"), ch(TB, i), start=True, stop=True).then_inc(*done("varD", i))

            for i in range(NCH + 1):
                for f in range(NF) if i < NCH else ():
                    pe.wait_ge(*upto("f_x_hi", i))
                    if i:
                        pe.wait_ge(*upto(f"gelu{f}", i - 1))
                    by_parts(bank(4 + f), [f_w_parts[:, k, f * P:(f + 1) * P] for k in range(2)], [ch(f_x_parts[:, k, :], i) for k in range(2)],
                             ("f_x_lo", i)).then_inc(*done(f"up{f}", i))
                for f in range(NF) if i else ():
                    pe.wait_ge(*upto(f"f_hi{f}", i - 1))
                    by_parts(half(0, i - 1), [f_w_parts[:, k, F + f * P:F + (f + 1) * P] for k in range(2)], [f_parts[k][:, f, :] for k in range(2)],
                             (f"f_lo{f}", i - 1), start=(f == 0), stop=(f == NF - 1)).then_inc(*done(f"down{f}", i - 1))
                if i >= 2:
                    centre_d(i - 2)
            var_d(0)
            var_d(1)
            centre_d(NCH - 1)
            var_d(2)
            var_d(3)

            pe.wait_ge(cstb_loaded, 16)
            for t in range(NT):
                pe.wait_ge(*upto("modD", t // 4))
                last = mm(ps[:, t * E0:(t + 1) * E0], HB[:, t * P:(t + 1) * P], CB_("w_switch"), start=True, stop=True)
            last.then_inc(*done("router"))
            pe.wait_ge(*upto("lnD", NCH - 1))
            for t in range(NT):
                nc.tensor.transpose(ps[:, 4 * N + t * P:4 * N + (t + 1) * P], HB[:, t * P:(t + 1) * P], CORE_("eye")).then_inc(*done("h_turn", t))
            pe.wait_ge(*upto("r_oh"))
            mm(bank(1)[:, 0:P], CB_("tri"), small(3), start=True, stop=True).then_inc(*done("prefix"))
            mm(bank(2)[:, 0:P], CB_("ones"), small(3), start=True, stop=True).then_inc(*done("totals"))
            def slot_spread():
                pe.wait_ge(*upto("ones_r"))
                pe.wait_ge(*upto("h_turned_lo", NCH - 1))
                for i in range(NCH):
                    pe.wait_ge(*upto("slot_diag", 4 * i + 3))
                    mm(half(1, i), ONES_R, ch(DG, i), start=True, stop=True).then_inc(*done("slot_spread", i))

            for t in range(NT):
                if t == SPREAD_AT:
                    slot_spread()
                pe.wait_ge(*upto("onehot", t))
                pe.wait_ge(*upto("h_turned_lo", t // 4))
                for part in range(2):
                    for j in range(2):
                        last = mm(bank(3 * j), HT[:, part, t * P:(t + 1) * P], OH1[:, t % 2, j * N:(j + 1) * N],
                                  start=(t == 0 and part == 0), stop=(t == NT - 1 and part == 1))
                last.then_inc(*done("dispatch", t))
            pe.wait_ge(*upto("buf0"))
            pe.wait_ge(*upto("buf1"))
            pe.wait_ge(wb_loaded, 32)

            def e_up(e):
                for f in range(NF):
                    last = mm(bank(6 + e % 2)[:, f * P:(f + 1) * P], w1B[:, e, f * P:(f + 1) * P], BUF[:, e * CAP:(e + 1) * CAP], start=True, stop=True)
                last.then_inc(*done("e_up", e))

            pe.wait_ge(*upto("slots", NCH - 1))
            e_up(0)
            e_up(1)
            for e in range(E0):
                pe.wait_ge(*upto("e_relu", e))
                if e >= 2:
                    pe.wait_ge(*upto("y_lo", e - 2))
                o = bank(2 + e % 2)[:, 0:P]
                a = cb_at["b2"][0] + e * P
                mm(o, CB_("ones")[0:1, :], cstB[0:1, a:a + P], start=True, stop=False)
                for f in range(NF):
                    last = mm(o, HS[:, e % 2, f, :], w2B[:, e, f, :], start=False, stop=(f == NF - 1))
                last.then_inc(*done("e_down", e))
                if e + 2 < E0:
                    e_up(e + 2)
                if e < NCH:
                    pe.wait_ge(*upto("scale_diag", 4 * e + 3))
                    if e >= 2:
                        pe.wait_ge(*upto("scales", e - 2))
                    mm(bank(4 + e % 2), CB_("ones"), ch(DG2, e), start=True, stop=True).then_inc(*done("scale_spread", e))
            pe.wait_ge(*upto("y_lo", E0 - 1))
            for i in range(NCH):
                for e in range(E0):
                    pe.wait_ge(*upto(f"place{e}", i))
                    for part in range(2):
                        last = mm(half(0, i), YB[:, part, e, :], PTS[i % 2][:, e, :], start=(e == 0 and part == 0), stop=(e == E0 - 1 and part == 1))
                    last.then_inc(*done(f"combine{e}", i))

            sweep("centreE", CORE_("centre"), X, 1, ["x_moe", "scales"])
            sweep("varE", CORE_("mean"), TE, 0, ["sqE", "moe_sum"])
            pe.wait_ge(wc_loaded, 48)
            a = wc_at["in"][0]
            sweep("xb0", wC[:, a:a + P], HC, 1, ["normE", "modE"])
            sweep("xb1", wC[:, a + P:a + 2 * P], HC, 0, ["lnE", "modE"])

            def x_proj(step, h, i, col0, rows, waits):
                for w in waits:
                    pe.wait_ge(*upto(w, i))
                for c in range(DI):
                    b = c * XPW + col0
                    for k, (wp, up) in enumerate(((0, 0), (1, 0), (0, 1))):
                        pe.wait_ge(*upto(("u_hi", "u_lo")[up] + str(c), i))
                        last = mm(half(h, i, rows), xp_parts[:, wp, b:b + rows], ch(u_parts[up][:, c, :], i),
                                  start=(c == 0 and k == 0), stop=(c == DI - 1 and k == 2))
                last.then_inc(*done(step, i))

            def gate1_dt(i):
                x_proj("gate1", 1, i, P, P, ["dt_raw_copy", "bc_r1"])
                a = wc_at["dtp"][0]
                for c, w in enumerate(("gate0_tanh", "gate1_tanh")):
                    pe.wait_ge(*upto(w, i))
                    mm(half(c, i), wC[BC3:BC3 + DTR, a + c * P:a + (c + 1) * P], ch(DRAW, i)[BC3:BC3 + DTR],
                       start=True, stop=True).then_inc(*done(f"dt{c}", i))

            pe.wait_ge(*upto("xp_lo"))
            for i in range(NCH):
                x_proj("bc", 1, i, DI * P, BC3 + DTR, ["xb0_copy"])
                x_proj("gate0", 0, i, 0, P, ["xb1_copy"])
                if i:
                    gate1_dt(i - 1)
            gate1_dt(NCH - 1)
            a = wc_at["in"][0] + DI * P
            for i in range(NCH):
                for c in range(DI):
                    pe.wait_ge(*upto(f"sp_relu_{c}", i))
                    mm(half(c, i), wC[:, a + c * P:a + (c + 1) * P], ch(HC, i), start=True, stop=True).then_inc(*done(f"z{c}", i))

            def y_sum(q):
                i, n = divmod(q, NS)
                for c in range(DI):
                    if n == 0 and i >= 2:
                        pe.wait_ge(*upto("g_exp", i - 2))
                    pe.wait_ge(*upto(f"sc{n}_{c}", i))
                    mm(bank(c + 2 * (i % 2)), CORE_("eye"), PRC[:, (2 * q + c) % PR_RING, :], start=(n == 0), stop=(n == NS - 1)).then_inc(*done(f"y{n}_{c}", i))

            def m_out(i):
                a = wc_at["out"][0]
                for c in range(DI):
                    pe.wait_ge(*upto(f"gated_{c}", i))
                    last = mm(bank(2 * (i % 2)), wC[:, a + c * P:a + (c + 1) * P], ch(U[:, c, :], i), start=(c == 0), stop=(c == DI - 1))
                last.then_inc(*done("m_out", i))

            def centre_f(i):
                pe.wait_ge(*upto("x_mamba", i))
                mm(bank(2 * (i % 2) + 1), CORE_("centre"), ch(X, i), start=True, stop=True).then_inc(*done("centreF", i))

            def var_f(i):
                pe.wait_ge(*upto("sqF", i))
                mm(bank(2 * (i % 2)), CORE_("mean"), ch(TF, i), start=True, stop=True).then_inc(*done("varF", i))

            def g_router(i):
                pe.wait_ge(*upto("modF", i))
                pe.wait_ge(*upto("lnF", i))
                for t in range(NT // NCH):
                    last = mm(bank(2 * (i % 2))[:, t * E1:(t + 1) * E1], HD[:, (4 * i + t) * P:(4 * i + t + 1) * P], WC_("gate"), start=True, stop=True)
                last.then_inc(*done("g_router", i))

            side = dict(zip(SIDE["pe"], (m_out, centre_f, var_f, g_router)))
            pe.wait_ge(*upto("z1_silu", NCH - 1))
            pe.wait_ge(*upto("bc_lo", NCH - 1))
            for q in range(ALL_TURNS):
                i, n = divmod(q, NS)
                for kind, b, last_use, row in (("b", 4, "dbu{}", n), ("c", 6, "c_copy{}", NS + n)) if q < NQ else ():
                    if q >= 2:
                        pe.wait_ge(*turn(last_use, q - 2))
                    mm(bank(b + q % 2), sel[:, row, :], BC[:, i * N:(i + 1) * N], start=True, stop=True).then_inc(*done(f"{kind}{n}", i))
                if LAG <= q < NQ + LAG:
                    y_sum(q - LAG)
                for d, j in side_steps("pe", q):
                    side[d](j)
            pe.wait_ge(*upto(f"dbu{NS - 1}", NCH - 1))
            pe.wait_ge(*upto(f"c_copy{NS - 1}", NCH - 1))
            def product(out, k, x, wait_lo, start=True, stop=True):
                for wp, xp, last in ((0, 0, False), (1, 0, False), (0, 1, True)):
                    if last and wait_lo:
                        pe.wait_ge(*upto(*wait_lo))
                    r = mm(out, w_parts[:, wp, k, :], x[xp], start=start and (wp, xp) == (0, 0), stop=stop and last)
                return r

            def down(q):
                i, e = divmod(q, E1 + 1)
                if e == 0 and i >= 2:
                    pe.wait_ge(*upto("x_out", i - 2))
                pe.wait_ge(*upto(f"h_hi{e}", i))
                product(bank(6 + i % 2), 3 * e + 2, [HWP[:, p, q % 4, :] for p in range(2)], (f"h_lo{e}", i),
                        start=(e == 0), stop=(e == E1)).then_inc(*done(f"hd{e}", i))

            def weight(q):
                i, e = divmod(q, E1 + 1)
                if e < E1:
                    if q >= 2:
                        pe.wait_ge(*expert("hw{}" if (q - 2) % (E1 + 1) < E1 else "hh{}", q - 2))
                    mm(bank(4 + q % 2), sel[:, e, :], BC[:, i * N:(i + 1) * N], start=True, stop=True).then_inc(*done(f"w{e}", i))

            def turn_weights():
                pe.wait_ge(*upto("g_lo"))
                for t in range(NT):
                    o = ps[0:96, 6 * N:8 * N].bitcast(bf16)[:, t * P:(t + 1) * P]
                    nc.tensor.transpose(o, CS[:, t, :], EYEB[:]).then_inc(*done("g_turn", t))
                pe.wait_ge(*upto("g_turned", 1))

            for q in range(TURNS):
                i, e = divmod(q, E1 + 1)
                k = q % 2
                x = [ch(x_parts[:, p, :], i) for p in range(2)]
                pe.wait_ge(*upto("x_lo", i))
                if i == 0:
                    pe.wait_ge(*upto("w_lo", part_of(3 * e + 2)))
                if q >= 2:
                    pe.wait_ge(*expert("silu{}", q - 2))
                product(bank(0 + k), 3 * e, x, None).then_inc(*done(f"hg{e}", i))
                if q >= 2:
                    pe.wait_ge(*expert("hh{}", q - 2))
                product(bank(2 + k), 3 * e + 1, x, None).then_inc(*done(f"hu{e}", i))
                if q == 1:
                    turn_weights()
                    weight(0)
                if q:
                    weight(q)
                if q >= LAG_E:
                    down(q - LAG_E)
            for q in range(TURNS - LAG_E, TURNS):
                down(q)

        @block.scalar
        def _(act):
            A = nc.scalar.activation

            def square_of(step, src, dst, waits, i):
                for w in waits:
                    act.wait_ge(*upto(w, i))
                A(ch(dst, i), src, ACT.Square).then_inc(*done(step, i))

            def square(step, src, dst, waits):
                for i in range(NCH):
                    square_of(step, src(i), dst, waits, i)

            def rsqrt(k, h, buf, eps, waits):
                for i in range(NCH):
                    for w in waits:
                        act.wait_ge(*upto(w, i))
                    A(ch(buf, i), half(h, i), ACT.Ln, bias=eps).then_inc(*done(f"ln{k}", i))
                    act.wait_ge(*upto(f"ln{k}", i))
                    A(ch(buf, i), ch(buf, i), ACT.Exp, scale=-0.5).then_inc(*done(f"rs{k}", i))

            def evict(step, h, dst, func, waits, rows=P, scale=1.0):
                for i in range(NCH):
                    for w in waits:
                        act.wait_ge(*upto(w, i))
                    A(ch(dst, i)[0:rows], half(h, i, rows), func, scale=scale).then_inc(*done(step, i))

            nc.scalar.preload_act_table_set("natural_log_exp_and_others")
            act.wait_ge(vec_loaded, 16)
            A(mtmp[:, 0:2], vec[:, VEC.index("c0"):VEC.index("c1") + 1], ACT.Exp, scale=-1.0).then_inc(*done("c_exp"))
            square("sqA", lambda i: half(0, i), T1, ["centreA"])
            rsqrt("A", 1, T1, col("eps5"), ["varA"])
            square("sqB", lambda i: ch(HLN, i), T2, ["modA"])
            rsqrt("B", 0, T2, col("eps6"), ["msB"])
            act.wait_ge(*upto("normB", NCH - 1))
            evict("r_copy", 1, R, ACT.Copy, ["r"])
            evict("k_copy", 0, K, ACT.Copy, ["k"])
            evict("v_copy", 1, V, ACT.Copy, ["v"])
            nc.scalar.preload_act_table_set("silu_and_others")
            evict("lora_tanh", 0, TA, ACT.Tanh, ["lora_a"], rows=LORA)
            evict("g_silu", 1, G, ACT.Silu, ["g"])
            A(spread_r, C("spread"), ACT.Copy).then_inc(*done("spread_r"))
            for i in range(NCH):
                A(ch(v_parts[:, 0, :], i), ch(V, i), ACT.Copy).then_inc(*done("v_hi", i))
            nc.scalar.preload_act_table_set("natural_log_exp_and_others")
            for i in range(NCH):
                act.wait_ge(*upto("lora_b", i))
                A(ch(DEC, i), half(0, i), ACT.Exp, bias=col("w0")).then_inc(*done("w_exp", i))
                act.wait_ge(*upto("w_exp", i))
                A(ch(DEC, i), ch(DEC, i), ACT.Exp, scale=-1.0).then_inc(*done("decay", i))
            def gn_affine(i):
                act.wait_ge(*upto("gn_norm", i))
                A(ch(O, i), ch(O, i), ACT.Identity, scale=col("gn_w"), bias=col("gn_b")).then_inc(*done("gn_affine", i))

            square("gn_sq", lambda i: half(1, i), T1, ["gn_centred"])
            for i in range(NCH):
                act.wait_ge(*upto("gn_var", i))
                A(ch(T1, i), half(0, i), ACT.Ln, bias=col("eps5")).then_inc(*done("gn_ln", i))
                act.wait_ge(*upto("gn_ln", i))
                A(ch(T1, i), ch(T1, i), ACT.Exp, scale=-0.5).then_inc(*done("gn_rs", i))
                act.wait_ge(*upto("gn_rs", i))
                A(ch(T3, i), ch(T1, i), ACT.Square).then_inc(*done("gn_rs2", i))
                if i:
                    gn_affine(i - 1)
            gn_affine(NCH - 1)
            square("sqC", lambda i: ch(HLN, i), T2, ["x1"])

            def f_x_hi(i):
                act.wait_ge(*upto("normC", i))
                A(ch(f_x_parts[:, 0, :], i), ch(M0, i), ACT.Copy).then_inc(*done("f_x_hi", i))

            for i in range(NCH):
                act.wait_ge(*upto("msC", i))
                A(ch(T2, i), half(0, i), ACT.Ln, bias=col("eps6")).then_inc(*done("lnC", i))
                act.wait_ge(*upto("lnC", i))
                A(ch(T2, i), ch(T2, i), ACT.Exp, scale=-0.5).then_inc(*done("rsC", i))
                if i:
                    f_x_hi(i - 1)
            f_x_hi(NCH - 1)
            nc.scalar.preload_act_table_set("gelu_and_others")

            def gelu(f, i):
                act.wait_ge(*upto(f"up{f}", i))
                if i:
                    act.wait_ge(*upto(f"f_lo{f}", i - 1))
                A(GEL[:, f, :], bank(4 + f), ACT.Gelu).then_inc(*done(f"gelu{f}", i))

            def f_hi(f, i):
                if i:
                    act.wait_ge(*upto(f"down{f}", i - 1))
                act.wait_ge(*upto(f"gelu{f}", i))
                A(f_parts[0][:, f, :], GEL[:, f, :], ACT.Copy).then_inc(*done(f"f_hi{f}", i))

            for i in range(NCH):
                for f in range(NF):
                    gelu(f, i)
                    if f:
                        f_hi(f - 1, i)
                f_hi(NF - 1, i)
            for i in range(2):
                square_of("sqD", half(0, i), TB, ["centreD"], i)
            nc.scalar.preload_act_table_set("natural_log_exp_and_others")

            for i in range(2, NCH):
                square_of("sqD", half(0, i), TB, ["centreD"], i)
            rsqrt("D", 1, TB, col("eps5"), ["varD"])
            act.wait_ge(*upto("r_shift"))
            A(small(1), small(0), ACT.Exp).then_inc(*done("r_exp"))
            for q in range(NCH):
                act.wait_ge(*upto("h_turn", 4 * q + 3))
                A(ch(HT[:, 0, :], q), half(1, q), ACT.Copy).then_inc(*done("h_turned", q))
            A(ONES_R, CB_("ones"), ACT.Copy).then_inc(*done("ones_r"))
            act.wait_ge(*upto("r_kept"))
            for t in range(NT):
                A(DG[:, t * P:(t + 1) * P], CORE_("eye"), ACT.Copy, scale=tiny(9)[:, t:t + 1]).then_inc(*done("slot_diag", t))
            act.wait_ge(*upto("r_scale"))
            for t in range(NT):
                A(DG2[:, t * P:(t + 1) * P], CORE_("eye"), ACT.Copy, scale=tiny(4)[:, t:t + 1]).then_inc(*done("scale_diag", t))
            evict("slots", 1, SLB, ACT.Copy, ["slot_spread"])
            act.wait_ge(*upto("dispatch", NT - 1))
            A(BUF[:, 0:N], bank(0), ACT.Copy).then_inc(*done("buf0"))

            def e_relu(e):
                act.wait_ge(*upto("e_up", e))
                if e >= 2:
                    act.wait_ge(*upto("e_down", e - 2))
                for f in range(NF):
                    last = A(HS[:, e % 2, f, :], bank(6 + e % 2)[:, f * P:(f + 1) * P], ACT.Relu, bias=expert_b1(e, f))
                last.then_inc(*done("e_relu", e))

            e_relu(1)
            for e in range(E0):
                act.wait_ge(*upto("e_down", e))
                A(YB[:, 0, e, :], bank(2 + e % 2)[:, 0:P], ACT.Copy).then_inc(*done("y_hi", e))
                if e + 2 < E0 and e % 2:
                    e_relu(e + 2)
                if e < NCH:
                    act.wait_ge(*upto("scale_spread", e))
                    A(ch(SCB, e), bank(4 + e % 2), ACT.Copy, scale=modcol(0, GB)).then_inc(*done("scales", e))

            square("sqE", lambda i: half(1, i), TE, ["centreE"])
            rsqrt("E", 0, TE, col("eps5"), ["varE"])
            nc.scalar.preload_act_table_set("silu_and_others")
            for c in range(DI):
                for i in range(NCH):
                    act.wait_ge(*upto(f"xb{c}", i))
                    A(XBP[:, c, i * N + 3:(i + 1) * N + 3], half(1 - c, i), ACT.Copy).then_inc(*done(f"xb{c}_copy", i))
            act.wait_ge(*upto("x_moe", NCH - 1))
            def proj_out(i):
                act.wait_ge(*upto("bc", i))
                A(ch(BC, i), half(1, i, BC3), ACT.Copy).then_inc(*done("bc_hi", i))
                A(ch(DRAW, i)[BC3:BC3 + DTR], ps[BC3:BC3 + DTR, (4 + i) * N:(5 + i) * N], ACT.Copy).then_inc(*done("dt_raw_copy", i))

            def u(c, i):
                act.wait_ge(*upto(f"conv{c}_{KC - 1}", i))
                A(ch(U[:, c, :], i), ch(CV[:, c, :], i), ACT.Silu).then_inc(*done(f"u{c}", i))
                act.wait_ge(*upto(f"u{c}", i))
                A(ch(u_parts[0][:, c, :], i), ch(U[:, c, :], i), ACT.Copy).then_inc(*done(f"u_hi{c}", i))

            def bc_mid(i):
                act.wait_ge(*upto("bc_r1", i))
                A(ch(BC, i)[0:64], ch(R1, i)[0:64], ACT.Copy).then_inc(*done("bc_mid", i))

            def gate0_tanh(i):
                act.wait_ge(*upto("gate0", i))
                A(ch(DTG[:, 0, :], i), half(0, i), ACT.Tanh, scale=0.5).then_inc(*done("gate0_tanh", i))

            def gate1_tanh(i):
                act.wait_ge(*upto("gate1", i))
                A(ch(DTG[:, 1, :], i), half(1, i), ACT.Tanh, scale=0.5).then_inc(*done("gate1_tanh", i))

            def sp_abs(i):
                for c in range(DI):
                    act.wait_ge(*upto(f"dt{c}", i))
                    A(ch(SPE[:, c, :], i), half(c, i), ACT.Abs, bias=col(f"dt_b{c}")).then_inc(*done(f"sp_abs_{c}", i))
                    A(ch(SPR[:, c, :], i), half(c, i), ACT.Relu, bias=col(f"dt_b{c}")).then_inc(*done(f"sp_relu_{c}", i))

            for i in range(NCH + 1):
                if i:
                    proj_out(i - 1)
                if i < NCH:
                    u(0, i)
                    u(1, i)
                if i:
                    gate0_tanh(i - 1)
                    bc_mid(i - 1)
                if i >= 2:
                    gate1_tanh(i - 2)
                if i >= 3:
                    sp_abs(i - 3)
            gate1_tanh(NCH - 1)
            nc.scalar.preload_act_table_set("natural_log_exp_and_others")
            a0 = VEC.index("A0_0")
            A(ABASE[:], vec[:, a0:a0 + DI * NS], ACT.Exp).then_inc(*done("a_exp"))

            for i in range(NCH):
                if i >= NCH - 2:
                    sp_abs(i)
                for c in range(DI):
                    act.wait_ge(*upto(f"sp_abs_{c}", i))
                    A(ch(SPE[:, c, :], i), ch(SPE[:, c, :], i), ACT.Exp, scale=-1.0).then_inc(*done(f"sp_e_{c}", i))
                for c in range(DI):
                    act.wait_ge(*upto(f"sp_e_{c}", i))
                    A(ch(SPW[:, c, :], i), ch(SPE[:, c, :], i), ACT.Identity, bias=1.0).then_inc(*done(f"sp_w_{c}", i))
                for c in range(DI):
                    act.wait_ge(*upto(f"sp_w_{c}", i))
                    A(ch(SPL[:, c, :], i), ch(SPW[:, c, :], i), ACT.Ln).then_inc(*done(f"sp_ln_{c}", i))
            nc.scalar.preload_act_table_set("silu_and_others")
            for i in range(NCH):
                for c in range(DI):
                    act.wait_ge(*upto(f"z{c}", i))
                    act.wait_ge(*upto(f"sp_r_{c}", i))
                    act.wait_ge(*upto(f"sp_ln_{c}", i))
                    A(ch(Z[:, c, :], i), half(c, i), ACT.Silu).then_inc(*done(f"z{c}_silu", i))
            nc.scalar.preload_act_table_set("natural_log_exp_and_others")
            def sq_f(i):
                act.wait_ge(*upto("centreF", i))
                A(ch(TF, i), bank(2 * (i % 2) + 1), ACT.Square).then_inc(*done("sqF", i))

            def rs_f(i):
                act.wait_ge(*upto("varF", i))
                A(ch(TF, i), bank(2 * (i % 2)), ACT.Ln, bias=col("eps5")).then_inc(*done("lnF", i))
                act.wait_ge(*upto("lnF", i))
                A(ch(TF, i), ch(TF, i), ACT.Exp, scale=-0.5).then_inc(*done("rsF", i))

            def g_exp(i):
                act.wait_ge(*upto("g_router", i))
                w = NT // NCH * E1
                A(gsmall(0)[:, i * w:(i + 1) * w], bank(2 * (i % 2))[:, 0:w], ACT.Exp, scale=-1.0).then_inc(*done("g_exp", i))
                A(ch(x_parts[:, 0, :], i), ch(HD, i), ACT.Copy).then_inc(*done("x_hi", i))

            side = dict(zip(SIDE["act"], (sq_f, rs_f, g_exp)))
            act.wait_ge(*upto("a_neg"))
            act.wait_ge(*upto("bc_lo", NCH - 1))
            act.wait_ge(*upto("dt1", NCH - 1))
            act.wait_ge(*upto("dtg_1", NCH - 1))
            def decays(q):
                i, n = divmod(q, NS)
                act.wait_ge(*upto(f"c{n}", i))
                if q >= C_RING:
                    act.wait_ge(*turn("sc{}_1", q - C_RING))
                A(CBR[:, q % C_RING, :], bank(6 + q % 2), ACT.Copy).then_inc(*done(f"c_copy{n}", i))
                for c in range(DI):
                    if q >= DEC_RING // DI:
                        act.wait_ge(*turn(f"st{{}}_{c}", q - DEC_RING // DI))
                    if n == 0:
                        act.wait_ge(*upto(f"dtg_{c}", i))
                    A(DECR[:, (2 * q + c) % DEC_RING, :], ch(DTG[:, c, :], i), ACT.Exp,
                      scale=ABASE[:, c * NS + n:c * NS + n + 1]).then_inc(*done(f"dec{n}_{c}", i))

            for q in range(ALL_TURNS):
                if q < NQ:
                    decays(q)
                for d, j in side_steps("act", q):
                    side[d](j)

            nc.scalar.preload_act_table_set("silu_and_others")
            for k in range(WD_PARTS):
                act.wait_ge(wd_loaded[k], 16)
                A(w_parts[:, 0, wd_part(k), :], wD[:, wd_part(k), :], ACT.Copy).then_inc(*done("w_hi", k))
            def h_hi(q):
                i, e = divmod(q, E1 + 1)
                act.wait_ge(*upto(f"hw{e}" if e < E1 else f"hh{e}", i))
                if q >= 4:
                    act.wait_ge(*expert("hd{}", q - 4))
                A(HWP[:, 0, q % 4, :], (HW if e < E1 else HH)[:, q % 2, :], ACT.Copy).then_inc(*done(f"h_hi{e}", i))

            for q in range(TURNS):
                i, e = divmod(q, E1 + 1)
                act.wait_ge(*upto(f"hg{e}", i))
                if q >= 2:
                    act.wait_ge(*expert("hh{}", q - 2))
                A(SG[:, q % 2, :], bank(q % 2), ACT.Silu).then_inc(*done(f"silu{e}", i))
                if q == 1:
                    for j in range(2):
                        act.wait_ge(*upto("g_turn", 8 * j + 7))
                        A(BC[:, j * 2 * N:(j + 1) * 2 * N], ps[0:96, 6 * N:8 * N].bitcast(bf16)[:, j * 2 * N:(j + 1) * 2 * N], ACT.Copy).then_inc(*done("g_turned", j))
                if q:
                    h_hi(q - 1)
            h_hi(TURNS - 1)

        @block.vector
        def _(dve):
            tt, ts, stt = nc.vector.tensor_tensor, nc.vector.tensor_scalar, nc.vector.scalar_tensor_tensor
            red = nc.vector.tensor_reduce

            def skip(i):
                for c in range(DI):
                    dve.wait_ge(*upto(f"y{NS - 1}_{c}", i))
                    stt(ch(U[:, c, :], i), ch(U[:, c, :], i), col(f"D{c}"), bank(c + 2 * (i % 2)), ALU.mult, ALU.add).then_inc(*done(f"skip_{c}", i))

            dve.wait_ge(*upto("c_exp"))
            ts(mtmp[:, 2:4], mtmp[:, 0:2], 1.0, None, ALU.add).then_inc(*done("c_one"))
            dve.wait_ge(*upto("c_one"))
            nc.vector.reciprocal(mtmp[:, 0:2], mtmp[:, 2:4]).then_inc(*done("c_recip"))
            dve.wait_ge(*upto("c_recip"))
            tt(mtmp[:, 4:6], mtmp[:, 0:2], vec[:, VEC.index("c0"):VEC.index("c1") + 1], ALU.mult).then_inc(*done("c_silu"))
            dve.wait_ge(*upto("mod"))
            nc.vector.tensor_copy(mod[:], ps[:, 7 * N:7 * N + 12]).then_inc(*done("mod_copy"))
            dve.wait_ge(*upto("mod_copy"))
            m3 = mod[:].rearrange("p (k s) -> p k s", s=3)
            g3 = mtmp[:, 8:12]
            a3 = mtmp[:, 12:16]
            s3 = mtmp[:, 16:20]
            ts(m3[:, :, 1], m3[:, :, 1], 1.0, None, ALU.add).then_inc(*done("mod_ca"))
            ts(g3, m3[:, :, 2], 0.0, None, ALU.is_ge).then_inc(*done("mod_sign"))
            dve.wait_ge(*upto("mod_sign"))
            ts(s3, g3, 2.0, -1.0, ALU.mult, ALU.add).then_inc(*done("mod_sign2"))
            stt(a3, m3[:, :, 2], -1.0, m3[:, :, 2], ALU.mult, ALU.max).then_inc(*done("mod_abs"))
            dve.wait_ge(*upto("mod_abs"))
            ts(a3, a3, GATE_FLOOR, None, ALU.max).then_inc(*done("mod_floor"))
            dve.wait_ge(*upto("mod_floor"))
            tt(m3[:, :, 2], s3, a3, ALU.mult).then_inc(*done("mod_gate"))
            dve.wait_ge(*upto("mod_gate"))

            def norm(k, h, dst, buf, layer, scale, shift, waits=()):
                for i in range(NCH):
                    dve.wait_ge(*upto(f"rs{k}", i))
                    for w in waits:
                        dve.wait_ge(*upto(w, i))
                    tt(ch(dst, i), half(h, i), ch(buf, i), ALU.mult).then_inc(*done(f"norm{k}", i))
                    dve.wait_ge(*upto(f"norm{k}", i))
                    ts(ch(dst, i), ch(dst, i), modcol(layer, scale), modcol(layer, shift), ALU.mult, ALU.add).then_inc(*done(f"mod{k}", i))

            norm("A", 0, HLN, T1, 0, CA, SA)
            dve.wait_ge(*upto("h1_zero"))
            for i in range(NCH):
                dve.wait_ge(*upto("rsB", i))
                stt(ch(H1, i, 1), ch(HLN, i), col("ln1_w"), ch(T2, i), ALU.mult, ALU.mult).then_inc(*done("normB", i))
            for i in range(NCH):
                dve.wait_ge(*upto("normB", i))
                tt(ch(XX, i), ch(H1, i), ch(H1, i, 1), ALU.subtract).then_inc(*done("xx", i))

            def mix(step, mu, dst, waits):
                for i in range(NCH):
                    dve.wait_ge(*upto("xx", i))
                    for w in waits:
                        dve.wait_ge(*upto(w, i))
                    stt(ch(dst, i), ch(XX, i), col(mu), ch(H1, i, 1), ALU.mult, ALU.add).then_inc(*done(step, i))

            mix("mix_r", "mu_r", M0, [])
            dve.wait_ge(*upto("mod"))
            mix("mix_k", "mu_k", M1, [])
            mix("mix_v", "mu_v", M2, [])
            mix("mix_w", "mu_w", M0, ["r"])
            mix("mix_g", "mu_g", M1, ["k"])
            for i in range(NCH):
                dve.wait_ge(*upto("k_copy", i))
                dve.wait_ge(*upto("mix_g", i))
                stt(ch(XX, i), ch(R, i), col("u"), ch(K, i), ALU.mult, ALU.mult).then_inc(*done("ruk", i))
            for i in range(NCH):
                dve.wait_ge(*upto("head_ruk", i))
                tt(ch(BONUS, i), half(1, i), ch(V, i), ALU.mult).then_inc(*done("bonus", i))
            nc.vector.memset(S[:, :, 0:1], 0.0).then_inc(*done("s_zero"))
            dve.wait_ge(*upto("s_zero"))

            def kv(q):
                i, v = q // DK, ORDER[q % DK]
                dve.wait_ge(*upto(f"spread{v}", i))
                if q >= 4:
                    dve.wait_ge(*column("scan{}", q - 4))
                tt(KV[:, q % 4, :], bank(4 + q % 4), ch(K, i), ALU.mult).then_inc(*done(f"kv{v}", i))

            def o(i):
                dve.wait_ge(*upto(f"reduce{ORDER[-1]}", i))
                tt(ch(O, i), bank(i % 2), ch(BONUS, i), ALU.add).then_inc(*done("o", i))

            kv(0)
            for q in range(NR):
                i, v = q // DK, ORDER[q % DK]
                if q + 1 < NR:
                    kv(q + 1)
                if q % DK == 0:
                    dve.wait_ge(*upto("decay", i))
                dve.wait_ge(*upto(f"kv{v}", i))
                nc.vector.tensor_tensor_scan(S[:, v, i * N + 1:(i + 1) * N + 1], ch(DEC, i), KV[:, q % 4, :],
                                             S[:, v, i * N:i * N + 1], ALU.mult, ALU.add).then_inc(*done(f"scan{v}", i))
                if i and q % DK == DK - 1:
                    o(i - 1)
            o(NCH - 1)
            for i in range(NCH):
                dve.wait_ge(*upto("gn_rs2", i))
                stt(ch(T3, i), half(0, i), EPS_GN, ch(T3, i), ALU.add, ALU.mult).then_inc(*done("gn_err", i))
                dve.wait_ge(*upto("gn_err", i))
                ts(ch(T3, i), ch(T3, i), -0.5, 1.5, ALU.mult, ALU.add).then_inc(*done("gn_half", i))
                dve.wait_ge(*upto("gn_half", i))
                tt(ch(T1, i), ch(T1, i), ch(T3, i), ALU.mult).then_inc(*done("gn_rsqrt", i))
                dve.wait_ge(*upto("gn_rsqrt", i))
                tt(ch(O, i), half(1, i), ch(T1, i), ALU.mult).then_inc(*done("gn_norm", i))
            for i in range(NCH):
                dve.wait_ge(*upto("wo", i))
                tt(ch(HLN, i), half(1, i), ch(HLN, i), ALU.add).then_inc(*done("x1", i))
            for i in range(NCH):
                dve.wait_ge(*upto("rsC", i))
                stt(ch(M0, i), ch(HLN, i), col("ln2_w"), ch(T2, i), ALU.mult, ALU.mult).then_inc(*done("normC", i))
            for i in range(NCH + 1):
                for f in (1, 3) if i < NCH else ():
                    dve.wait_ge(*upto(f"f_hi{f}", i))
                    if i:
                        dve.wait_ge(*upto(f"down{f}", i - 1))
                    tt(f_parts[1][:, f, :], GEL[:, f, :], f_parts[0][:, f, :].bitcast(f32), ALU.subtract).then_inc(*done(f"f_lo{f}", i))
                if i:
                    dve.wait_ge(*upto("down3", i - 1))
                    tt(ch(HLN, i - 1), half(0, i - 1), ch(HLN, i - 1), ALU.add).then_inc(*done("ffn_sum", i - 1))
                    dve.wait_ge(*upto("ffn_sum", i - 1))
                    stt(ch(X, i - 1), ch(HLN, i - 1), modcol(0, GA), ch(X, i - 1), ALU.mult, ALU.add).then_inc(*done("x_attn", i - 1))

            norm("D", 0, HB, TB, 0, CB, SB_)
            steps = iter(R_STEPS)
            state = {"last": None}

            def step(op, *args, **kw):
                name = next(state["names"])
                if state["last"]:
                    dve.wait_ge(*upto(state["last"]))
                for w in kw.pop("waits", []):
                    dve.wait_ge(*upto(*w))
                op(*args, **kw).then_inc(*done(name))
                state["last"] = name

            L_, E_, PR_, OH_, RK_, CU_, TO_ = (small3(k) for k in (0, 1, 2, 3, 4, 5, 6))
            flat = small
            MX, SM, RC, PM, SC, BEST, POS, KEEP, BASE, SLOT = (tiny(k) for k in (0, 1, 2, 3, 4, 5, 6, 7, 8, 9))
            state["names"] = steps
            dve.wait_ge(cstb_loaded, 16)
            step(tt, flat(0), ps[:, 0:NT * E0], CB_("b_switch"), ALU.add, waits=[("router",)])
            step(red, MX, L_, AX, ALU.max)
            step(tt, L_, L_, bcast(MX, E0), ALU.subtract)
            step(red, SM, E_, AX, ALU.add, waits=[("r_exp",)])
            step(nc.vector.reciprocal, RC, SM)
            step(tt, PR_, E_, bcast(RC, E0), ALU.mult)
            step(red, PM, PR_, AX, ALU.max)
            step(tt, RK_, PR_, bcast(PM, E0), ALU.is_equal)
            step(tt, flat(4), flat(4), CB_("rank"), ALU.mult)
            step(red, BEST, RK_, AX, ALU.max)
            step(tt, OH_, CB_("rank").rearrange("p (t e) -> p t e", e=E0), bcast(BEST, E0), ALU.is_equal)
            step(nc.vector.reciprocal, RC, PM)
            step(tt, SC, PM, RC, ALU.mult)
            step(nc.vector.tensor_copy, TO_.rearrange("p t e -> p (t e)").rearrange("p (e t) -> p e t", e=E0),
                 bank(2)[:, 0:P].rearrange("p (t e) -> p e t", e=E0), waits=[("totals",)])
            step(nc.vector.tensor_tensor_scan, flat(5), CB_("seg"), flat(6), 0.0, ALU.mult, ALU.add)
            step(tt, flat(5), flat(5), flat(6), ALU.subtract)
            step(tt, RK_, bank(1)[:, 0:P].rearrange("p (t e) -> p t e", e=E0), flat(5).rearrange("p (e t) -> p t e", e=E0), ALU.add)
            step(tt, RK_, RK_, OH_, ALU.mult)
            step(red, POS, RK_, AX, ALU.add)
            step(ts, KEEP, POS, float(CAP), None, ALU.is_le)
            step(ts, BASE, BEST, -float(CAP), float(E0 * CAP), ALU.mult, ALU.add)
            step(tt, SLOT, BASE, POS, ALU.add)
            step(tt, SLOT, SLOT, KEEP, ALU.mult)
            dve.wait_ge(*upto("r_kept"))
            for t in range(NT):
                if t % 4 == 0:
                    i = t // 4
                    dve.wait_ge(*upto("h_turned", i))
                    tt(ch(HT[:, 1, :], i), half(1, i), ch(HT[:, 0, :], i).bitcast(f32), ALU.subtract).then_inc(*done("h_turned_lo", i))
                if t >= 2:
                    dve.wait_ge(*upto("dispatch", t - 2))
                ts(OH1[:, t % 2, :], CB_("iota"), SLOT[:, t:t + 1], None, ALU.is_equal).then_inc(*done("onehot", t))
            dve.wait_ge(*upto("dispatch", NT - 1))
            nc.vector.tensor_copy(BUF[:, N:2 * N], bank(3)).then_inc(*done("buf1"))

            def e_relu(e):
                dve.wait_ge(*upto("e_up", e))
                if e >= 2:
                    dve.wait_ge(*upto("e_down", e - 2))
                for f in range(NF):
                    last = ts(HS[:, e % 2, f, :], bank(6 + e % 2)[:, f * P:(f + 1) * P], expert_b1(e, f), 0.0, ALU.add, ALU.max)
                last.then_inc(*done("e_relu", e))

            def place(e, i):
                dve.wait_ge(*upto("slots", i))
                if i >= 2:
                    dve.wait_ge(*upto(f"combine{e}", i - 2))
                ts(PTS[i % 2][:, e, :], ch(SLB, i), CB_("iota_p")[:, e:e + 1], None, ALU.is_equal).then_inc(*done(f"place{e}", i))

            e_relu(0)
            for e in range(E0):
                for j in range(2):
                    place((2 * e + j) % E0, (2 * e + j) // E0)
                dve.wait_ge(*upto("y_hi", e))
                tt(YB[:, 1, e, :], bank(2 + e % 2)[:, 0:P], YB[:, 0, e, :].bitcast(f32), ALU.subtract).then_inc(*done("y_lo", e))
                if e + 2 < E0 and e % 2 == 0:
                    e_relu(e + 2)
                if e < NCH:
                    stt(ch(HB, e), ch(SLB, e), 0.5, ch(HB, e), ALU.is_lt, ALU.mult).then_inc(*done("kept_x", e))
            for i in range(NCH):
                dve.wait_ge(*upto("kept_x", i))
                dve.wait_ge(*upto(f"combine{E0 - 1}", i))
                tt(ch(HB, i), half(0, i), ch(HB, i), ALU.add).then_inc(*done("moe_sum", i))
                dve.wait_ge(*upto("moe_sum", i))
                dve.wait_ge(*upto("scales", i))
                tt(ch(HB, i), ch(HB, i), ch(SCB, i), ALU.mult).then_inc(*done("moe_scaled", i))
                if i + 2 < NCH:
                    for e in range(E0):
                        place(e, i + 2)

            norm("E", 1, HC, TE, 1, CA, SA)
            nc.vector.memset(XBP[:, :, 0:3], 0.0).then_inc(*done("xb_zero"))
            dve.wait_ge(*upto("xb_zero"))
            def bc_r1(i):
                dve.wait_ge(*upto("bc_hi", i))
                tt(ch(R1, i)[0:BC3], half(1, i, BC3), ch(BC, i), ALU.subtract).then_inc(*done("bc_r1", i))

            def conv(c, i):
                dve.wait_ge(*upto(f"xb{c}_copy", i))
                for j in range(KC):
                    src = XBP[:, c, i * N + j:(i + 1) * N + j]
                    if j == 0:
                        ts(ch(CV[:, c, :], i), src, col(f"cw{c}_0"), col(f"cb{c}"), ALU.mult, ALU.add).then_inc(*done(f"conv{c}_0", i))
                    else:
                        dve.wait_ge(*upto(f"conv{c}_{j - 1}", i))
                        stt(ch(CV[:, c, :], i), src, col(f"cw{c}_{j}"), ch(CV[:, c, :], i), ALU.mult, ALU.add).then_inc(*done(f"conv{c}_{j}", i))

            for i in range(NCH + 1):
                if i < NCH:
                    conv(0, i)
                    conv(1, i)
                if i:
                    bc_r1(i - 1)
            dve.wait_ge(*upto("a_exp"))
            ts(ABASE[:], ABASE[:], -0.5, None, ALU.mult).then_inc(*done("a_neg"))
            nc.vector.memset(CARRY[:], 0.0).then_inc(*done("st_zero"))

            def dt_of(i):
                for c in range(DI):
                    dve.wait_ge(*upto(f"sp_ln_{c}", i))
                    dve.wait_ge(*upto(f"sp_r_{c}", i))
                    tt(ch(SPL[:, c, :], i), ch(SPL[:, c, :], i), ch(SPX[:, c, :], i), ALU.subtract).then_inc(*done(f"sp_log_{c}", i))
                for c in range(DI):
                    dve.wait_ge(*upto(f"sp_log_{c}", i))
                    stt(ch(SPL[:, c, :], i), ch(SPE[:, c, :], i), E_SMALL, ch(SPL[:, c, :], i), ALU.is_gt, ALU.mult).then_inc(*done(f"sp_mask_{c}", i))
                for c in range(DI):
                    dve.wait_ge(*upto(f"sp_mask_{c}", i))
                    dve.wait_ge(*upto(f"sp_lo_{c}", i))
                    tt(ch(SPL[:, c, :], i), ch(SPL[:, c, :], i), ch(DU[:, c, :], i), ALU.max).then_inc(*done(f"sp_max_{c}", i))
                for c in range(DI):
                    dve.wait_ge(*upto(f"sp_relu_{c}", i))
                    dve.wait_ge(*upto(f"sp_max_{c}", i))
                    tt(ch(SPR[:, c, :], i), ch(SPR[:, c, :], i), ch(SPL[:, c, :], i), ALU.add).then_inc(*done(f"dt_{c}", i))
                for c in range(DI):
                    dve.wait_ge(*upto(f"dt_{c}", i))
                    stt(ch(DTG[:, c, :], i), ch(DTG[:, c, :], i), 2.0, ch(SPR[:, c, :], i), ALU.add, ALU.mult).then_inc(*done(f"dtg_{c}", i))

            for i in range(NCH):
                for c in range(DI):
                    dve.wait_ge(*upto(f"sp_w_{c}", i))
                    stt(ch(SPX[:, c, :], i), ch(SPW[:, c, :], i), -1.0, ch(SPE[:, c, :], i), ALU.add, ALU.subtract).then_inc(*done(f"sp_r_{c}", i))
                dt_of(i)

            def dbu(q):
                i, n = divmod(q, NS)
                dve.wait_ge(*upto(f"b{n}", i))
                if n == 0:
                    dve.wait_ge(*upto("du_1", i))
                if q >= DBU_RING // DI:
                    dve.wait_ge(*turn("st{}_1", q - DBU_RING // DI))
                a = (DI * q) % DBU_RING
                tt(DBU[:, a:a + DI, :], bank(4 + q % 2).unsqueeze(1).to_broadcast([P, DI, N]), DU[:, :, i * N:(i + 1) * N],
                   ALU.mult).then_inc(*done(f"dbu{n}", i))

            def x_mamba(i):
                dve.wait_ge(*upto("m_out", i))
                stt(ch(X, i), bank(2 * (i % 2)), modcol(1, GA), ch(X, i), ALU.mult, ALU.add).then_inc(*done("x_mamba", i))

            def norm_f(i):
                dve.wait_ge(*upto("rsF", i))
                tt(ch(HD, i), bank(2 * (i % 2) + 1), ch(TF, i), ALU.mult).then_inc(*done("normF", i))
                dve.wait_ge(*upto("normF", i))
                ts(ch(HD, i), ch(HD, i), modcol(1, CB), modcol(1, SB_), ALU.mult, ALU.add).then_inc(*done("modF", i))

            side = dict(zip(SIDE["dve"], (skip, x_mamba, norm_f)))
            dve.wait_ge(*upto("bc_lo", NCH - 1))
            dbu(0)
            def states(q):
                i, n = divmod(q, NS)
                for c in range(DI):
                    k = 2 * n + c
                    dve.wait_ge(*upto(f"dec{n}_{c}", i))
                    dve.wait_ge(*upto(f"dbu{n}", i))
                    if i:
                        dve.wait_ge(*upto(f"sc{n}_{c}", i - 1))
                    first = ST[:, k, N - 1:N] if i else CARRY[:]
                    nc.vector.tensor_tensor_scan(ST[:, k, :], DECR[:, (2 * q + c) % DEC_RING, :], DBU[:, (2 * q + c) % DBU_RING, :], first,
                                                 ALU.mult, ALU.add).then_inc(*done(f"st{n}_{c}", i))

            for q in range(ALL_TURNS):
                if q + 1 < NQ:
                    dbu(q + 1)
                if q == 0:
                    dve.wait_ge(*upto("du_1", NCH - 1))
                if q < NQ:
                    states(q)
                for d, j in side_steps("dve", q):
                    side[d](j)

            state["names"], state["last"] = iter(G_STEPS), None
            g, g3 = gsmall, gsmall3
            M8 = gsmall(12)[:, 0:NT * 8].rearrange("p (t k) -> p t k", k=8)
            THR = M8[:, :, 7]
            NG, LEFT, TOT, INV = (gtiny(k) for k in range(4))
            step(ts, g(1), g(0), 1.0, None, ALU.add, waits=[("g_exp", NCH - 1)])
            step(nc.vector.reciprocal, g(2), g(1))
            step(tt, g(3), g(2), WC_("g_bias"), ALU.add)
            for t in range(NT):
                step(nc.vector.max, M8[:, t, :], g3(3)[:, t, :])
            step(tt, g3(4), g3(3), bcast(THR, E1), ALU.is_gt)
            step(tt, g3(5), g3(3), bcast(THR, E1), ALU.is_equal)
            step(red, NG, g3(4), AX, ALU.add)
            step(ts, LEFT, NG, -1.0, float(TOPK), ALU.mult, ALU.add)
            step(nc.vector.tensor_tensor_scan, g(6), WC_("g_seg"), g(5), 0.0, ALU.mult, ALU.add)
            step(tt, g3(6), g3(6), bcast(LEFT, E1), ALU.is_le)
            step(tt, g(6), g(6), g(5), ALU.mult)
            step(tt, g(6), g(6), g(4), ALU.add)
            step(tt, g(6), g(6), g(2), ALU.mult)
            step(red, TOT, g3(6), AX, ALU.add)
            step(nc.vector.reciprocal, INV, TOT)
            step(stt, g3(7), g3(6), ROUTE_SCALE, bcast(INV, E1), ALU.mult, ALU.mult)
            step(nc.vector.memset, CS, 0.0)
            step(nc.vector.tensor_copy, CS[:, :, 0:E1], g3(7))
            step(tt, g3(8), g3(7), CS[:, :, 0:E1], ALU.subtract)
            step(nc.vector.tensor_copy, CS[:, :, 32:32 + E1], g3(8))
            step(tt, CS[:, :, 64:64 + E1], g3(8), CS[:, :, 32:32 + E1], ALU.subtract)
            def x_out(i):
                dve.wait_ge(*upto(f"hd{E1}", i))
                stt(ch(X, i), bank(6 + i % 2), modcol(1, GB), ch(X, i), ALU.mult, ALU.add).then_inc(*done("x_out", i))

            for q in range(TURNS):
                i, e = divmod(q, E1 + 1)
                k = q % 2
                dve.wait_ge(*upto(f"silu{e}", i))
                dve.wait_ge(*upto(f"hu{e}", i))
                if q >= 2:
                    dve.wait_ge(*expert("h_lo{}", q - 2))
                tt(HH[:, k, :], bank(2 + k), SG[:, k, :], ALU.mult).then_inc(*done(f"hh{e}", i))
                if e < E1:
                    dve.wait_ge(*upto(f"hh{e}", i))
                    dve.wait_ge(*upto(f"w{e}", i))
                    tt(HW[:, k, :], bank(4 + k), HH[:, k, :], ALU.mult).then_inc(*done(f"hw{e}", i))
                if i and e == LAG_E + 1:
                    x_out(i - 1)
            x_out(NCH - 1)

        @block.gpsimd
        def _(pool):
            mul = lambda o, a, b: nc.gpsimd.tensor_tensor(o, a, b, ALU.mult)
            nc.gpsimd.memset(H1[:, 0:1], 0.0).then_inc(*done("h1_zero"))
            for i in range(NCH):
                pool.wait_ge(*upto("v_hi", i))
                nc.gpsimd.tensor_tensor(ch(v_parts[:, 1, :], i), ch(V, i), ch(v_parts[:, 0, :], i).bitcast(f32), ALU.subtract).then_inc(*done("v_lo", i))
            for q in range(NR):
                i, v = q // DK, ORDER[q % DK]
                pool.wait_ge(*upto(f"scan{v}", i))
                if q >= 8:
                    pool.wait_ge(*column("reduce{}", q - 8))
                mul(PR[:, q % 8, :], S[:, v, i * N:(i + 1) * N], ch(R, i)).then_inc(*done(f"prod{v}", i))
            a = wa_at["w1"][0]
            w = wA[:, a:a + 2 * F]
            pool.wait_ge(*upto("reduce7", NCH - 1))
            nc.gpsimd.tensor_scalar(f_w_parts[:, 0, :], w, 1.0, None, ALU.mult).then_inc(*done("f_w_hi"))
            pool.wait_ge(*upto("f_w_hi"))
            nc.gpsimd.tensor_tensor(f_w_parts[:, 1, :], w, f_w_parts[:, 0, :].bitcast(f32), ALU.subtract).then_inc(*done("f_w_lo"))
            for i in range(NCH):
                pool.wait_ge(*upto("gn_affine", i))
                mul(ch(O, i), ch(O, i), ch(G, i)).then_inc(*done("gn_gate", i))
            for i in range(NCH):
                pool.wait_ge(*upto("f_x_hi", i))
                nc.gpsimd.tensor_tensor(ch(f_x_parts[:, 1, :], i), ch(M0, i), ch(f_x_parts[:, 0, :], i).bitcast(f32), ALU.subtract).then_inc(*done("f_x_lo", i))
            for i in range(NCH):
                for f in (0, 2):
                    pool.wait_ge(*upto(f"f_hi{f}", i))
                    if i:
                        pool.wait_ge(*upto(f"down{f}", i - 1))
                    nc.gpsimd.tensor_tensor(f_parts[1][:, f, :], GEL[:, f, :], f_parts[0][:, f, :].bitcast(f32), ALU.subtract).then_inc(*done(f"f_lo{f}", i))
            for i in range(NCH):
                pool.wait_ge(*upto("moe_scaled", i))
                nc.gpsimd.tensor_tensor(ch(X, i), ch(HB, i), ch(X, i), ALU.add).then_inc(*done("x_moe", i))
            xp = WC_("xp")
            pool.wait_ge(wc_loaded, 48)
            pool.wait_ge(*upto("combine7", NCH - 1))
            nc.gpsimd.tensor_scalar(xp_parts[:, 0, :], xp, 1.0, None, ALU.mult).then_inc(*done("xp_hi"))
            pool.wait_ge(*upto("xp_hi"))
            nc.gpsimd.tensor_tensor(xp_parts[:, 1, :], xp, xp_parts[:, 0, :].bitcast(f32), ALU.subtract).then_inc(*done("xp_lo"))

            def u_lo(c, i):
                pool.wait_ge(*upto(f"u_hi{c}", i))
                nc.gpsimd.tensor_tensor(ch(u_parts[1][:, c, :], i), ch(U[:, c, :], i), ch(u_parts[0][:, c, :], i).bitcast(f32), ALU.subtract).then_inc(*done(f"u_lo{c}", i))

            for i in range(NCH + 1):
                if i < NCH:
                    u_lo(0, i)
                    u_lo(1, i)
                if i:
                    pool.wait_ge(*upto("bc_mid", i - 1))
                    nc.gpsimd.tensor_tensor(ch(BC, i - 1)[0:32], ch(R1, i - 1)[0:32], ch(BC, i - 1)[0:32], ALU.subtract).then_inc(*done("bc_lo", i - 1))

            def du(i):
                for c in range(DI):
                    pool.wait_ge(*upto(f"dt_{c}", i))
                    mul(ch(DU[:, c, :], i), ch(U[:, c, :], i), ch(SPR[:, c, :], i)).then_inc(*done(f"du_{c}", i))

            for i in range(NCH):
                for c in range(DI):
                    pool.wait_ge(*upto(f"sp_e_{c}", i))
                    nc.gpsimd.tensor_scalar(ch(DU[:, c, :], i), ch(SPE[:, c, :], i), -0.5, 1.0, ALU.mult, ALU.add).then_inc(*done(f"sp_p_{c}", i))
                    pool.wait_ge(*upto(f"sp_p_{c}", i))
                    mul(ch(DU[:, c, :], i), ch(DU[:, c, :], i), ch(SPE[:, c, :], i)).then_inc(*done(f"sp_lo_{c}", i))
                if i:
                    du(i - 1)
            du(NCH - 1)

            def gated(i):
                for c in range(DI):
                    pool.wait_ge(*upto(f"skip_{c}", i))
                    mul(ch(U[:, c, :], i), ch(U[:, c, :], i), ch(Z[:, c, :], i)).then_inc(*done(f"gated_{c}", i))

            def times_c(q):
                i, n = divmod(q, NS)
                for c in range(DI):
                    pool.wait_ge(*upto(f"st{n}_{c}", i))
                    pool.wait_ge(*upto(f"c_copy{n}", i))
                    if q >= LAG:
                        pool.wait_ge(*turn(f"y{{}}_{c}", q - LAG))
                    mul(PRC[:, (2 * q + c) % PR_RING, :], ST[:, 2 * n + c, :], CBR[:, q % C_RING, :]).then_inc(*done(f"sc{n}_{c}", i))

            for q in range(ALL_TURNS):
                if q < NQ:
                    times_c(q)
                for _, j in side_steps("pool", q):
                    gated(j)

            def x_lo(i):
                pool.wait_ge(*upto("x_hi", i))
                nc.gpsimd.tensor_tensor(ch(x_parts[:, 1, :], i), ch(HD, i), ch(x_parts[:, 0, :], i).bitcast(f32), ALU.subtract).then_inc(*done("x_lo", i))

            x_lo(0)
            for k in range(WD_PARTS):
                pool.wait_ge(*upto("w_hi", k))
                nc.gpsimd.tensor_tensor(w_parts[:, 1, wd_part(k), :], wD[:, wd_part(k), :], w_parts[:, 0, wd_part(k), :].bitcast(f32),
                                        ALU.subtract).then_inc(*done("w_lo", k))
            for i in range(1, NCH):
                x_lo(i)
            for q in range(TURNS):
                i, e = divmod(q, E1 + 1)
                pool.wait_ge(*upto(f"h_hi{e}", i))
                if q >= 4:
                    pool.wait_ge(*expert("hd{}", q - 4))
                nc.gpsimd.tensor_tensor(HWP[:, 1, q % 4, :], (HW if e < E1 else HH)[:, q % 2, :], HWP[:, 0, q % 4, :].bitcast(f32),
                                        ALU.subtract).then_inc(*done(f"h_lo{e}", i))
        assert not any(order.values()), {k: v[:3] for k, v in order.items()}


def kernel(**inputs):
    import numpy as np
    import concourse.bacc as bacc
    from concourse.bass_utils import run_bass_kernel_spmd

    a = {k: np.asarray(v) for k, v in inputs.items()}

    def by_value(w, axis):
        s = w.shape
        return np.moveaxis(w.reshape(s[:axis] + (H, DK) + s[axis + 1:]), axis, axis + 1).reshape(s)

    L0 = {k[8:]: v for k, v in a.items() if k.startswith("L0_attn_")}
    vecs = dict(L0, u=L0["u"].reshape(-1), gn_w=by_value(L0["gn_w"].reshape(-1), 0), gn_b=by_value(L0["gn_b"].reshape(-1), 0),
                c0=a["L0_c"][0], c1=a["L1_c"][0], eps5=np.full(P, 1e-5, np.float32), eps6=np.full(P, 1e-6, np.float32))
    x = np.ascontiguousarray(L0["x"][0].T)
    w = dict(L0, Wv=by_value(L0["Wv"], 1), Wg=by_value(L0["Wg"], 1), Wo=by_value(L0["Wo"], 0),
             wB=np.concatenate([L0["wB"], L0["wB"]]), w1=L0["ffn_w1"],
             w2=L0["ffn_w2"].reshape(NF, P, P).transpose(1, 0, 2).reshape(P, F))
    wA = np.concatenate([w[n] for n in WA], 1)
    wmod = np.stack([a["L0_wmod"], a["L1_wmod"]], 1)
    F0 = {k[7:]: v for k, v in a.items() if k.startswith("L0_ffn_")}
    M = {k[8:]: v for k, v in a.items() if k.startswith("L1_attn_")}
    F1 = {k[7:]: v for k, v in a.items() if k.startswith("L1_ffn_")}
    w1B = F0["w1"].transpose(1, 0, 2)
    w2B = F0["w2"].reshape(E0, NF, P, P).transpose(2, 0, 1, 3).reshape(P, E0, NF, P)
    xp = M["x_proj_w"].T.reshape(DI, P, -1)
    dt_c, bc_c, gate_c = xp[:, :, :DTR], xp[:, :, DTR:DTR + 2 * NS], xp[:, :, DTR + 2 * NS:]
    xp = np.concatenate([gate_c, bc_c, bc_c, bc_c, dt_c], 2).transpose(1, 0, 2).reshape(P, -1)
    dtp = np.zeros((P, DI * P), np.float32)
    dtp[BC3:BC3 + DTR] = M["dt_proj_w"].T
    wc = {"in": M["in_proj_w"].T, "xp": xp, "dtp": dtp, "out": M["out_proj_w"].T.reshape(DI, P, P).transpose(1, 0, 2).reshape(P, -1),
          "gate": F1["gate_w"].T, "g_bias": np.broadcast_to(np.tile(F1["expert_bias"], NT), (P, NT * E1)),
          "g_seg": np.broadcast_to(np.tile(np.arange(E1) > 0, NT), (P, NT * E1)).astype(np.float32)}
    wC = np.concatenate([wc[n] for n in WC], 1)
    shared = [F1["shared_gate_w"][None], F1["shared_up_w"][None], F1["shared_down_w"][None]]
    wD = np.stack([np.concatenate([F1[n], sh]) for n, sh in zip(["w_gate", "w_up", "w_down"], shared)], 1)
    wD = wD.transpose(3, 0, 1, 2).reshape(P, 3 * (E1 + 1), P)
    for c in range(DI):
        part = slice(c * P, (c + 1) * P)
        vecs.update({f"dt_b{c}": M["dt_proj_b"][part], f"D{c}": M["D_param"][part], f"cb{c}": M["conv_b"][part]})
        vecs.update({f"cw{c}_{j}": M["conv_w"][part, 0, j] for j in range(KC)})
        vecs.update({f"A{c}_{n}": M["A_log"][part, n] for n in range(NS)})
    vec = np.stack([vecs[n] for n in VEC], 1)

    eye = np.eye(P, dtype=np.float32)
    head_k = np.arange(P) // DK
    head_v = np.arange(P) % H
    gn_mean = (head_v[:, None] == head_v[None]).astype(np.float32) / DK
    reduce = np.zeros((P, 2, 32), np.float32)
    spread = np.zeros((P, DK, P), np.float32)
    for b in range(2):
        reduce[:, b, b * H:(b + 1) * H] = head_k[:, None] == np.arange(H)[None]
    for v in range(DK):
        spread[v * H:(v + 1) * H, v] = np.arange(H)[:, None] == head_k[None]
    c = {"head_sum": head_k[:, None] == head_v[None],
         "gn_mean": gn_mean, "gn_centre": eye - gn_mean, "reduce": reduce.reshape(P, -1), "spread": spread.reshape(P, -1)}
    cst = np.concatenate([c[n].astype(np.float32) for n in CST], 1)
    c = {"centre": eye - 1.0 / P, "mean": np.full((P, P), 1.0 / P), "eye": eye}
    core = np.concatenate([c[n].astype(np.float32) for n in CORE], 1)
    row = lambda v: np.broadcast_to(np.asarray(v, np.float32).reshape(1, -1), (P, np.size(v)))
    experts = np.arange(E0)
    slots = 1 + np.arange(P)[:, None] + CAP * experts[None]
    c = {"iota": row(1 + np.arange(E0 * CAP)), "tri": np.triu(np.ones((P, P))), "ones": np.ones((P, P)),
         "rank": row(np.tile(E0 - experts, NT)), "seg": row(np.tile(np.arange(NT) > 0, E0)), 
         "iota_p": slots, "b_switch": row(np.tile(F0["b_switch"], NT)), "w_switch": F0["w_switch"],
         "b1": F0["b1"].reshape(E0, NF, P).transpose(2, 0, 1).reshape(P, -1), "b2": row(F0["b2"].reshape(-1))}
    cstB = np.concatenate([c[n].astype(np.float32) for n in CSTB], 1)
    bf = mybir.dt.np(mybir.dt.bfloat16)
    sel = np.zeros((3, 2 * NS, 2 * NS, P), np.float32)
    sel[:, np.arange(2 * NS), np.arange(2 * NS)] = 1
    sel = sel.reshape(96, 2 * NS, P).astype(bf)

    nc = bacc.Bacc("TRN2", target_bir_lowering=False, num_devices=1)
    arrays = {"x": x, "vec": vec, "core": core, "cst": cst, "wA": wA, "wmod": wmod, "cstB": cstB, "wB1": w1B, "wB2": w2B, "wC": wC,
              "sel": sel, "eyeb": eye.astype(bf), "wD": wD}
    aps = []
    for name, v in arrays.items():
        arrays[name] = v = np.ascontiguousarray(v)
        aps.append(nc.dram_tensor(f"in_{name}", v.shape, mybir.dt.from_np(v.dtype), kind="ExternalInput").ap())
    o = nc.dram_tensor("out_x", (P, T), mybir.dt.float32, kind="ExternalOutput").ap()
    build(nc, *aps, o)
    r = run_bass_kernel_spmd(nc, [{f"in_{k}": v for k, v in arrays.items()}], core_ids=[0])
    return np.ascontiguousarray(r.results[0]["out_x"].T)[None]
```
